# Optimizing a Trainium2 kernel written in Bass

```python
import numpy as np
import jax
import jax.numpy as jnp

def _softmax(x, axis=-1):
    return jax.nn.softmax(x, axis=axis)

def _gelu(x):
    return jax.nn.gelu(x, approximate=True)

def _silu(x):
    return jax.nn.silu(x)

def _sigmoid(x):
    return jax.nn.sigmoid(x)

def _layernorm(x, axis=-1, eps=1e-05):
    m = jnp.mean(x, axis=axis, keepdims=True)
    v = jnp.var(x, axis=axis, keepdims=True)
    return (x - m) / jnp.sqrt(v + eps)

def _scatter_add(tgt, idx, src, axis=0):
    return tgt.at[idx].add(src)

def _segment_sum(src, seg, n):
    return jax.ops.segment_sum(src, seg, n)
kernel_name = 'mk_xattn_ffn_d2_seqx_r4_23f0f0'

def setup_inputs(seed: int=0):
    np.random.seed(seed)
    _w = jnp.asarray

    def _rec_inputs():
        import jax
        import jax.numpy as jnp
        _rk = jax.random.key(seed)
        x = -0.000125 + 0.9999 * jax.random.normal(jax.random.fold_in(_rk, 1), (2, 1024, 256), jnp.float32)
        _lenS = 1024 - jax.random.randint(jax.random.fold_in(_rk, 7), (2,), 0, max(1, 1024 // 4) + 1, jnp.int32)
        _lenS2 = 64 - jax.random.randint(jax.random.fold_in(_rk, 8), (2,), 0, max(1, 64 // 4) + 1, jnp.int32)
        _ctx_1024P = jax.random.normal(jax.random.fold_in(_rk, 11), (2, 16, 256), jnp.float32)
        _ctx_1024c = jax.random.dirichlet(jax.random.fold_in(_rk, 511), 0.3 * jnp.ones((16,), jnp.float32), (2, 64))
        _ctx_1024t = jnp.einsum('bsk,bkd->bsd', _ctx_1024c, _ctx_1024P)
        _ctx_1024t = _ctx_1024t * jax.lax.rsqrt(jnp.mean(jnp.square(_ctx_1024t)) + 1e-12) * 0.953939
        ctx_1024 = -0.000514642 + 1.00011 * (_ctx_1024t + 0.3 * jax.random.normal(jax.random.fold_in(_rk, 611), (2, 64, 256), jnp.float32))
        return (x, ctx_1024)
    x, ctx_1024 = _rec_inputs()

    def _L0_xattn_setup():
        import jax, jax.numpy as jnp
        import numpy as np
        H, DH, WSIZE, PE_LEN = (8, 64, 4, 75)

        def sinusoidal_pe(T, d, n=10000.0):
            pos = jnp.arange(T, dtype=jnp.float32)[:, None]
            denom = jnp.power(n, 2.0 * jnp.arange(d // 2, dtype=jnp.float32) / d)
            ang = pos / denom
            pe = jnp.zeros((T, d), dtype=jnp.float32)
            pe = pe.at[:, 0::2].set(jnp.sin(ang))
            pe = pe.at[:, 1::2].set(jnp.cos(ang))
            return pe
        key = jax.random.key(seed)
        ks = jax.random.split(key, 6)
        B, NQ, NK, QD, VD = (8, 1024, 64, 256, 256)
        inner = H * DH
        return {'x': jax.random.normal(ks[0], (B, NQ, QD), jnp.float32), 'hint_control': jax.random.normal(ks[1], (B, NK, VD), jnp.float32), 'Wq': jax.random.normal(ks[2], (QD, inner), jnp.float32) / np.sqrt(QD), 'Wk': jax.random.normal(ks[3], (VD, inner), jnp.float32) / np.sqrt(VD), 'Wv': jax.random.normal(ks[4], (VD, inner), jnp.float32) / np.sqrt(VD), 'Wo': jax.random.normal(ks[5], (inner, QD), jnp.float32) / np.sqrt(inner), 'bo': jnp.zeros((QD,), jnp.float32)}
    _L0_xattn_all = _L0_xattn_setup()
    _L0_xattn_in = {k: v for k, v in _L0_xattn_all.items() if k in ('Wq', 'Wk', 'Wv', 'Wo', 'bo')}
    del _L0_xattn_all

    def _L0_ffn_setup():
        import jax, jax.numpy as jnp
        import numpy as np
        NUM_GEMMS = 8
        HIDDEN = 256
        INTER = 1024
        key = jax.random.key(seed)
        k_x, k_w1, k_b1, k_w2, k_b2 = jax.random.split(key, 5)
        x = jax.random.normal(k_x, (8, 512, HIDDEN), dtype=jnp.float32)
        s1 = 1.0 / np.sqrt(HIDDEN)
        s2 = 1.0 / np.sqrt(INTER)
        W1 = jax.random.uniform(k_w1, (NUM_GEMMS, INTER, HIDDEN), jnp.float32, -s1, s1)
        b1 = jax.random.uniform(k_b1, (NUM_GEMMS, INTER), jnp.float32, -s1, s1)
        W2 = jax.random.uniform(k_w2, (NUM_GEMMS, HIDDEN, INTER), jnp.float32, -s2, s2)
        b2 = jax.random.uniform(k_b2, (NUM_GEMMS, HIDDEN), jnp.float32, -s2, s2)
        return {'x': x, 'W1': W1, 'b1': b1, 'W2': W2, 'b2': b2}
    _L0_ffn_all = _L0_ffn_setup()
    _L0_ffn_in = {k: v for k, v in _L0_ffn_all.items() if k in ('W1', 'b1', 'W2', 'b2')}
    del _L0_ffn_all

    def _L1_xattn_setup():
        import jax, jax.numpy as jnp
        import numpy as np
        EMBED_DIM = 256
        NUM_HEADS = 16
        HEAD_DIM = EMBED_DIM // NUM_HEADS
        key = jax.random.key(seed)
        ks = jax.random.split(key, 7)
        B, S, E = (2, 512, EMBED_DIM)
        bound = float(np.sqrt(6.0 / (E + E)))
        mkw = lambda k: jax.random.uniform(k, (E, E), jnp.float32, -bound, bound)
        return {'query': jax.random.normal(ks[0], (B, S, E), jnp.float32), 'key': jax.random.normal(ks[1], (B, S, E), jnp.float32), 'value': jax.random.normal(ks[2], (B, S, E), jnp.float32), 'Wq': mkw(ks[3]), 'Wk': mkw(ks[4]), 'Wv': mkw(ks[5]), 'Wo': mkw(ks[6])}
    _L1_xattn_all = _L1_xattn_setup()
    _L1_xattn_in = {k: v for k, v in _L1_xattn_all.items() if k in ('Wq', 'Wk', 'Wv', 'Wo')}
    del _L1_xattn_all

    def _L1_ffn_setup():
        import jax, jax.numpy as jnp
        import numpy as np
        EPS = 1e-12

        def rms_norm(t, gamma):
            n = jnp.maximum(jnp.linalg.norm(t, axis=-1, keepdims=True), EPS)
            scale = jnp.sqrt(jnp.asarray(t.shape[-1], t.dtype))
            return t / n * scale * gamma
        key = jax.random.key(seed)
        ks = jax.random.split(key, 4)
        b, s, d = (4, 1024, 256)
        e, t = (8, 128)
        hidden = 4 * d
        return {'x': jax.random.normal(ks[0], (b, s, d), dtype=jnp.float32), 'gamma_x': jnp.ones((d,), dtype=jnp.float32), 'gamma_slot': jnp.ones((d,), dtype=jnp.float32), 'slot_embeds': jax.random.normal(ks[1], (e, t, d), dtype=jnp.float32), 'w1': jax.random.normal(ks[2], (d, hidden), dtype=jnp.float32) * (1.0 / np.sqrt(d)), 'w2': jax.random.normal(ks[3], (hidden, d), dtype=jnp.float32) * (1.0 / np.sqrt(hidden))}
    _L1_ffn_all = _L1_ffn_setup()
    _L1_ffn_in = {k: v for k, v in _L1_ffn_all.items() if k in ('gamma_x', 'gamma_slot', 'slot_embeds', 'w1', 'w2')}
    del _L1_ffn_all
    return {'x': x, 'ctx_1024': ctx_1024, 'L0_xattn_Wq': _L0_xattn_in['Wq'], 'L0_xattn_Wk': _L0_xattn_in['Wk'], 'L0_xattn_Wv': _L0_xattn_in['Wv'], 'L0_xattn_Wo': _L0_xattn_in['Wo'], 'L0_xattn_bo': _L0_xattn_in['bo'], 'L0_ffn_W1': _L0_ffn_in['W1'], 'L0_ffn_b1': _L0_ffn_in['b1'], 'L0_ffn_W2': _L0_ffn_in['W2'], 'L0_ffn_b2': _L0_ffn_in['b2'], 'L1_xattn_Wq': _L1_xattn_in['Wq'], 'L1_xattn_Wk': _L1_xattn_in['Wk'], 'L1_xattn_Wv': _L1_xattn_in['Wv'], 'L1_xattn_Wo': _L1_xattn_in['Wo'], 'L1_ffn_gamma_x': _L1_ffn_in['gamma_x'], 'L1_ffn_gamma_slot': _L1_ffn_in['gamma_slot'], 'L1_ffn_slot_embeds': _L1_ffn_in['slot_embeds'], 'L1_ffn_w1': _L1_ffn_in['w1'], 'L1_ffn_w2': _L1_ffn_in['w2']}

def reference(x, ctx_1024, L0_xattn_Wq, L0_xattn_Wk, L0_xattn_Wv, L0_xattn_Wo, L0_xattn_bo, L0_ffn_W1, L0_ffn_b1, L0_ffn_W2, L0_ffn_b2, L1_xattn_Wq, L1_xattn_Wk, L1_xattn_Wv, L1_xattn_Wo, L1_ffn_gamma_x, L1_ffn_gamma_slot, L1_ffn_slot_embeds, L1_ffn_w1, L1_ffn_w2):
    import jax
    import jax.numpy as jnp

    def _L0_xattn_ref(x, hint_control, Wq, Wk, Wv, Wo, bo):
        import jax, jax.numpy as jnp
        import numpy as np
        H, DH, WSIZE, PE_LEN = (8, 64, 4, 75)

        def sinusoidal_pe(T, d, n=10000.0):
            pos = jnp.arange(T, dtype=jnp.float32)[:, None]
            denom = jnp.power(n, 2.0 * jnp.arange(d // 2, dtype=jnp.float32) / d)
            ang = pos / denom
            pe = jnp.zeros((T, d), dtype=jnp.float32)
            pe = pe.at[:, 0::2].set(jnp.sin(ang))
            pe = pe.at[:, 1::2].set(jnp.cos(ang))
            return pe
        B, NQ, _ = x.shape
        NK = hint_control.shape[1]
        scale = DH ** (-0.5)
        pe = sinusoidal_pe(PE_LEN, hint_control.shape[-1])[:NK]
        hc = hint_control + pe[None]
        q = (x @ Wq).reshape(B, NQ, H, DH).transpose(0, 2, 1, 3)
        k = (hc @ Wk).reshape(B, NK, H, DH).transpose(0, 2, 1, 3)
        v = (hc @ Wv).reshape(B, NK, H, DH).transpose(0, 2, 1, 3)
        qb = q.reshape(B, H, WSIZE, NQ // WSIZE, DH)
        kb = k.reshape(B, H, WSIZE, NK // WSIZE, DH)
        vb = v.reshape(B, H, WSIZE, NK // WSIZE, DH)
        sim = jnp.einsum('bhwid,bhwjd->bhwij', qb, kb) * scale
        attn = jax.nn.softmax(sim, axis=-1)
        out = jnp.einsum('bhwij,bhwjd->bhwid', attn, vb)
        out = out.reshape(B, H, NQ, DH).transpose(0, 2, 1, 3).reshape(B, NQ, H * DH)
        return out @ Wo + bo

    def _L0_ffn_ref(x, W1, b1, W2, b2):
        import jax, jax.numpy as jnp
        import numpy as np
        NUM_GEMMS = 8
        HIDDEN = 256
        INTER = 1024
        orig_shape = x.shape
        token_num = int(np.prod(orig_shape[:-1]))
        m = token_num // NUM_GEMMS
        xg = x.reshape(NUM_GEMMS, m, HIDDEN)
        h1 = jnp.einsum('gmh,goh->gmo', xg, W1) + b1[:, None, :]
        h2 = jnp.einsum('gmo,gho->gmh', h1, W2) + b2[:, None, :]
        return h2.reshape(orig_shape)

    def _L1_xattn_ref(query, key, value, Wq, Wk, Wv, Wo):
        import jax, jax.numpy as jnp
        import numpy as np
        EMBED_DIM = 256
        NUM_HEADS = 16
        HEAD_DIM = EMBED_DIM // NUM_HEADS
        B, L, E = query.shape
        H, D = (NUM_HEADS, HEAD_DIM)
        scale = D ** (-0.5)
        q = (query @ Wq.T).reshape(B, L, H, D) * scale
        k = (key @ Wk.T).reshape(B, -1, H, D)
        v = (value @ Wv.T).reshape(B, -1, H, D)
        scores = jax.nn.sigmoid(jnp.einsum('blhd,bshd->bhls', q, k))
        o = jnp.einsum('bhls,bshd->blhd', scores, v).reshape(B, L, E)
        return o @ Wo.T

    def _L1_ffn_ref(x, gamma_x, gamma_slot, slot_embeds, w1, w2):
        import jax, jax.numpy as jnp
        import numpy as np
        EPS = 1e-12

        def rms_norm(t, gamma):
            n = jnp.maximum(jnp.linalg.norm(t, axis=-1, keepdims=True), EPS)
            scale = jnp.sqrt(jnp.asarray(t.shape[-1], t.dtype))
            return t / n * scale * gamma
        b, s, d = x.shape
        e, t, _ = slot_embeds.shape
        xn = rms_norm(x, gamma_x)
        se = rms_norm(slot_embeds, gamma_slot)
        logits = jnp.einsum('bsd,etd->bset', xn, se)
        dispatch = jax.nn.softmax(logits, axis=1)
        slots = jnp.einsum('bsd,bset->betd', xn, dispatch)
        h = jax.nn.gelu(slots @ w1, approximate=False)
        processed = h @ w2
        combine = jax.nn.softmax(logits.reshape(b, s, e * t), axis=-1)
        out = jnp.einsum('bnd,bsn->bsd', processed.reshape(b, e * t, d), combine)
        return out
    x = x + _L0_xattn_ref(_layernorm(x, axis=-1), ctx_1024, L0_xattn_Wq, L0_xattn_Wk, L0_xattn_Wv, L0_xattn_Wo, L0_xattn_bo)
    x = x + _L0_ffn_ref(_layernorm(x, axis=-1), L0_ffn_W1, L0_ffn_b1, L0_ffn_W2, L0_ffn_b2)
    x = x + _L1_xattn_ref(_layernorm(x, axis=-1), ctx_1024, ctx_1024, L1_xattn_Wq, L1_xattn_Wk, L1_xattn_Wv, L1_xattn_Wo)
    x = x + _L1_ffn_ref(_layernorm(x, axis=-1), L1_ffn_gamma_x, L1_ffn_gamma_slot, L1_ffn_slot_embeds, L1_ffn_w1, L1_ffn_w2)
    return x

_drawn_inputs = setup_inputs


def setup_inputs(seed=0):
    import zlib

    import numpy as np

    out = dict(_drawn_inputs(seed))
    spreads = {'L0_xattn_bo': (0.0, 0.526), 'L1_ffn_gamma_x': (1.0, 0.6), 'L1_ffn_gamma_slot': (1.0, 0.6)}
    factors = {'L0_ffn_b1': 8.0, 'L0_ffn_b2': 8.0, 'L1_ffn_slot_embeds': 8.0}
    for name, (base, spread) in spreads.items():
        noise = np.random.default_rng([zlib.crc32(name.encode()), seed]).standard_normal(out[name].shape)
        drawn = base * np.exp(spread * noise) if base else spread * noise
        out[name] = jnp.asarray(drawn.astype(out[name].dtype))
    for name, factor in factors.items():
        out[name] = (out[name] * factor).astype(out[name].dtype)
    return out
```

```python
import numpy as np
import concourse.bass as bass
from concourse import mybir
from contextlib import ExitStack

F32 = mybir.dt.float32
F32R = mybir.dt.float32r
ALU = mybir.AluOpType
ACT = mybir.ActivationFunctionType
AXX = mybir.AxisListType.X

P = 128
BATCH, SEQ, D = 2, 1024, 256
TOKENS = BATCH * SEQ
TILES = TOKENS // P
GROUPS = 8
GT = TOKENS // GROUPS
KT = D // P
KEYS = 64
H0, DH0 = 8, 64
WK = KEYS // 4
H1, DH1 = 16, 16
PAIRS = H1 // 2
INTER = 1024
OC = INTER // P
SLOTS = 1024
SM = SLOTS // P
XW = D + 2
LN_EPS, NORM_EPS = 1e-5, 1e-12
WPARTS = 4
LOWEST = -3.0e38


def build(nc, x, ctx2, pe, wq0T, wk0, wv0, wo0, bo, fw1, fb1, fw2T, fb2, wq1T, wk1T, wv1T, wo1T,
          gx, gs, slot, w1, w2, ident_in, mask_k, mask_v, out):
    es = ExitStack()
    with es:
        base = 1152
        KB = 1024

        def place(name, cols, kb, dt=F32):
            return nc.alloc_sbuf_tensor_at(name, [P, cols], dt, offset=base + int(kb * KB))

        def sem(name):
            return es.enter_context(nc.semaphore(name))

        xs = place("xs", TILES * D, 0)
        ident = place("ident", P, 16)
        ones = place("ones", P, 16.5)
        ones_r = place("ones_r", P, 17, F32R)
        small = place("small", 256, 17.5)
        se_hi = place("se_hi", KT * SLOTS, 19, F32R)
        se_lo = place("se_lo", KT * SLOTS, 27, F32R)
        se_f = place("se_f", KT * SLOTS, 27)
        wq1_hi = place("wq1_hi", KT * D, 35, F32R)
        wq1_lo = place("wq1_lo", KT * D, 37, F32R)
        wq1_f = place("wq1_f", KT * D, 37)
        wo1_hi = place("wo1_hi", KT * D, 39, F32R)
        wo1_lo = place("wo1_lo", KT * D, 41, F32R)
        wo1_f = place("wo1_f", KT * D, 41)
        kc_hi = place("kc_hi", BATCH * KT * P, 43, F32R)
        kc_lo = place("kc_lo", BATCH * KT * P, 45, F32R)
        kc_f = place("kc_f", BATCH * KT * P, 45)
        vc_hi = place("vc_hi", BATCH * PAIRS * 32, 47, F32R)
        vc_lo = place("vc_lo", BATCH * PAIRS * 32, 49, F32R)
        vc_f = place("vc_f", BATCH * PAIRS * 32, 49)
        a_hi = place("a_hi", GROUPS * KT * P, 51, F32R)
        a_lo = place("a_lo", GROUPS * KT * P, 59, F32R)
        vw_hi = place("vw_hi", GROUPS * D, 67, F32R)
        vw_lo = place("vw_lo", GROUPS * D, 75, F32R)
        vw_f = place("vw_f", GROUPS * D, 75)
        w1r = place("w1r", OC * D, 83)
        w2r = place("w2r", OC * D, 91)
        c_hi = place("c_hi", KT * D, 99, F32R)
        c_lo = place("c_lo", KT * D, 101, F32R)
        z0 = place("z0", D, 103)
        z = place("z", D, 104)
        z_hi = place("z_hi", D, 105, F32R)
        z_lo = place("z_lo", D, 106, F32R)
        b1t = place("b1t", OC, 107)
        prod = place("prod", OC * D, 139.5)
        probs = place("probs", 2 * P, 108)
        pT_hi = place("pT_hi", 2 * P, 109, F32R)
        pT_lo = place("pT_lo", 2 * P, 110, F32R)
        vwt = place("vwt", H0 * D, 123)
        wk0s = place("wk0s", KT * 512, 176)
        wv0s = place("wv0s", KT * 512, 180)
        wq0s = place("wq0s", 4 * D, 184)
        wo0s = place("wo0s", 4 * D, 188)
        kT0 = place("kT0", 512, 192)
        vT0 = place("vT0", 512, 194)
        ctx_s = place("ctx_s", KT * BATCH * P, 196)
        hcT = place("hcT", KT * P, 198)
        pe_s = place("pe_s", KT * KEYS, 199)
        mk_s = place("mk_s", P, 199.5)
        mv_s = place("mv_s", 32, 200)
        bo_s = place("bo_s", D, 201)
        wk1s = place("wk1s", KT * D, 202)
        wv1s = place("wv1s", KT * D, 204)
        slot_s = place("slot_s", SM * D, 131)
        sq = place("sq", SM * D, 206.5)
        xn_hi = place("xn_hi", TILES * XW, 51, F32R)
        xn_lo = place("xn_lo", TILES * XW, 67.125, F32R)
        logits = place("logits", TILES * SLOTS, 84)
        kw_hi = place("kw_hi", PAIRS * P, 148, F32R)
        kw_lo = place("kw_lo", PAIRS * P, 152, F32R)
        vw1_hi = place("vw1_hi", PAIRS * P, 156, F32R)
        vw1_lo = place("vw1_lo", PAIRS * P, 160, F32R)
        q_hi = place("q_hi", KT * GT, 176, F32R)
        q_lo = place("q_lo", KT * GT, 178, F32R)
        o_hi = place("o_hi", KT * GT, 180, F32R)
        o_lo = place("o_lo", KT * GT, 182, F32R)
        sig = [place(f"sig{i}", 2 * GT, 184 + 2 * i) for i in range(2)]
        sig_hi = [place(f"sig_hi{i}", 2 * GT, 188 + 2 * i, F32R) for i in range(2)]
        sig_lo = [place(f"sig_lo{i}", 2 * GT, 192 + 2 * i, F32R) for i in range(2)]
        colmax = place("colmax", BATCH * SLOTS, 196)
        lnx, xT_hi, xT_lo = {}, {}, {}
        for ch, kb in zip("ABCD", (111, 117, 164, 170)):
            lnx[ch] = place(f"ln{ch}", 2 * D, kb)
            xT_hi[ch] = place(f"xT_hi{ch}", KT * GT, kb + 2, F32R)
            xT_lo[ch] = place(f"xT_lo{ch}", KT * GT, kb + 4, F32R)
        w1_hi = place("w1_hi", KT * INTER, 19, F32R)
        w1_lo = place("w1_lo", KT * INTER, 27, F32R)
        w1_f = place("w1_f", KT * INTER, 27)
        w2_hi = place("w2_hi", OC * D, 35, F32R)
        w2_lo = place("w2_lo", OC * D, 43, F32R)
        w2_f = place("w2_f", OC * D, 43)
        ef = [place(f"ef{i}", SLOTS, 148 + 4 * i) for i in range(2)]
        e_hi = [place(f"e_hi{i}", SLOTS, 156 + 4 * i, F32R) for i in range(2)]
        e_lo = [place(f"e_lo{i}", SLOTS, 164 + 4 * i, F32R) for i in range(2)]
        slT_hi = place("slT_hi", KT * BATCH * SLOTS, 172, F32R)
        slT_lo = place("slT_lo", KT * BATCH * SLOTS, 188, F32R)
        sf = [place(f"sf{i}", D, 204 + i) for i in range(2)]
        cmb = place("cmb", BATCH * SLOTS, 206)
        hf = [place(f"hf{i}", 2 * GT, 148 + 2 * i) for i in range(2)]
        h_hi = [place(f"h_hi{i}", 2 * GT, 152 + 4 * i, F32R) for i in range(4)]
        h_lo = [place(f"h_lo{i}", 2 * GT, 154 + 4 * i, F32R) for i in range(4)]
        e2T_hi = [place(f"e2T_hi{i}", SLOTS, 156 + 8 * i, F32R) for i in range(2)]
        e2T_lo = [place(f"e2T_lo{i}", SLOTS, 160 + 8 * i, F32R) for i in range(2)]
        y = [place(f"y{i}", D, 172 + i) for i in range(2)]

        sc = {}
        at = 0
        for name, n in [("bnA", 12), ("bnB", 12), ("bnC", 12), ("bnD", 12), ("mvA", 4), ("mvB", 4),
                        ("mvC", 4), ("mvD", 4), ("veA", 2), ("veB", 2), ("veC", 2), ("veD", 2),
                        ("rsA", 2), ("rsB", 2), ("rsC", 2), ("rsD", 2), ("t1", 2), ("t2", 2), ("t3", 2),
                        ("rstd", 2), ("eps", 2), ("mhalf", 8), ("mx", 16), ("sm", 16), ("rc", 16),
                        ("rowmax", 16), ("nrow", 16), ("cm", 16), ("ss", 8), ("rss", 8), ("gxs", 2),
                        ("gss", 2), ("gg", 2), ("rec", 2), ("rec4", 2)]:
            sc[name] = small[:, at:at + n]
            at += n
        assert at <= 256

        bank = [es.enter_context(nc.psum_tensor(f"bank{i}", [P, 512], F32)) for i in range(8)]
        vw_dram = nc.dram_tensor("vw_bounce", [P, H0 * D], F32).ap()

        in_x0, in_x, in_ctx, in_kv0, in_o0, in_l1, in_slot, in_g, in_id = (
            sem(n) for n in ("in_x0", "in_x", "in_ctx", "in_kv0", "in_o0", "in_l1", "in_slot", "in_g", "in_id"))
        in_w = [sem(f"in_w{k}") for k in range(WPARTS)]
        in_b, in_ew, vw_out, vw_in, kv_in = (sem(n) for n in ("in_b", "in_ew", "vw_out", "vw_in", "kv_in"))
        out_done = [sem(f"out_done{i}") for i in range(2)]
        consts, pro_dve, pro_act, pro_pe, pro_pool = (sem(n) for n in ("consts", "pro_dve", "pro_act", "pro_pe", "pro_pool"))
        tick = sem("tick")
        bn_done, st_ready, rs_step, rs_ready, ln_ready, xT_psum, xT_hid, xT_lod = ({} for _ in range(8))
        for ch in "ABCD":
            bn_done[ch] = sem(f"bn_done{ch}")
            st_ready[ch] = sem(f"st_ready{ch}")
            rs_step[ch] = sem(f"rs_step{ch}")
            rs_ready[ch] = sem(f"rs_ready{ch}")
            ln_ready[ch] = sem(f"ln_ready{ch}")
            xT_psum[ch] = sem(f"xT_psum{ch}")
            xT_hid[ch] = sem(f"xT_hi_done{ch}")
            xT_lod[ch] = sem(f"xT_lo_done{ch}")
        x_ready = {"B": sem("x1_ready"), "C": sem("x2_ready"), "D": sem("x3_ready")}
        (sc_psum, sm_step, e_in, e_out, p_ready, pT_psum, pT_hid, pT_lod, a_out, w_used, c_hid, c_lod, z_prod, z_step,
         z_hid, z_lod, b_out) = (sem(n) for n in (
             "sc_psum", "sm_step", "e_in", "e_out", "p_ready", "pT_psum", "pT_hi_done", "pT_lo_done", "a_out",
             "w_used", "c_hi_done", "c_lo_done", "z_prod", "z_step", "z_hi_done", "z_lo_done", "b_out"))
        (q_psum, q_hid, q_lod, s_psum, s_sig, s_hid, s_lod, o_part, o_hid, o_lod, c_out, l_psum, l_sb, rowmax_done,
         colmax_done, xn_hid, xn_lod) = (sem(n) for n in (
             "q_psum", "q_hi_done", "q_lo_done", "s_psum", "s_sig", "s_hi_done", "s_lo_done", "o_part", "o_hi_done",
             "o_lo_done", "c_out", "l_psum", "l_sb", "rowmax_done", "colmax_done", "xn_hi_done", "xn_lo_done"))
        cmT, cm_red, cm_diag, cm_bc, cm_sb = (sem(n) for n in ("cmT", "cm_red", "cm_diag", "cm_bc", "cm_sb"))
        (d_sub, d_exp, d_hi, d_lo, d_lo2, sl_psum, sl_rec, sl_norm, slT_psum, slT_hid, slT_lod) = (sem(n) for n in (
            "d_sub", "d_exp", "d_hi", "d_lo", "d_lo2", "sl_psum", "sl_rec", "sl_norm", "slT_psum", "slT_hi_done", "slT_lo_done"))
        (ew_scaled, ew_hi, ew_lo, h_psum, g_act, g_hi, g_lo, p_part, pr_hi, pr_lo) = (sem(n) for n in (
            "ew_scaled", "ew_hi", "ew_lo", "h_psum", "g_act", "g_hi", "g_lo", "p_part", "pr_hi", "pr_lo"))
        (nrow_done, e2_act, e2_psum, e2_hi, e2_lo, y_psum, y_rec, y_ready) = (sem(n) for n in (
            "nrow_done", "e2_act", "e2_psum", "e2_hi", "e2_lo", "y_psum", "y_rec", "y_ready"))

        def cols(t, start, n):
            return t[:, start:start + n] if isinstance(start, int) else t[:, bass.ds(start, n)]

        def xg(g):
            return cols(xs, g * (2 * D), 2 * D)

        def f(ap):
            return ap.bitcast(F32)

        def split3(outp, lhs, rhs, start, stop):
            nc.tensor.matmul(outp, lhs[0], rhs[1], start=start, stop=False, skip_group_check=True)
            nc.tensor.matmul(outp, lhs[1], rhs[0], start=False, stop=False, skip_group_check=True)
            return nc.tensor.matmul(outp, lhs[0], rhs[0], start=False, stop=stop, skip_group_check=True)

        def later(v, least=1):
            return not isinstance(v, int) or v >= least

        def loop(eng, body, peel, lo, hi):
            for r in range(0, lo):
                body(r)
            with eng.Fori(lo, hi) as r:
                body(r)
            for r in range(hi, peel):
                body(r)

        def has(r, shift, n=GROUPS):
            return not isinstance(r, int) or 0 <= r - shift < n

        def held(eng, s, v):
            eng.wait_ge(s, v)
            if not isinstance(v, int):
                eng.sem_inc(tick, 1)

        block = es.enter_context(nc.Block())

        @block.sync
        def _(sp):
            def load_w(g, k):
                part = slice(2 * k * D, 2 * (k + 1) * D)
                if later(g):
                    held(sp, w_used, 4 * g - 3 + k)
                    held(sp, z_prod, OC * (g - 1) + 2 * k + 2)
                for dst, src in ((w1r, fw1), (w2r, fw2T)):
                    s = src[g, :, part] if isinstance(g, int) else src[bass.ds(g, 1), :, part].rearrange("a p n -> (a p) n")
                    sp.dma_start(dst[:, part], s).then_inc(in_w[k], 16)

            def load_b(g):
                if later(g):
                    held(sp, z_step, 4 * g)
                s1 = fb1[g, :, :] if isinstance(g, int) else fb1[bass.ds(g, 1), :, :].rearrange("a p n -> (a p) n")
                s2 = fb2[g:g + 1, :] if isinstance(g, int) else fb2[bass.ds(g, 1), :]
                sp.dma_start(b1t[:, :], s1).then_inc(in_b, 16)
                sp.dma_start(z0[0:1, :], s2).then_inc(in_b, 16)

            xv = x.rearrange("(t p) d -> p t d", p=P)
            xsv = xs[:, :].rearrange("p (t d) -> p t d", d=D)
            sp.dma_start(xsv[:, 0:2], xv[:, 0:2]).then_inc(in_x0, 16)
            for k in range(WPARTS):
                load_w(0, k)
            sp.wait_ge(consts, 4)
            load_b(0)
            sp.dma_start(xsv[:, 2:], xv[:, 2:]).then_inc(in_x, 16)
            sp.wait_ge(pro_dve, 9)
            sp.dma_start(vw_dram, vwt[:, :]).then_inc(vw_out, 16)
            sp.wait_ge(vw_out, 16)
            for h in range(H0):
                sp.dma_start(vw_f[WK * h:WK * (h + 1), :].rearrange("j (g n) -> j g n", g=GROUPS),
                             vw_dram[:, h * D:(h + 1) * D].rearrange("(g j) n -> j g n", g=GROUPS)).then_inc(vw_in, 16)

            def load_kv(b):
                for dst, src in ((kw_hi, kc_hi), (kw_lo, kc_lo)):
                    d4 = f(dst[:, :]).rearrange("p (c i n) -> p c i n", c=KT, i=4)
                    s3 = f(src[:, b * KT * P:(b + 1) * KT * P]).rearrange("p (c n) -> p c n", c=KT)
                    for i in range(4):
                        sp.dma_start(d4[32 * i:32 * i + 32, :, i, :], s3[32 * i:32 * i + 32, :, :]).then_inc(kv_in, 16)
                for dst, src in ((vw1_hi, vc_hi), (vw1_lo, vc_lo)):
                    d4 = f(dst[:, :]).rearrange("p (c i n) -> p c i n", c=KT, i=4)
                    s4 = f(src[:, b * PAIRS * 32:(b + 1) * PAIRS * 32]).rearrange("p (c i n) -> p c i n", c=KT, i=4)
                    for i in range(4):
                        sp.dma_start(d4[:, :, i, 32 * i:32 * i + 32], s4[:, :, i, :]).then_inc(kv_in, 16)

            with sp.Fori(1, GROUPS) as g:
                for k in range(WPARTS):
                    load_w(g, k)
                load_b(g)
            sp.wait_ge(consts, 6)
            sp.wait_ge(pro_act, 13)
            sp.wait_ge(pro_dve, 18)
            load_kv(0)
            sp.wait_ge(o_part, 4 * (GROUPS // 2))
            load_kv(1)
            sp.wait_ge(c_out, GROUPS)
            sp.wait_ge(l_psum, 4 * GROUPS)
            sp.dma_start(w1_f[:, :].rearrange("p (k n) -> p k n", k=KT), w1.rearrange("(k p) n -> p k n", p=P)).then_inc(in_ew, 16)
            sp.dma_start(w2_f[:, :].rearrange("p (c n) -> p c n", c=OC), w2.rearrange("(c p) n -> p c n", p=P)).then_inc(in_ew, 16)

            ov = out.rearrange("(t p) d -> t p d", p=P)
            with sp.Fori(0, TILES - 1, 2) as t:
                for s in range(2):
                    held(sp, y_ready, t + s + 1)
                    sp.dma_start(ov[bass.ds(t + s, 1), :, :].rearrange("a p d -> (a p) d"), y[s][:, :]).then_inc(out_done[s], 16)
            for s in range(2):
                sp.wait_ge(out_done[s], 16 * (TILES // 2))

        @block.gpsimd
        def _(pool):
            g_ = nc.gpsimd

            def await_(s, v):
                held(pool, s, v)

            g_.memset(ones[:, :], 1.0).then_inc(consts, 1)
            g_.memset(sc["eps"], LN_EPS).then_inc(consts, 1)
            g_.memset(sc["mhalf"], -0.5).then_inc(consts, 1)
            g_.memset(z0[:, :], 0.0).then_inc(consts, 1)
            for t in (kw_hi, kw_lo, vw1_hi, vw1_lo):
                last = g_.memset(f(t[:, :]), 0.0)
            last.then_inc(consts, 2)
            pool.wait_ge(consts, 6)

            def rstd(ch, g):
                await_(st_ready[ch], 2 * g + 2)
                n = 1 if ch != "D" else 6
                step = [0]

                def own(ins):
                    step[0] += 1
                    ins.then_inc(rs_step[ch], 1)
                    await_(rs_step[ch], n * g + step[0])

                var = sc["mv" + ch][:, 1:4:2]
                own(g_.tensor_tensor(sc["ve" + ch], var, sc["eps"], ALU.add))
                if ch != "D":
                    g_.tensor_tensor(sc["rs" + ch], sc["ve" + ch], sc["mhalf"][:, 0:2], ALU.pow).then_inc(rs_ready[ch], 1)
                    return
                own(g_.tensor_tensor(sc["rstd"], sc["veD"], sc["mhalf"][:, 0:2], ALU.pow))
                own(g_.tensor_tensor(sc["t1"], var, sc["rstd"], ALU.mult))
                own(g_.tensor_tensor(sc["t2"], sc["t1"], sc["rstd"], ALU.mult))
                own(g_.tensor_scalar(sc["t3"], sc["t2"], NORM_EPS ** 2 / D, None, ALU.max))
                own(g_.tensor_tensor(sc["t1"], sc["t3"], sc["mhalf"][:, 0:2], ALU.pow))
                g_.tensor_tensor(sc["rsD"], sc["t1"], sc["rstd"], ALU.mult).then_inc(rs_ready[ch], 1)

            rstd("A", 0)
            pool.wait_ge(pro_act, 1)
            g_.tensor_scalar(sc["ss"], sc["ss"], NORM_EPS ** 2, None, ALU.max).then_inc(pro_pool, 1)
            pool.wait_ge(pro_pool, 1)
            g_.tensor_tensor(sc["rss"], sc["ss"], sc["mhalf"], ALU.pow).then_inc(pro_pool, 1)
            pool.wait_ge(pro_pool, 2)
            g_.tensor_scalar(sc["rss"], sc["rss"], float(D) ** 0.5, None, ALU.mult).then_inc(pro_pool, 1)

            def bias(g):
                def own(n, ins):
                    ins.then_inc(z_step, 1)
                    await_(z_step, 4 * g + n)

                await_(z_prod, OC * (g + 1))
                own(1, g_.tensor_tensor(prod[:, 0:4 * D], prod[:, 0:4 * D], prod[:, 4 * D:8 * D], ALU.add))
                own(2, g_.tensor_tensor(prod[:, 0:2 * D], prod[:, 0:2 * D], prod[:, 2 * D:4 * D], ALU.add))
                own(3, g_.tensor_tensor(prod[:, 0:D], prod[:, 0:D], prod[:, D:2 * D], ALU.add))
                if later(g):
                    await_(z_hid, g)
                await_(in_b, 32 * (g + 1))
                g_.tensor_tensor(z[:, :], prod[:, 0:D], z0[:, :], ALU.add).then_inc(z_step, 1)

            def bias_lo(g):
                await_(z_hid, g + 1)
                g_.tensor_tensor(z_lo[:, :], z[:, :], f(z_hi[:, :]), ALU.subtract).then_inc(z_lod, 1)

            def round_1a(r):
                if has(r, 1):
                    rstd("B", r - 1)
                if has(r, 0):
                    bias(r)
                if has(r, -1):
                    rstd("A", r + 1)
                if has(r, 0):
                    bias_lo(r)

            loop(pool, round_1a, GROUPS + 1, 2, GROUPS - 1)

            pool.wait_ge(b_out, GROUPS)
            for t, v in ((xn_hi, 1.0), (xn_lo, 0.0)):
                g_.memset(f(t[:, :]).rearrange("p (t n) -> p t n", n=XW)[:, :, D:XW], v)

            def xn_low(g):
                await_(xn_hid, g + 1)
                g_.tensor_tensor(cols(xn_lo, g * (2 * XW), 2 * XW).rearrange("p (t n) -> p t n", n=XW)[:, :, 0:D],
                                 lnx["D"][:, :].rearrange("p (t n) -> p t n", n=D),
                                 f(cols(xn_hi, g * (2 * XW), 2 * XW)).rearrange("p (t n) -> p t n", n=XW)[:, :, 0:D],
                                 ALU.subtract).then_inc(xn_lod, 1)

            def round_1b(r):
                if has(r, 1):
                    rstd("D", r - 1)
                if has(r, 1):
                    xn_low(r - 1)
                if has(r, -1):
                    rstd("C", r + 1)

            rstd("C", 0)
            loop(pool, round_1b, GROUPS + 1, 2, GROUPS - 1)

            def low2(n, s):
                await_(d_hi, n + 1)
                if later(n, 2):
                    await_(sl_psum, n - 1)
                g_.tensor_tensor(e_lo[s][:, 512:], ef[s][:, 512:], f(e_hi[s][:, 512:]), ALU.subtract).then_inc(d_lo2, 1)

            pool.wait_ge(xn_lod, GROUPS)
            for n in range(2):
                low2(n, n)
            with pool.Fori(2, 15, 2) as n:
                for s in range(2):
                    low2(n + s, s)

        @block.scalar
        def _(act):
            a_ = nc.scalar
            act.dma_start(ctx_s[:, :], ctx2).then_inc(in_ctx, 16)
            act.dma_start(pe_s[:, :], pe).then_inc(in_ctx, 16)
            act.dma_start(wk0s[:, :].rearrange("p (k n) -> p k n", k=KT), wk0.rearrange("(k p) n -> p k n", p=P)).then_inc(in_kv0, 16)
            act.dma_start(wv0s[:, :].rearrange("p (k n) -> p k n", k=KT), wv0.rearrange("(k p) n -> p k n", p=P)).then_inc(in_kv0, 16)
            act.dma_start(wq0s[:, :].rearrange("p (k n) -> p k n", k=4), wq0T.rearrange("(k p) n -> p k n", p=P)).then_inc(in_o0, 16)
            act.dma_start(wo0s[:, :].rearrange("p (k n) -> p k n", k=4), wo0.rearrange("(k p) n -> p k n", p=P)).then_inc(in_o0, 16)
            act.dma_start(bo_s[:, :], bo.to_broadcast([P, D])).then_inc(in_o0, 16)
            act.dma_start(ident[:, :], ident_in).then_inc(in_id, 16)
            act.dma_start(slot_s[:, :].rearrange("p (m n) -> p m n", m=SM), slot.rearrange("(m p) n -> p m n", p=P)).then_inc(in_slot, 16)
            act.dma_start(sc["gxs"], gx).then_inc(in_g, 16)
            act.dma_start(sc["gss"], gs).then_inc(in_g, 16)
            for dst, src in ((wk1s, wk1T), (wv1s, wv1T), (wq1_f, wq1T), (wo1_f, wo1T)):
                act.dma_start(dst[:, :].rearrange("p (k n) -> p k n", k=KT), src.rearrange("(k p) n -> p k n", p=P)).then_inc(in_l1, 16)
            act.dma_start(mk_s[:, :], mask_k).then_inc(in_l1, 16)
            act.dma_start(mv_s[:, :], mask_v).then_inc(in_l1, 16)

            def copy(dst, src, done, n=1):
                a_.activation(dst, src, ACT.Copy).then_inc(done, n)

            act.wait_ge(in_slot, 16)
            for m in range(SM):
                last = a_.activation(sq[:, m * D:(m + 1) * D], slot_s[:, m * D:(m + 1) * D], ACT.Square, accum_out=sc["ss"][:, m:m + 1])
            last.then_inc(pro_act, 1)
            act.wait_ge(consts, 1)
            copy(ones_r[:, :], ones[:, :], pro_act)
            act.wait_ge(pro_pe, 1)
            copy(kT0[:, :], bank[0][:, :], pro_act)
            for k in range(KT):
                for par in range(2):
                    act.wait_ge(pro_pe, 3)
                    copy(a_hi[:, :].rearrange("p (g k h j) -> p k h g j", g=GROUPS, k=KT, h=H0)[:, k, par::2],
                         bank[2 + 2 * k + par][:, :].rearrange("p (h g j) -> p h g j", h=4, g=GROUPS), pro_act)
            act.wait_ge(in_l1, 96)
            copy(wq1_hi[:, :], wq1_f[:, :], pro_act)
            copy(wo1_hi[:, :], wo1_f[:, :], pro_act)
            act.wait_ge(vw_in, 16 * H0)
            copy(vw_hi[:, :], vw_f[:, :], pro_act)

            def norm_T_hi(ch, g):
                act.wait_ge(xT_psum[ch], g + 1)
                bk = {"A": 0, "B": 3, "C": 0, "D": 1}[ch]
                copy(xT_hi[ch][:, :], bank[bk][:, :], xT_hid[ch])

            def late_prologue():
                act.wait_ge(pro_dve, 16)
                copy(kc_hi[:, :], kc_f[:, :], pro_act)
                copy(vc_hi[:, :], vc_f[:, :], pro_act, 2)
                act.wait_ge(pro_pe, 6)
                act.wait_ge(pro_dve, 17)
                for k in range(KT):
                    for hlf in range(2):
                        a_.activation(se_f[:, k * SLOTS + hlf * 512:k * SLOTS + hlf * 512 + 512], bank[4 + 2 * k + hlf][:, :],
                                      ACT.Copy, scale=sc["gg"][:, k:k + 1]).then_inc(pro_act, 1)
                act.wait_ge(pro_act, 17)
                copy(se_hi[:, :], se_f[:, :], pro_act)

            def bias_product(g, k):
                act.wait_ge(in_w[k], 32 * (g + 1))
                if k == 0:
                    act.wait_ge(in_b, 32 * (g + 1))
                    if later(g):
                        act.wait_ge(z_step, 4 * g)
                for c in (2 * k, 2 * k + 1):
                    a_.activation(prod[:, c * D:(c + 1) * D], w2r[:, c * D:(c + 1) * D], ACT.Copy, scale=b1t[:, c:c + 1]).then_inc(z_prod, 1)

            def round_1a(r):
                if has(r, 0):
                    bias_product(r, 0)
                    bias_product(r, 1)
                    norm_T_hi("A", r)
                if has(r, 1):
                    norm_T_hi("B", r - 1)
                if has(r, 0):
                    act.wait_ge(e_in, r + 1)
                    a_.activation(probs[:, :], probs[:, :], ACT.Exp, scale=DH0 ** -0.5).then_inc(e_out, 1)
                    bias_product(r, 2)
                    bias_product(r, 3)
                    act.wait_ge(z_step, 4 * r + 4)
                    if later(r):
                        act.wait_ge(b_out, r)
                    copy(z_hi[:, :], z[:, :], z_hid)
                    act.wait_ge(pT_psum, r + 1)
                    copy(pT_hi[:, :], bank[2][:, 0:2 * P], pT_hid)
                    act.wait_ge(w_used, 4 * r + 4)
                    copy(c_hi[:, :], bank[5][:, :], c_hid)

            late_prologue()
            loop(act, round_1a, GROUPS + 1, 2, GROUPS - 1)

            def logit_copy(g, i):
                act.wait_ge(l_psum, 4 * g + i + 1)
                copy(cols(logits, g * (2 * SLOTS) + i * 512, 512), bank[6 + i % 2][:, :], l_sb)

            def sigmoid(g, j):
                act.wait_ge(s_psum, 4 * g + j + 1)
                if later(4 * g + j, 2):
                    act.wait_ge(s_lod, 4 * g + j - 1)
                a_.activation(sig[j % 2][:, :], bank[3 + j % 2][:, :], ACT.Sigmoid, scale=DH1 ** -0.5).then_inc(s_sig, 1)
                act.wait_ge(s_sig, 4 * g + j + 1)
                if later(4 * g + j, 2):
                    act.wait_ge(o_part, 4 * g + j - 1)
                copy(sig_hi[j % 2][:, :], sig[j % 2][:, :], s_hid)

            def round_1b(r):
                if has(r, 0):
                    norm_T_hi("C", r)
                if has(r, 2):
                    logit_copy(r - 2, 2)
                if has(r, 0):
                    act.wait_ge(q_psum, r + 1)
                    copy(q_hi[:, :], bank[2][:, :], q_hid)
                if has(r, 2):
                    logit_copy(r - 2, 3)
                if has(r, 0):
                    sigmoid(r, 0)
                    sigmoid(r, 1)
                if has(r, 1):
                    norm_T_hi("D", r - 1)
                if has(r, 0):
                    sigmoid(r, 2)
                if has(r, 1):
                    act.wait_ge(ln_ready["D"], 2 * r)
                    copy(cols(xn_hi, (r - 1) * (2 * XW), 2 * XW).rearrange("p (t n) -> p t n", n=XW)[:, :, 0:D],
                         lnx["D"][:, :].rearrange("p (t n) -> p t n", n=D), xn_hid)
                if has(r, 0):
                    sigmoid(r, 3)
                if has(r, 1):
                    logit_copy(r - 1, 0)
                if has(r, 0):
                    act.wait_ge(o_part, 4 * r + 4)
                    copy(o_hi[:, :], bank[5][:, :], o_hid)
                if has(r, 1):
                    logit_copy(r - 1, 1)

            loop(act, round_1b, GROUPS + 2, 2, GROUPS - 1)

            for b in range(BATCH):
                for i in range(2):
                    act.wait_ge(cm_bc, 2 * b + i + 1)
                    copy(cmb[:, b * SLOTS + i * 512:b * SLOTS + i * 512 + 512], bank[4 + 2 * b + i][:, :], cm_sb)

            def e_exp(n, s):
                act.wait_ge(d_sub, n + 1)
                a_.activation(ef[s][:, :], ef[s][:, :], ACT.Exp).then_inc(d_exp, 1)

            def e_high(n, s):
                act.wait_ge(d_exp, n + 1)
                if later(n, 2):
                    act.wait_ge(sl_psum, n - 1)
                copy(e_hi[s][:, :], ef[s][:, :], d_hi)

            def slT_high(n, s):
                act.wait_ge(slT_psum, n + 1)
                copy(cols(slT_hi, n * (2 * P), 2 * P), bank[2 + s][:, 0:2 * P], slT_hid)

            def step_2(n, s):
                if has(n, -2, 16):
                    e_high(n + 2, s)
                if has(n, 0, 16):
                    slT_high(n, s)
                if has(n, -3, 16):
                    e_exp(n + 3, 1 - s)

            for n in range(-3, 2):
                step_2(n, n % 2)
            with act.Fori(2, 11, 2) as n:
                for s in range(2):
                    step_2(n + s, s)
            for n in range(12, 16):
                step_2(n, n % 2)
            act.wait_ge(in_ew, 32)
            for k in range(KT):
                a_.activation(w1_f[:, k * INTER:(k + 1) * INTER], w1_f[:, k * INTER:(k + 1) * INTER], ACT.Copy,
                              scale=sc["gxs"][:, k:k + 1]).then_inc(ew_scaled, 1)
            act.wait_ge(ew_scaled, 2)
            copy(w1_hi[:, :], w1_f[:, :], ew_hi)
            copy(w2_hi[:, :], w2_f[:, :], ew_hi)

            def gelu(c, j):
                act.wait_ge(h_psum, 4 * c + j + 1)
                if later(4 * c + j, 2):
                    act.wait_ge(g_lo, 4 * c + j - 1)
                a_.activation(hf[j % 2][:, :], bank[4 + j % 2][:, :], ACT.Gelu).then_inc(g_act, 1)

            def expert_hi(c):
                act.wait_ge(p_part, 4 * c + 4)
                copy(cols(xn_hi, c * (2 * XW), 2 * XW).rearrange("p (t n) -> p t n", n=XW)[:, :, 0:D],
                     bank[6][:, :].rearrange("p (t n) -> p t n", n=D), pr_hi)

            def chunk(c):
                gelu(c, 0)
                if has(c, 1):
                    expert_hi(c - 1)
                for j in range(1, 4):
                    gelu(c, j)

            loop(act, chunk, GROUPS, 1, GROUPS)
            expert_hi(GROUPS - 1)

            def comb_exp(t, s):
                act.wait_ge(nrow_done, 1)
                if later(t, 2):
                    act.wait_ge(e2_psum, 2 * t - 2)
                a_.activation(ef[s][:, :], cols(logits, t * SLOTS, SLOTS), ACT.Exp,
                              bias=cols(sc["nrow"], t, 1)).then_inc(e2_act, 1)

            def comb_hi(t, s):
                for i in range(2):
                    act.wait_ge(e2_psum, 2 * t + i + 1)
                    if i == 0 and later(t, 2):
                        act.wait_ge(y_psum, t - 1)
                    copy(e2T_hi[s][:, i * 512:(i + 1) * 512], bank[2 * s + i][:, :], e2_hi)

            def step_4(t, s):
                if has(t, -1, TILES):
                    comb_hi(t + 1, 1 - s)
                if has(t, -2, TILES):
                    comb_exp(t + 2, s)

            for t in range(-2, 2):
                step_4(t, t % 2)
            with act.Fori(2, 13, 2) as t:
                for s in range(2):
                    step_4(t + s, s)
            for t in range(14, 16):
                step_4(t, t % 2)

        @block.vector
        def _(dve):
            v_ = nc.vector

            def stats(ch, g):
                if ch == "A":
                    dve.wait_ge(in_x0, 16)
                    if later(g):
                        dve.wait_ge(in_x, 16)
                else:
                    held(dve, x_ready[ch], g + 1)
                for u in range(2):
                    v_.bn_stats(sc["bn" + ch][:, 6 * u:6 * u + 6], cols(xs, g * (2 * D) + u * D, D)).then_inc(bn_done[ch], 1)
                held(dve, bn_done[ch], 2 * g + 2)
                for u in range(2):
                    v_.bn_aggr(sc["mv" + ch][:, 2 * u:2 * u + 2], sc["bn" + ch][:, 6 * u:6 * u + 6]).then_inc(st_ready[ch], 1)

            def normed(ch, g):
                dve.wait_ge(rs_ready[ch], g + 1)
                if ch == "D" and later(g):
                    dve.wait_ge(xn_lod, g)
                for u in range(2):
                    v_.tensor_scalar(lnx[ch][:, u * D:(u + 1) * D], cols(xs, g * (2 * D) + u * D, D),
                                     sc["mv" + ch][:, 2 * u:2 * u + 1], sc["rs" + ch][:, u:u + 1],
                                     ALU.subtract, ALU.mult).then_inc(ln_ready[ch], 1)

            def low(dst, src, hi, done, n=1):
                v_.tensor_tensor(dst, src, f(hi), ALU.subtract).then_inc(done, n)

            def norm_T_lo(ch, g):
                dve.wait_ge(xT_hid[ch], g + 1)
                bk = {"A": 0, "B": 3, "C": 0, "D": 1}[ch]
                low(xT_lo[ch][:, :], bank[bk][:, :], xT_hi[ch][:, :], xT_lod[ch])

            def residual(ch, g, bk):
                v_.tensor_tensor(xg(g), xg(g), bank[bk][:, :], ALU.add).then_inc(x_ready[ch], 1)

            stats("A", 0)
            dve.wait_ge(in_ctx, 32)
            ctx5 = ctx_s[:, :].rearrange("p (k b c s) -> p k b c s", k=KT, b=BATCH, c=2)
            v_.tensor_tensor(hcT[:, :].rearrange("p (k b s) -> p k b s", k=KT, b=BATCH), ctx5[:, :, :, 0, :],
                             pe_s[:, :].rearrange("p (k s) -> p k s", k=KT).unsqueeze(2).to_broadcast([P, KT, BATCH, KEYS]),
                             ALU.add).then_inc(pro_dve, 1)
            normed("A", 0)
            dve.wait_ge(in_o0, 48)
            v_.tensor_scalar(bo_s[:, :], bo_s[:, :], 1.0 / H0, None, ALU.mult).then_inc(pro_dve, 1)
            dve.wait_ge(pro_pe, 2)
            v_.tensor_copy(vT0[:, :], bank[1][:, :]).then_inc(pro_dve, 1)
            for i in range(4):
                k, par = i // 2, i % 2
                dve.wait_ge(pro_act, 4 + i)
                view = lambda t: t[:, :].rearrange("p (g k h j) -> p k h g j", g=GROUPS, k=KT, h=H0)[:, k, par::2]
                last = v_.tensor_tensor(view(a_lo), bank[2 + i][:, :].rearrange("p (h g j) -> p h g j", h=4, g=GROUPS),
                                        f(view(a_hi)), ALU.subtract)
            last.then_inc(pro_dve, 1)
            dve.wait_ge(pro_pe, 4)
            for i, (bk, h) in enumerate(((6, 0), (7, 1), (0, 4), (1, 5))):
                v_.tensor_tensor(vwt[:, :].rearrange("p (h n) -> p h n", h=H0)[:, h:h + 3:2], bank[bk][:, :].rearrange("p (h n) -> p h n", h=2),
                                 bo_s[:, :].unsqueeze(1).to_broadcast([P, 2, D]), ALU.add).then_inc(pro_dve, 1 if i < 3 else 2)
            dve.wait_ge(pro_pool, 3)
            v_.tensor_tensor(slot_s[:, :].rearrange("p (m n) -> p m n", m=SM), slot_s[:, :].rearrange("p (m n) -> p m n", m=SM),
                             sc["rss"].unsqueeze(2).to_broadcast([P, SM, D]), ALU.mult).then_inc(pro_dve, 1)
            dve.wait_ge(in_l1, 96)
            dve.wait_ge(pro_act, 9)
            low(wq1_lo[:, :], wq1_f[:, :], wq1_hi[:, :], pro_dve)
            low(wo1_lo[:, :], wo1_f[:, :], wo1_hi[:, :], pro_dve)
            dve.wait_ge(pro_pe, 5)
            kb = bank[2][:, 0:256].rearrange("p (c b s) -> p c b s", c=KT, b=BATCH)
            for b in range(BATCH):
                v_.tensor_tensor(kc_f[:, b * KT * P:(b + 1) * KT * P].rearrange("p (c h s) -> p c h s", c=KT, h=2),
                                 kb[:, :, b, :].unsqueeze(2).to_broadcast([P, KT, 2, KEYS]),
                                 mk_s[:, :].rearrange("p (h s) -> p h s", h=2).unsqueeze(1).to_broadcast([P, KT, 2, KEYS]),
                                 ALU.mult).then_inc(pro_dve, 1)
            v_.tensor_tensor(vc_f[:, :].rearrange("p (m n) -> p m n", n=32), bank[3][:, :].rearrange("p (m n) -> p m n", n=32),
                             mv_s[:, :].unsqueeze(1).to_broadcast([P, BATCH * PAIRS, 32]), ALU.mult).then_inc(pro_dve, 2)
            dve.wait_ge(in_g, 32)
            v_.tensor_tensor(sc["gg"], sc["gxs"], sc["gss"], ALU.mult).then_inc(pro_dve, 1)
            dve.wait_ge(pro_act, 13)
            low(kc_lo[:, :], kc_f[:, :], kc_hi[:, :], tick)
            low(vc_lo[:, :], vc_f[:, :], vc_hi[:, :], pro_dve)
            dve.wait_ge(pro_act, 10)
            low(vw_lo[:, :], vw_f[:, :], vw_hi[:, :], pro_dve)
            dve.wait_ge(pro_act, 18)
            low(se_lo[:, :], se_f[:, :], se_hi[:, :], pro_dve)

            pv = probs[:, :].rearrange("p (a j) -> p a j", j=WK)
            bcast = lambda ap: ap.unsqueeze(2).to_broadcast([P, 2 * H0, WK])

            def round_1a(r):
                if has(r, 1):
                    dve.wait_ge(a_out, r)
                    residual("B", r - 1, 1)
                    stats("B", r - 1)
                if has(r, 0):
                    norm_T_lo("A", r)
                if has(r, 1):
                    normed("B", r - 1)
                if has(r, 0):
                    scores = bank[1][:, 0:2 * P].rearrange("p (a j) -> p a j", j=WK)
                    dve.wait_ge(sc_psum, r + 1)
                    v_.tensor_reduce(sc["mx"], scores, AXX, ALU.max).then_inc(sm_step, 1)
                    dve.wait_ge(sm_step, 3 * r + 1)
                    if later(r):
                        dve.wait_ge(pT_psum, r)
                    v_.tensor_tensor(pv, scores, bcast(sc["mx"]), ALU.subtract).then_inc(e_in, 1)
                if has(r, 1):
                    norm_T_lo("B", r - 1)
                if has(r, 0):
                    dve.wait_ge(e_out, r + 1)
                    v_.tensor_reduce(sc["sm"], pv, AXX, ALU.add).then_inc(sm_step, 1)
                    dve.wait_ge(sm_step, 3 * r + 2)
                    v_.reciprocal(sc["rc"], sc["sm"]).then_inc(sm_step, 1)
                    dve.wait_ge(sm_step, 3 * r + 3)
                    v_.tensor_tensor(pv, pv, bcast(sc["rc"]), ALU.mult).then_inc(p_ready, 1)
                if has(r, -1):
                    stats("A", r + 1)
                if has(r, 1):
                    dve.wait_ge(b_out, r)
                    residual("C", r - 1, 4)
                if has(r, 0):
                    dve.wait_ge(pT_hid, r + 1)
                    low(pT_lo[:, :], bank[2][:, 0:2 * P], pT_hi[:, :], pT_lod)
                if has(r, -1):
                    normed("A", r + 1)
                if has(r, 0):
                    dve.wait_ge(c_hid, r + 1)
                    low(c_lo[:, :], bank[5][:, :], c_hi[:, :], c_lod)

            loop(dve, round_1a, GROUPS + 1, 2, GROUPS - 1)

            v_.memset(colmax[:, :], LOWEST).then_inc(colmax_done, 1)
            dve.wait_ge(colmax_done, 1)

            def sig_low(g, j):
                dve.wait_ge(s_hid, 4 * g + j + 1)
                low(sig_lo[j % 2][:, :], sig[j % 2][:, :], sig_hi[j % 2][:, :], s_lod)

            def maxima(g, u):
                dve.wait_ge(l_sb, 4 * g + 2 * u + 2)
                tile = cols(logits, g * (2 * SLOTS) + u * SLOTS, SLOTS)
                v_.tensor_reduce(cols(sc["rowmax"], 2 * g + u, 1), tile, AXX, ALU.max).then_inc(rowmax_done, 1)
                dve.wait_ge(colmax_done, 2 * g + u + 1)
                acc = cols(colmax, (g // 4) * SLOTS, SLOTS)
                v_.tensor_tensor(acc, acc, tile, ALU.max).then_inc(colmax_done, 1)

            def round_1b(r):
                if has(r, 1):
                    dve.wait_ge(c_out, r)
                    residual("D", r - 1, 2)
                    stats("D", r - 1)
                if has(r, 0):
                    norm_T_lo("C", r)
                if has(r, 1):
                    normed("D", r - 1)
                if has(r, 0):
                    dve.wait_ge(q_hid, r + 1)
                    low(q_lo[:, :], bank[2][:, :], q_hi[:, :], q_lod)
                    sig_low(r, 0)
                    sig_low(r, 1)
                if has(r, 1):
                    norm_T_lo("D", r - 1)
                if has(r, 0):
                    sig_low(r, 2)
                if has(r, 2):
                    maxima(r - 2, 0)
                if has(r, 0):
                    sig_low(r, 3)
                if has(r, 2):
                    maxima(r - 2, 1)
                if has(r, -1):
                    stats("C", r + 1)
                if has(r, 0):
                    dve.wait_ge(o_hid, r + 1)
                    low(o_lo[:, :], bank[5][:, :], o_hi[:, :], o_lod)
                if has(r, -1):
                    normed("C", r + 1)

            stats("C", 0)
            normed("C", 0)
            loop(dve, round_1b, GROUPS + 2, 2, GROUPS - 1)

            dve.wait_ge(rowmax_done, TILES)
            v_.tensor_scalar(sc["nrow"], sc["rowmax"], -1.0, None, ALU.mult).then_inc(nrow_done, 1)
            for b in range(BATCH):
                for i in range(2):
                    dve.wait_ge(cmT, 2 * b + i + 1)
                    v_.tensor_reduce(sc["cm"][:, b * SM + 4 * i:b * SM + 4 * i + 4],
                                     bank[2 * b + i][:, :].rearrange("p (m t) -> p m t", m=4), AXX, ALU.max).then_inc(cm_red, 1)
                dve.wait_ge(cm_red, 2 * b + 2)
                v_.tensor_tensor(ef[b][:, :].rearrange("p (m s) -> p m s", m=SM),
                                 ident[:, :].unsqueeze(1).to_broadcast([P, SM, P]),
                                 sc["cm"][:, b * SM:(b + 1) * SM].unsqueeze(2).to_broadcast([P, SM, P]), ALU.mult).then_inc(cm_diag, 1)

            def e_sub(n, s):
                b, m = n // SM, n % SM
                if isinstance(n, int):
                    dve.wait_ge(cm_sb, 4)
                if later(n, 2):
                    dve.wait_ge(d_lo, n - 1)
                    dve.wait_ge(d_lo2, n - 1)
                v_.tensor_tensor(ef[s][:, :].rearrange("p (t s) -> p t s", t=SM), logits_view(b, m),
                                 cols(cmb, b * SLOTS + m * P, P).unsqueeze(1).to_broadcast([P, SM, P]), ALU.subtract).then_inc(d_sub, 1)

            def logits_view(b, m):
                v4 = logits[:, :].rearrange("p (b t n) -> p b t n", b=BATCH, t=SM)
                if isinstance(b, int):
                    return v4[:, b, :, m * P:(m + 1) * P]
                return v4[:, bass.ds(b, 1), :, bass.ds(m * P, P)].rearrange("p b t n -> p (b t) n")

            def e_low(n, s):
                dve.wait_ge(d_hi, n + 1)
                low(e_lo[s][:, 0:512], ef[s][:, 0:512], e_hi[s][:, 0:512], d_lo)

            def slot_norm(n, s):
                dve.wait_ge(sl_psum, n + 1)
                v_.reciprocal(sc["rec"][:, s:s + 1], bank[s][:, D:D + 1]).then_inc(sl_rec, 1)
                dve.wait_ge(sl_rec, n + 1)
                v_.tensor_scalar(sf[s][:, :], bank[s][:, 0:D], sc["rec"][:, s:s + 1], None, ALU.mult).then_inc(sl_norm, 1)

            def slT_low(n, s):
                dve.wait_ge(slT_hid, n + 1)
                low(cols(slT_lo, n * (2 * P), 2 * P), bank[2 + s][:, 0:2 * P], cols(slT_hi, n * (2 * P), 2 * P), slT_lod)

            def step_2(n, s):
                if has(n, 0, 16):
                    slot_norm(n, s)
                if has(n, -2, 16):
                    e_low(n + 2, s)
                if has(n, -3, 16):
                    e_sub(n + 3, 1 - s)
                if has(n, 0, 16):
                    slT_low(n, s)

            for n in range(-3, 2):
                step_2(n, n % 2)
            with dve.Fori(2, 11, 2) as n:
                for s in range(2):
                    step_2(n + s, s)
            for n in range(12, 16):
                step_2(n, n % 2)
            dve.wait_ge(ew_hi, 2)
            low(w1_lo[:, :], w1_f[:, :], w1_hi[:, :], ew_lo)
            low(w2_lo[:, :], w2_f[:, :], w2_hi[:, :], ew_lo)

            def gelu_split(c, j):
                dve.wait_ge(g_act, 4 * c + j + 1)
                if later(4 * c + j, 4):
                    dve.wait_ge(p_part, 4 * c + j - 3)
                v_.tensor_copy(h_hi[j][:, :], hf[j % 2][:, :]).then_inc(g_hi, 1)
                dve.wait_ge(g_hi, 4 * c + j + 1)
                low(h_lo[j][:, :], hf[j % 2][:, :], h_hi[j][:, :], g_lo)

            def expert_lo(c):
                dve.wait_ge(pr_hi, c + 1)
                view = lambda t: cols(t, c * (2 * XW), 2 * XW).rearrange("p (t n) -> p t n", n=XW)[:, :, 0:D]
                v_.tensor_tensor(view(xn_lo), bank[6][:, :].rearrange("p (t n) -> p t n", n=D), f(view(xn_hi)), ALU.subtract).then_inc(pr_lo, 1)

            def chunk(c):
                gelu_split(c, 0)
                if has(c, 1):
                    expert_lo(c - 1)
                for j in range(1, 4):
                    gelu_split(c, j)

            loop(dve, chunk, GROUPS, 1, GROUPS)
            expert_lo(GROUPS - 1)

            def comb_lo(t, s):
                for i in range(2):
                    dve.wait_ge(e2_hi, 2 * t + i + 1)
                    low(e2T_lo[s][:, i * 512:(i + 1) * 512], bank[2 * s + i][:, :], e2T_hi[s][:, i * 512:(i + 1) * 512], e2_lo)

            def finish(t, s):
                dve.wait_ge(y_psum, t + 1)
                v_.reciprocal(sc["rec4"][:, s:s + 1], bank[4 + s][:, D:D + 1]).then_inc(y_rec, 1)
                dve.wait_ge(y_rec, t + 1)
                if later(t, 2):
                    dve.wait_ge(out_done[s], (t // 2) * 16)
                v_.scalar_tensor_tensor(out=y[s][:, :], in0=bank[4 + s][:, 0:D], scalar=sc["rec4"][:, s:s + 1],
                                        in1=cols(xs, t * D, D), op0=ALU.mult, op1=ALU.add).then_inc(y_ready, 1)

            def step_4(t, s):
                if has(t, -1, TILES):
                    comb_lo(t + 1, 1 - s)
                if has(t, 0, TILES):
                    finish(t, s)

            for t in range(-1, 2):
                step_4(t, t % 2)
            with dve.Fori(2, 13, 2) as t:
                for s in range(2):
                    step_4(t + s, s)
            for t in range(14, 16):
                step_4(t, t % 2)

        @block.tensor
        def _(pe_):
            mm = nc.tensor.matmul

            pe_.wait_ge(pro_dve, 1)
            pe_.wait_ge(in_kv0, 32)
            for bk, w in ((0, wk0s), (1, wv0s)):
                for ct in range(4):
                    for k in range(KT):
                        last = mm(bank[bk][:, ct * P:(ct + 1) * P], w[:, k * 512 + ct * P:k * 512 + (ct + 1) * P],
                                  hcT[:, k * P:(k + 1) * P], start=k == 0, stop=k == KT - 1)
                last.then_inc(pro_pe, 1)
            pe_.wait_ge(in_o0, 48)
            pe_.wait_ge(pro_act, 3)
            for k in range(KT):
                for h in range(H0):
                    par, i = h % 2, h // 2
                    rows = slice(DH0 * par, DH0 * (par + 1))
                    last = mm(bank[2 + 2 * k + par][:, i * P:(i + 1) * P], wq0s[rows, i * D + k * P:i * D + (k + 1) * P],
                              kT0[rows, i * P:(i + 1) * P], start=True, stop=True)
            last.then_inc(pro_pe, 1)
            pe_.wait_ge(pro_dve, 3)
            for h in range(H0):
                par, i = h % 2, h // 2
                rows = slice(DH0 * par, DH0 * (par + 1))
                bk = (6 if i < 2 else 0) + par
                last = mm(bank[bk][:, (i % 2) * D:(i % 2 + 1) * D], vT0[rows, i * P:(i + 1) * P],
                          wo0s[rows, i * D:(i + 1) * D], start=True, stop=True)
            last.then_inc(pro_pe, 1)
            pe_.wait_ge(in_l1, 96)
            pe_.wait_ge(pro_dve, 9)
            ctx5 = ctx_s[:, :].rearrange("p (k b c s) -> p k b c s", k=KT, b=BATCH, c=2)
            for ct in range(KT):
                for k in range(KT):
                    mm(bank[2][:, ct * P:(ct + 1) * P], wk1s[:, k * D + ct * P:k * D + (ct + 1) * P], ctx5[:, k, :, 0, :],
                       start=k == 0, stop=k == KT - 1)
            for b in range(BATCH):
                for k in range(KT):
                    last = mm(bank[3][:, b * D:(b + 1) * D], ctx_s[:, (k * BATCH + b) * P:(k * BATCH + b + 1) * P],
                              wv1s[:, k * D:(k + 1) * D], start=k == 0, stop=k == KT - 1)
            last.then_inc(pro_pe, 1)
            pe_.wait_ge(in_id, 16)
            pe_.wait_ge(pro_dve, 10)
            for k in range(KT):
                for m in range(SM):
                    last = nc.tensor.transpose(bank[4 + 2 * k + m // 4][:, (m % 4) * P:(m % 4 + 1) * P],
                                               slot_s[:, m * D + k * P:m * D + (k + 1) * P], ident[:, :])
            last.then_inc(pro_pe, 1)

            def norm_T(ch, g):
                pe_.wait_ge(ln_ready[ch], 2 * g + 2)
                bk = {"A": 0, "B": 3, "C": 0, "D": 1}[ch]
                for k in range(KT):
                    for u in range(2):
                        last = nc.tensor.transpose(bank[bk][:, k * GT + u * P:k * GT + (u + 1) * P],
                                                   lnx[ch][:, u * D + k * P:u * D + (k + 1) * P], ident[:, :])
                last.then_inc(xT_psum[ch], 1)

            def xT(ch, k, u=None):
                lo, n = (k * GT, GT) if u is None else (k * GT + u * P, P)
                return xT_hi[ch][:, lo:lo + n], xT_lo[ch][:, lo:lo + n]

            def pair(hi, lo, start, n):
                return cols(hi, start, n), cols(lo, start, n)

            def fuse(g, k):
                pe_.wait_ge(in_w[k], 32 * (g + 1))
                if k == 0 and later(g):
                    pe_.wait_ge(c_lod, g)
                for c in (2 * k, 2 * k + 1):
                    for m in range(KT):
                        last = mm(bank[5][:, m * D:(m + 1) * D], w1r[:, c * D + m * P:c * D + (m + 1) * P],
                                  w2r[:, c * D:(c + 1) * D], start=c == 0 and m == 0, stop=c == OC - 1 and m == KT - 1,
                                  skip_group_check=True)
                last.then_inc(w_used, 1)

            def scores(g):
                pe_.wait_ge(xT_lod["A"], g + 1)
                for u in range(2):
                    for k in range(KT):
                        last = split3(bank[1][:, u * P:(u + 1) * P], xT("A", k, u),
                                      pair(a_hi, a_lo, g * (KT * P) + k * P, P), k == 0, k == KT - 1)
                last.then_inc(sc_psum, 1)

            def probs_T(g):
                pe_.wait_ge(p_ready, g + 1)
                for u in range(2):
                    last = nc.tensor.transpose(bank[2][:, u * P:(u + 1) * P], probs[:, u * P:(u + 1) * P], ident[:, :])
                last.then_inc(pT_psum, 1)

            def attend(g):
                pe_.wait_ge(pT_lod, g + 1)
                for u in range(2):
                    last = split3(bank[1][:, u * D:(u + 1) * D],
                                  (pT_hi[:, u * P:(u + 1) * P], pT_lo[:, u * P:(u + 1) * P]),
                                  pair(vw_hi, vw_lo, g * D, D), True, True)
                last.then_inc(a_out, 1)

            def ffn(g):
                pe_.wait_ge(xT_lod["B"], g + 1)
                pe_.wait_ge(c_lod, g + 1)
                pe_.wait_ge(z_lod, g + 1)
                for u in range(2):
                    o = bank[4][:, u * D:(u + 1) * D]
                    for k in range(KT):
                        split3(o, xT("B", k, u), (c_hi[:, k * D:(k + 1) * D], c_lo[:, k * D:(k + 1) * D]), k == 0, False)
                    mm(o, ones_r[:, :], z_lo[:, :], start=False, stop=False, skip_group_check=True)
                    last = mm(o, ones_r[:, :], z_hi[:, :], start=False, stop=True, skip_group_check=True)
                last.then_inc(b_out, 1)

            def round_1a(r):
                if has(r, 0):
                    norm_T("A", r)
                    fuse(r, 0)
                    fuse(r, 1)
                if has(r, 1):
                    norm_T("B", r - 1)
                if has(r, 0):
                    scores(r)
                    fuse(r, 2)
                if has(r, 1):
                    ffn(r - 1)
                if has(r, 0):
                    probs_T(r)
                    fuse(r, 3)
                    attend(r)

            pe_.wait_ge(pro_dve, 19)
            pe_.wait_ge(pro_act, 17)
            loop(pe_, round_1a, GROUPS + 1, 2, GROUPS - 1)

            def query(g):
                pe_.wait_ge(xT_lod["C"], g + 1)
                for ct in range(KT):
                    for k in range(KT):
                        o = k * D + ct * P
                        last = split3(bank[2][:, ct * GT:(ct + 1) * GT], (wq1_hi[:, o:o + P], wq1_lo[:, o:o + P]),
                                      xT("C", k), k == 0, k == KT - 1)
                last.then_inc(q_psum, 1)

            def sig_scores(g, j):
                if j == 0:
                    pe_.wait_ge(kv_in, (g // 4 + 1) * 256)
                    pe_.wait_ge(q_lod, g + 1)
                if later(4 * g + j, 2):
                    pe_.wait_ge(s_sig, 4 * g + j - 1)
                ct = j // 2
                for i in range(2):
                    m = 2 * j + i
                    last = split3(bank[3 + j % 2][:, i * GT:(i + 1) * GT], (kw_hi[:, m * P:(m + 1) * P], kw_lo[:, m * P:(m + 1) * P]),
                                  (q_hi[:, ct * GT:(ct + 1) * GT], q_lo[:, ct * GT:(ct + 1) * GT]), True, True)
                last.then_inc(s_psum, 1)

            def sig_values(g, j):
                pe_.wait_ge(s_lod, 4 * g + j + 1)
                if j == 0 and later(g):
                    pe_.wait_ge(o_lod, g)
                ct = j // 2
                for i in range(2):
                    m = 2 * j + i
                    last = split3(bank[5][:, ct * GT:(ct + 1) * GT], (vw1_hi[:, m * P:(m + 1) * P], vw1_lo[:, m * P:(m + 1) * P]),
                                  (sig_hi[j % 2][:, i * GT:(i + 1) * GT], sig_lo[j % 2][:, i * GT:(i + 1) * GT]),
                                  j % 2 == 0 and i == 0, j % 2 == 1 and i == 1)
                last.then_inc(o_part, 1)

            def project(g):
                pe_.wait_ge(o_lod, g + 1)
                for u in range(2):
                    for ct in range(KT):
                        o = ct * GT + u * P
                        last = split3(bank[2][:, u * D:(u + 1) * D], (o_hi[:, o:o + P], o_lo[:, o:o + P]),
                                      (wo1_hi[:, ct * D:(ct + 1) * D], wo1_lo[:, ct * D:(ct + 1) * D]), ct == 0, ct == KT - 1)
                last.then_inc(c_out, 1)

            def logit(g, i):
                u, half = i // 2, i % 2
                if i == 0:
                    pe_.wait_ge(xT_lod["D"], g + 1)
                if later(4 * g + i, 2):
                    pe_.wait_ge(l_sb, 4 * g + i - 1)
                for k in range(KT):
                    o = k * SLOTS + half * 512
                    last = split3(bank[6 + half][:, :], xT("D", k, u), (se_hi[:, o:o + 512], se_lo[:, o:o + 512]),
                                  k == 0, k == KT - 1)
                last.then_inc(l_psum, 1)

            def round_1b(r):
                if has(r, 0):
                    norm_T("C", r)
                if has(r, 2):
                    logit(r - 2, 2)
                if has(r, 0):
                    query(r)
                if has(r, 2):
                    logit(r - 2, 3)
                if has(r, 0):
                    sig_scores(r, 0)
                    sig_scores(r, 1)
                if has(r, 1):
                    norm_T("D", r - 1)
                if has(r, 0):
                    sig_scores(r, 2)
                    sig_values(r, 0)
                    sig_scores(r, 3)
                    sig_values(r, 1)
                if has(r, 1):
                    logit(r - 1, 0)
                if has(r, 0):
                    sig_values(r, 2)
                    sig_values(r, 3)
                if has(r, 1):
                    logit(r - 1, 1)
                if has(r, 0):
                    project(r)

            pe_.wait_ge(pro_dve, 20)
            loop(pe_, round_1b, GROUPS + 2, 2, GROUPS - 1)

            pe_.wait_ge(colmax_done, TILES + 1)
            for b in range(BATCH):
                for m in range(SM):
                    last = nc.tensor.transpose(bank[2 * b + m // 4][:, (m % 4) * P:(m % 4 + 1) * P],
                                               colmax[:, b * SLOTS + m * P:b * SLOTS + (m + 1) * P], ident[:, :])
                    if m % 4 == 3:
                        last.then_inc(cmT, 1)
            pe_.wait_ge(l_sb, 4 * GROUPS)
            for b in range(BATCH):
                pe_.wait_ge(cm_diag, b + 1)
                for i in range(2):
                    mm(bank[4 + 2 * b + i][:, :], ones[:, :], ef[b][:, i * 512:(i + 1) * 512], start=True, stop=True).then_inc(cm_bc, 1)

            def dispatch(n, s):
                b = n // SM
                pe_.wait_ge(d_lo, n + 1)
                pe_.wait_ge(d_lo2, n + 1)
                if later(n, 2):
                    pe_.wait_ge(sl_norm, n - 1)
                for t in range(SM):
                    last = split3(bank[s][:, 0:XW], (e_hi[s][:, t * P:(t + 1) * P], e_lo[s][:, t * P:(t + 1) * P]),
                                  pair(xn_hi, xn_lo, b * (SM * XW) + t * XW, XW), t == 0, t == SM - 1)
                last.then_inc(sl_psum, 1)

            def slots_T(n, s):
                pe_.wait_ge(sl_norm, n + 1)
                if later(n, 2):
                    pe_.wait_ge(slT_lod, n - 1)
                for k in range(KT):
                    last = nc.tensor.transpose(bank[2 + s][:, k * P:(k + 1) * P], sf[s][:, k * P:(k + 1) * P], ident[:, :])
                last.then_inc(slT_psum, 1)

            def step_2(n, s):
                dispatch(n, s)
                if has(n, 1, 16):
                    slots_T(n - 1, 1 - s)

            pe_.wait_ge(xn_lod, GROUPS)
            for n in range(2):
                step_2(n, n)
            with pe_.Fori(2, 15, 2) as n:
                for s in range(2):
                    step_2(n + s, s)
            slots_T(15, 1)

            def hidden(c, j):
                if later(4 * c + j, 2):
                    pe_.wait_ge(g_act, 4 * c + j - 1)
                for i in range(2):
                    for k in range(KT):
                        o = k * INTER + (2 * j + i) * P
                        rhs = [cols(t, c * (4 * P), 4 * P).rearrange("p (m k s) -> p k m s", m=2, k=KT)[:, k] for t in (slT_hi, slT_lo)]
                        last = split3(bank[4 + j % 2][:, i * GT:(i + 1) * GT], (w1_hi[:, o:o + P], w1_lo[:, o:o + P]), rhs,
                                      k == 0, k == KT - 1)
                last.then_inc(h_psum, 1)

            def expert(c, j):
                pe_.wait_ge(g_lo, 4 * c + j + 1)
                if j == 0 and later(c):
                    pe_.wait_ge(pr_lo, c)
                for u in range(2):
                    for i in range(2):
                        o = (2 * j + i) * D
                        last = split3(bank[6][:, u * D:(u + 1) * D],
                                      (h_hi[j][:, i * GT + u * P:i * GT + (u + 1) * P], h_lo[j][:, i * GT + u * P:i * GT + (u + 1) * P]),
                                      (w2_hi[:, o:o + D], w2_lo[:, o:o + D]), j == 0 and u == 0 and i == 0, j == 3 and u == 1 and i == 1)
                last.then_inc(p_part, 1)

            def chunk(c):
                hidden(c, 0)
                if has(c, 1):
                    expert(c - 1, 3)
                for j in range(1, 4):
                    hidden(c, j)
                    expert(c, j - 1)

            pe_.wait_ge(ew_lo, 2)
            pe_.wait_ge(slT_lod, 16)
            loop(pe_, chunk, GROUPS, 1, GROUPS)
            expert(GROUPS - 1, 3)

            def comb_T(t, s):
                pe_.wait_ge(e2_act, t + 1)
                if later(t, 2):
                    pe_.wait_ge(e2_lo, 2 * t - 2)
                for m in range(SM):
                    last = nc.tensor.transpose(bank[2 * s + m // 4][:, (m % 4) * P:(m % 4 + 1) * P],
                                               ef[s][:, m * P:(m + 1) * P], ident[:, :])
                    if m % 4 == 3:
                        last.then_inc(e2_psum, 1)

            def combine(t, s):
                b = t // SM
                pe_.wait_ge(e2_lo, 2 * t + 2)
                if later(t, 2):
                    pe_.wait_ge(y_ready, t - 1)
                for m in range(SM):
                    last = split3(bank[4 + s][:, 0:XW], (e2T_hi[s][:, m * P:(m + 1) * P], e2T_lo[s][:, m * P:(m + 1) * P]),
                                  pair(xn_hi, xn_lo, b * (SM * XW) + m * XW, XW), m == 0, m == SM - 1)
                last.then_inc(y_psum, 1)

            def step_4(t, s):
                if has(t, -1, TILES):
                    comb_T(t + 1, 1 - s)
                if has(t, 0, TILES):
                    combine(t, s)

            step_4(-1, 1)
            pe_.wait_ge(pr_lo, GROUPS)
            for t in range(2):
                step_4(t, t % 2)
            with pe_.Fori(2, 13, 2) as t:
                for s in range(2):
                    step_4(t + s, s)
            for t in range(14, 16):
                step_4(t, t % 2)


def position_table():
    pos = np.arange(75, dtype=np.float32)[:, None]
    denom = np.power(np.float32(10000.0), np.float32(2.0) * np.arange(D // 2, dtype=np.float32) / np.float32(D)).astype(np.float32)
    ang = (pos / denom).astype(np.float32)
    pe = np.zeros((75, D), np.float32)
    pe[:, 0::2] = np.sin(ang)
    pe[:, 1::2] = np.cos(ang)
    return pe[:KEYS].T


def kernel(**inputs):
    import concourse.bacc as bacc
    from concourse.bass_utils import run_bass_kernel_spmd

    a = {k: np.asarray(v) for k, v in inputs.items()}
    c = np.ascontiguousarray

    def ktiles(m):
        return c(m.reshape(-1, P, m.shape[1]).transpose(1, 0, 2).reshape(P, -1))

    ctxT = a["ctx_1024"].transpose(2, 0, 1)
    ctx2 = np.broadcast_to(ctxT.reshape(KT, P, BATCH, 1, KEYS).transpose(1, 0, 2, 3, 4), (P, KT, BATCH, 2, KEYS))
    p = np.arange(P)
    mask_k = np.repeat((p[:, None] % 32 // DH1 == np.arange(2)[None, :]), KEYS, axis=1).astype(np.float32)
    mask_v = (np.arange(32)[None, :] // DH1 == p[:, None] // KEYS).astype(np.float32)
    arrays = {
        "x": c(a["x"].reshape(TOKENS, D)),
        "ctx2": c(ctx2.reshape(P, -1)),
        "pe": ktiles(position_table()),
        "wq0T": c(a["L0_xattn_Wq"].T), "wk0": a["L0_xattn_Wk"], "wv0": a["L0_xattn_Wv"], "wo0": a["L0_xattn_Wo"],
        "bo": a["L0_xattn_bo"].reshape(1, D),
        "fw1": c(a["L0_ffn_W1"].reshape(GROUPS, P, OC * D)),
        "fb1": c(a["L0_ffn_b1"].reshape(GROUPS, P, OC)),
        "fw2T": c(a["L0_ffn_W2"].transpose(0, 2, 1).reshape(GROUPS, P, OC * D)),
        "fb2": a["L0_ffn_b2"],
        "wq1T": c(a["L1_xattn_Wq"].T), "wk1T": c(a["L1_xattn_Wk"].T), "wv1T": c(a["L1_xattn_Wv"].T), "wo1T": c(a["L1_xattn_Wo"].T),
        "gx": c(a["L1_ffn_gamma_x"].reshape(KT, P).T), "gs": c(a["L1_ffn_gamma_slot"].reshape(KT, P).T),
        "slot": a["L1_ffn_slot_embeds"].reshape(SLOTS, D), "w1": a["L1_ffn_w1"], "w2": a["L1_ffn_w2"],
        "ident_in": np.eye(P, dtype=np.float32), "mask_k": mask_k, "mask_v": mask_v,
    }
    nc = bacc.Bacc("TRN2", target_bir_lowering=False, num_devices=1, dynamic_dma_scratch_size=1024)
    args = {n: nc.dram_tensor(f"in_{n}", v.shape, F32, kind="ExternalInput").ap() for n, v in arrays.items()}
    outp = nc.dram_tensor("out_0", (TOKENS, D), F32, kind="ExternalOutput").ap()
    build(nc, out=outp, **args)
    r = run_bass_kernel_spmd(nc, [{f"in_{n}": c(v) for n, v in arrays.items()}], core_ids=[0])
    return np.asarray(r.results[0]["out_0"]).reshape(BATCH, SEQ, D)
```

```python
import numpy as np
import concourse.bass as bass
from concourse import mybir
from contextlib import ExitStack

F32 = mybir.dt.float32
F32R = mybir.dt.float32r
ALU = mybir.AluOpType
ACT = mybir.ActivationFunctionType
AXX = mybir.AxisListType.X

P = 128
BATCH, SEQ, D = 2, 1024, 256
TOKENS = BATCH * SEQ
TILES = TOKENS // P
GROUPS = 8
GT = TOKENS // GROUPS
KT = D // P
KEYS = 64
H0, DH0 = 8, 64
WK = KEYS // 4
H1, DH1 = 16, 16
PAIRS = H1 // 2
INTER = 1024
OC = INTER // P
SLOTS = 1024
SM = SLOTS // P
XW = D + 2
LN_EPS, NORM_EPS = 1e-5, 1e-12
WPARTS = 4
LOWEST = -3.0e38


def build(nc, x, ctx2, pe, wq0T, wk0, wv0, wo0, bo, fw1, fb1, fw2T, fb2, wq1T, wk1T, wv1T, wo1T,
          gx, gs, slot, w1, w2, ident_in, mask_k, mask_v, out):
    es = ExitStack()
    with es:
        base = 1152
        KB = 1024

        def place(name, cols, kb, dt=F32):
            return nc.alloc_sbuf_tensor_at(name, [P, cols], dt, offset=base + int(kb * KB))

        def sem(name):
            return es.enter_context(nc.semaphore(name))

        xs = place("xs", TILES * D, 0)
        ident = place("ident", P, 16)
        ones = place("ones", P, 16.5)
        ones_r = place("ones_r", P, 17, F32R)
        small = place("small", 256, 17.5)
        se_hi = place("se_hi", KT * SLOTS, 19, F32R)
        se_lo = place("se_lo", KT * SLOTS, 27, F32R)
        se_f = place("se_f", KT * SLOTS, 27)
        wq1_hi = place("wq1_hi", KT * D, 35, F32R)
        wq1_lo = place("wq1_lo", KT * D, 37, F32R)
        wq1_f = place("wq1_f", KT * D, 37)
        wo1_hi = place("wo1_hi", KT * D, 39, F32R)
        wo1_lo = place("wo1_lo", KT * D, 41, F32R)
        wo1_f = place("wo1_f", KT * D, 41)
        kc_hi = place("kc_hi", BATCH * KT * P, 43, F32R)
        kc_lo = place("kc_lo", BATCH * KT * P, 45, F32R)
        kc_f = place("kc_f", BATCH * KT * P, 45)
        vc_hi = place("vc_hi", BATCH * PAIRS * 32, 47, F32R)
        vc_lo = place("vc_lo", BATCH * PAIRS * 32, 49, F32R)
        vc_f = place("vc_f", BATCH * PAIRS * 32, 49)
        a_hi = place("a_hi", GROUPS * KT * P, 51, F32R)
        a_lo = place("a_lo", GROUPS * KT * P, 59, F32R)
        vw_hi = place("vw_hi", GROUPS * D, 67, F32R)
        vw_lo = place("vw_lo", GROUPS * D, 75, F32R)
        vw_f = place("vw_f", GROUPS * D, 75)
        w1r = place("w1r", OC * D, 83)
        w2r = place("w2r", OC * D, 91)
        c_hi = place("c_hi", KT * D, 99, F32R)
        c_lo = place("c_lo", KT * D, 101, F32R)
        z0 = place("z0", D, 103)
        z = place("z", D, 104)
        z_hi = place("z_hi", D, 105, F32R)
        z_lo = place("z_lo", D, 106, F32R)
        b1t = place("b1t", OC, 107)
        prod = place("prod", OC * D, 139.5)
        probs = place("probs", 2 * P, 108)
        pT_hi = place("pT_hi", 2 * P, 109, F32R)
        pT_lo = place("pT_lo", 2 * P, 110, F32R)
        vwt = place("vwt", H0 * D, 123)
        wk0s = place("wk0s", KT * 512, 176)
        wv0s = place("wv0s", KT * 512, 180)
        wq0s = place("wq0s", 4 * D, 184)
        wo0s = place("wo0s", 4 * D, 188)
        kT0 = place("kT0", 512, 192)
        vT0 = place("vT0", 512, 194)
        ctx_s = place("ctx_s", KT * BATCH * P, 196)
        hcT = place("hcT", KT * P, 198)
        pe_s = place("pe_s", KT * KEYS, 199)
        mk_s = place("mk_s", P, 199.5)
        mv_s = place("mv_s", 32, 200)
        bo_s = place("bo_s", D, 201)
        wk1s = place("wk1s", KT * D, 202)
        wv1s = place("wv1s", KT * D, 204)
        slot_s = place("slot_s", SM * D, 131)
        sq = place("sq", SM * D, 206.5)
        xn_hi = place("xn_hi", TILES * XW, 51, F32R)
        xn_lo = place("xn_lo", TILES * XW, 67.125, F32R)
        logits = place("logits", TILES * SLOTS, 84)
        kw_hi = place("kw_hi", PAIRS * P, 148, F32R)
        kw_lo = place("kw_lo", PAIRS * P, 152, F32R)
        vw1_hi = place("vw1_hi", PAIRS * P, 156, F32R)
        vw1_lo = place("vw1_lo", PAIRS * P, 160, F32R)
        q_hi = place("q_hi", KT * GT, 176, F32R)
        q_lo = place("q_lo", KT * GT, 178, F32R)
        o_hi = place("o_hi", KT * GT, 180, F32R)
        o_lo = place("o_lo", KT * GT, 170, F32R)
        sig = [place(f"sig{i}", 2 * GT, 172 + 2 * i) for i in range(2)]
        sig_hi = [place(f"sig_hi{i}", 2 * GT, (188, 190, 204, 206)[i], F32R) for i in range(4)]
        sig_lo = [place(f"sig_lo{i}", 2 * GT, (192, 194, 208, 210)[i], F32R) for i in range(4)]
        colmax = place("colmax", BATCH * SLOTS, 196)
        lnx, xT_hi, xT_lo = {}, {}, {}
        for ch, kb in zip("ABCD", (111, 117, 164, 182)):
            lnx[ch] = place(f"ln{ch}", 2 * D, kb)
            xT_hi[ch] = place(f"xT_hi{ch}", KT * GT, kb + 2, F32R)
            xT_lo[ch] = place(f"xT_lo{ch}", KT * GT, kb + 4, F32R)
        w1_hi = place("w1_hi", KT * INTER, 19, F32R)
        w1_lo = place("w1_lo", KT * INTER, 27, F32R)
        w1_f = place("w1_f", KT * INTER, 27)
        w2_hi = place("w2_hi", OC * D, 35, F32R)
        w2_lo = place("w2_lo", OC * D, 43, F32R)
        w2_f = place("w2_f", OC * D, 43)
        cmb = place("cmb", BATCH * SLOTS, 148)
        diag = [place(f"diag{b}", SLOTS, (218, 184)[b]) for b in range(BATCH)]
        e_hi = [place(f"e_hi{i}", SLOTS, 156 + 4 * i, F32R) for i in range(4)]
        e_lo = [place(f"e_lo{i}", SLOTS, 206 + 4 * i, F32R) for i in range(4)]
        ef = [place(f"ef{i}", SLOTS, 206 + 4 * i) for i in range(4)]
        slT_hi = place("slT_hi", KT * BATCH * SLOTS, 172, F32R)
        slT_lo = place("slT_lo", KT * BATCH * SLOTS, 188, F32R)
        sf = [place(f"sf{i}", D, 204 + i) for i in range(2)]
        hf = [place(f"hf{i}", 2 * GT, 148 + 2 * i) for i in range(2)]
        h_hi = [place(f"h_hi{i}", 2 * GT, 152 + 4 * i, F32R) for i in range(4)]
        h_lo = [place(f"h_lo{i}", 2 * GT, 154 + 4 * i, F32R) for i in range(4)]
        e2T_hi = [place(f"e2T_hi{i}", SLOTS, 156 + 8 * i, F32R) for i in range(2)]
        e2T_lo = [place(f"e2T_lo{i}", SLOTS, 160 + 8 * i, F32R) for i in range(2)]
        y = [place(f"y{i}", D, 172 + i) for i in range(2)]

        cmT_bank = ((3, 4), (4, 5))
        spread_bank = ((0, 5), (6, 7))

        sc = {}
        at = 0
        for name, n in [("bnA", 12), ("bnB", 12), ("bnC", 12), ("bnD", 12), ("mvA", 4), ("mvB", 4),
                        ("mvC", 4), ("mvD", 4), ("veA", 2), ("veB", 2), ("veC", 2), ("veD", 2),
                        ("rsA", 2), ("rsB", 2), ("rsC", 2), ("rsD", 2), ("t1", 2), ("t2", 2), ("t3", 2),
                        ("rstd", 2), ("eps", 2), ("mhalf", 8), ("mx", 16), ("sm", 16), ("rc", 16),
                        ("rowmax", 16), ("nrow", 16), ("cm", 16), ("ss", 8), ("rss", 8), ("gxs", 2),
                        ("gss", 2), ("gg", 2), ("rec", 2), ("rec4", 2)]:
            sc[name] = small[:, at:at + n]
            at += n
        assert at <= 256

        bank = [es.enter_context(nc.psum_tensor(f"bank{i}", [P, 512], F32)) for i in range(8)]
        vw_dram = nc.dram_tensor("vw_bounce", [P, H0 * D], F32).ap()

        in_x0, in_x, in_ctx, in_kv0, in_o0, in_l1, in_slot, in_g, in_id = (
            sem(n) for n in ("in_x0", "in_x", "in_ctx", "in_kv0", "in_o0", "in_l1", "in_slot", "in_g", "in_id"))
        in_w = [sem(f"in_w{k}") for k in range(WPARTS)]
        in_b, vw_out, vw_in, k1_in = (sem(n) for n in ("in_b", "vw_out", "vw_in", "k1_in"))
        v1_in = sem("v1_in")
        in_ew = [sem("in_ew1"), sem("in_ew2")]
        out_done = [sem(f"out_done{i}") for i in range(2)]
        consts, pro_dve, pro_act, pro_pe, pro_pool = (sem(n) for n in ("consts", "pro_dve", "pro_act", "pro_pe", "pro_pool"))
        tick = sem("tick")
        bn_done, st_ready, rs_step, rs_ready, ln_ready, xT_psum, xT_hid, xT_lod = ({} for _ in range(8))
        for ch in "ABCD":
            bn_done[ch] = sem(f"bn_done{ch}")
            st_ready[ch] = sem(f"st_ready{ch}")
            rs_step[ch] = sem(f"rs_step{ch}")
            rs_ready[ch] = sem(f"rs_ready{ch}")
            ln_ready[ch] = sem(f"ln_ready{ch}")
            xT_psum[ch] = sem(f"xT_psum{ch}")
            xT_hid[ch] = sem(f"xT_hi_done{ch}")
            xT_lod[ch] = sem(f"xT_lo_done{ch}")
        x_ready = {"B": sem("x1_ready"), "C": sem("x2_ready"), "D": sem("x3_ready")}
        (sc_psum, sm_step, e_in, e_out, p_ready, pT_psum, pT_hid, pT_lod, a_out, w_used, c_hid, c_lod, z_prod, z_step,
         z_hid, z_lod, b_out) = (sem(n) for n in (
             "sc_psum", "sm_step", "e_in", "e_out", "p_ready", "pT_psum", "pT_hi_done", "pT_lo_done", "a_out",
             "w_used", "c_hi_done", "c_lo_done", "z_prod", "z_step", "z_hi_done", "z_lo_done", "b_out"))
        (q_psum, q_hid, q_lod, s_psum, s_sig, s_hid, o_part, o_hid, o_lod, c_out, l_psum, l_sb, rowmax_done,
         colmax_done, xn_hid, xn_lod) = (sem(n) for n in (
             "q_psum", "q_hi_done", "q_lo_done", "s_psum", "s_sig", "s_hi_done", "o_part", "o_hi_done",
             "o_lo_done", "c_out", "l_psum", "l_sb", "rowmax_done", "colmax_done", "xn_hi_done", "xn_lo_done"))
        w1_hid = sem("w1_hi_done")
        s_lod = [sem("s_lo_even"), sem("s_lo_odd")]
        cmT, cm_red, cm_diag, cm_bc, cm_sb = (sem(n) for n in ("cmT", "cm_red", "cm_diag", "cm_bc", "cm_sb"))
        (d_sub, d_exp, d_hi, d_lo, sl_psum, sl_rec, sl_norm, slT_psum, slT_hid, slT_lod) = (sem(n) for n in (
            "d_sub", "d_exp", "d_hi", "d_lo", "sl_psum", "sl_rec", "sl_norm", "slT_psum", "slT_hi_done", "slT_lo_done"))
        (ew_hi, ew_lo, h_psum, g_act, g_hi, g_lo, p_part, pr_hi, pr_lo) = (sem(n) for n in (
            "ew_hi", "ew_lo", "h_psum", "g_act", "g_hi", "g_lo", "p_part", "pr_hi", "pr_lo"))
        (nrow_done, e2_act, e2_psum, e2_hi, e2_lo, y_psum, y_rec, y_ready) = (sem(n) for n in (
            "nrow_done", "e2_act", "e2_psum", "e2_hi", "e2_lo", "y_psum", "y_rec", "y_ready"))

        def cols(t, start, n):
            return t[:, start:start + n] if isinstance(start, int) else t[:, bass.ds(start, n)]

        def xg(g):
            return cols(xs, g * (2 * D), 2 * D)

        def f(ap):
            return ap.bitcast(F32)

        def split3(outp, lhs, rhs, start, stop):
            nc.tensor.matmul(outp, lhs[0], rhs[1], start=start, stop=False, skip_group_check=True)
            nc.tensor.matmul(outp, lhs[1], rhs[0], start=False, stop=False, skip_group_check=True)
            return nc.tensor.matmul(outp, lhs[0], rhs[0], start=False, stop=stop, skip_group_check=True)

        def later(v, least=1):
            return not isinstance(v, int) or v >= least

        def loop(eng, body, first, lo, hi, end):
            for r in range(first, lo):
                body(r)
            with eng.Fori(lo, hi) as r:
                body(r)
            for r in range(hi, end):
                body(r)

        def has(r, shift, n=GROUPS):
            return not isinstance(r, int) or 0 <= r - shift < n

        def is_tail(r, n=GROUPS):
            return isinstance(r, int) and r == n

        def dispatch_steps(eng, body, first, end):
            for n in range(first, 4):
                body(n, n % 4)
            with eng.Fori(4, 11, 4) as n:
                for s in range(4):
                    body(n + s, s)
            for n in range(12, end):
                body(n, n % 4)

        def logits_view(b, m):
            v4 = logits[:, :].rearrange("p (b t n) -> p b t n", b=BATCH, t=SM)
            if isinstance(b, int):
                return v4[:, b, :, m * P:(m + 1) * P]
            return v4[:, bass.ds(b, 1), :, bass.ds(m * P, P)].rearrange("p b t n -> p (b t) n")

        def held(eng, s, v):
            eng.wait_ge(s, v)
            if not isinstance(v, int):
                eng.sem_inc(tick, 1)

        block = es.enter_context(nc.Block())

        @block.sync
        def _(sp):
            def load_w(g, k):
                part = slice(2 * k * D, 2 * (k + 1) * D)
                if later(g):
                    held(sp, w_used, 4 * g - 3 + k)
                    held(sp, z_prod, OC * (g - 1) + 2 * k + 2)
                for dst, src in ((w1r, fw1), (w2r, fw2T)):
                    s = src[g, :, part] if isinstance(g, int) else src[bass.ds(g, 1), :, part].rearrange("a p n -> (a p) n")
                    sp.dma_start(dst[:, part], s).then_inc(in_w[k], 16)

            def load_b(g):
                if later(g):
                    held(sp, z_step, 4 * g)
                s1 = fb1[g, :, :] if isinstance(g, int) else fb1[bass.ds(g, 1), :, :].rearrange("a p n -> (a p) n")
                s2 = fb2[g:g + 1, :] if isinstance(g, int) else fb2[bass.ds(g, 1), :]
                sp.dma_start(b1t[:, :], s1).then_inc(in_b, 16)
                sp.dma_start(z0[0:1, :], s2).then_inc(in_b, 16)

            xv = x.rearrange("(t p) d -> p t d", p=P)
            xsv = xs[:, :].rearrange("p (t d) -> p t d", d=D)
            sp.dma_start(xsv[:, 0:2], xv[:, 0:2]).then_inc(in_x0, 16)
            for k in range(WPARTS):
                load_w(0, k)
            sp.wait_ge(consts, 4)
            load_b(0)
            sp.dma_start(xsv[:, 2:], xv[:, 2:]).then_inc(in_x, 16)
            sp.wait_ge(pro_dve, 9)
            sp.dma_start(vw_dram, vwt[:, :]).then_inc(vw_out, 16)
            sp.wait_ge(vw_out, 16)
            for h in range(H0):
                sp.dma_start(vw_f[WK * h:WK * (h + 1), :].rearrange("j (g n) -> j g n", g=GROUPS),
                             vw_dram[:, h * D:(h + 1) * D].rearrange("(g j) n -> j g n", g=GROUPS)).then_inc(vw_in, 16)

            def load_k1(b):
                for dst, src in ((kw_hi, kc_hi), (kw_lo, kc_lo)):
                    d4 = f(dst[:, :]).rearrange("p (c i n) -> p c i n", c=KT, i=4)
                    s3 = f(src[:, b * KT * P:(b + 1) * KT * P]).rearrange("p (c n) -> p c n", c=KT)
                    for i in range(4):
                        sp.dma_start(d4[32 * i:32 * i + 32, :, i, :], s3[32 * i:32 * i + 32, :, :]).then_inc(k1_in, 16)

            def load_v1(b):
                for dst, src in ((vw1_hi, vc_hi), (vw1_lo, vc_lo)):
                    d4 = f(dst[:, :]).rearrange("p (c i n) -> p c i n", c=KT, i=4)
                    s4 = f(src[:, b * PAIRS * 32:(b + 1) * PAIRS * 32]).rearrange("p (c i n) -> p c i n", c=KT, i=4)
                    for i in range(4):
                        sp.dma_start(d4[:, :, i, 32 * i:32 * i + 32], s4[:, :, i, :]).then_inc(v1_in, 16)

            with sp.Fori(1, GROUPS) as g:
                for k in range(WPARTS):
                    load_w(g, k)
                load_b(g)
            sp.wait_ge(consts, 6)
            sp.wait_ge(pro_act, 13)
            sp.wait_ge(pro_dve, 18)
            load_k1(0)
            load_v1(0)
            sp.wait_ge(s_psum, 4 * (GROUPS // 2))
            load_k1(1)
            sp.wait_ge(o_part, 4 * (GROUPS // 2))
            load_v1(1)
            sp.wait_ge(c_out, GROUPS)
            sp.dma_start(w2_f[:, :].rearrange("p (c n) -> p c n", c=OC), w2.rearrange("(c p) n -> p c n", p=P)).then_inc(in_ew[1], 16)
            sp.wait_ge(l_psum, 4 * GROUPS)
            sp.dma_start(w1_f[:, :].rearrange("p (k n) -> p k n", k=KT), w1.rearrange("(k p) n -> p k n", p=P)).then_inc(in_ew[0], 16)

            ov = out.rearrange("(t p) d -> t p d", p=P)
            with sp.Fori(0, TILES - 1, 2) as t:
                for s in range(2):
                    held(sp, y_ready, t + s + 1)
                    sp.dma_start(ov[bass.ds(t + s, 1), :, :].rearrange("a p d -> (a p) d"), y[s][:, :]).then_inc(out_done[s], 16)
            for s in range(2):
                sp.wait_ge(out_done[s], 16 * (TILES // 2))

        @block.gpsimd
        def _(pool):
            g_ = nc.gpsimd

            def await_(s, v):
                held(pool, s, v)

            g_.memset(ones[:, :], 1.0).then_inc(consts, 1)
            g_.memset(sc["eps"], LN_EPS).then_inc(consts, 1)
            g_.memset(sc["mhalf"], -0.5).then_inc(consts, 1)
            g_.memset(z0[:, :], 0.0).then_inc(consts, 1)
            for t in (kw_hi, kw_lo, vw1_hi, vw1_lo):
                last = g_.memset(f(t[:, :]), 0.0)
            last.then_inc(consts, 2)
            pool.wait_ge(consts, 6)

            def rstd(ch, g):
                await_(st_ready[ch], 2 * g + 2)
                n = 1 if ch != "D" else 6
                step = [0]

                def own(ins):
                    step[0] += 1
                    ins.then_inc(rs_step[ch], 1)
                    await_(rs_step[ch], n * g + step[0])

                var = sc["mv" + ch][:, 1:4:2]
                own(g_.tensor_tensor(sc["ve" + ch], var, sc["eps"], ALU.add))
                if ch != "D":
                    g_.tensor_tensor(sc["rs" + ch], sc["ve" + ch], sc["mhalf"][:, 0:2], ALU.pow).then_inc(rs_ready[ch], 1)
                    return
                own(g_.tensor_tensor(sc["rstd"], sc["veD"], sc["mhalf"][:, 0:2], ALU.pow))
                own(g_.tensor_tensor(sc["t1"], var, sc["rstd"], ALU.mult))
                own(g_.tensor_tensor(sc["t2"], sc["t1"], sc["rstd"], ALU.mult))
                own(g_.tensor_scalar(sc["t3"], sc["t2"], NORM_EPS ** 2 / D, None, ALU.max))
                own(g_.tensor_tensor(sc["t1"], sc["t3"], sc["mhalf"][:, 0:2], ALU.pow))
                g_.tensor_tensor(sc["rsD"], sc["t1"], sc["rstd"], ALU.mult).then_inc(rs_ready[ch], 1)

            rstd("A", 0)
            pool.wait_ge(pro_act, 1)
            g_.tensor_scalar(sc["ss"], sc["ss"], NORM_EPS ** 2, None, ALU.max).then_inc(pro_pool, 1)
            pool.wait_ge(pro_pool, 1)
            g_.tensor_tensor(sc["rss"], sc["ss"], sc["mhalf"], ALU.pow).then_inc(pro_pool, 1)
            pool.wait_ge(pro_pool, 2)
            g_.tensor_scalar(sc["rss"], sc["rss"], float(D) ** 0.5, None, ALU.mult).then_inc(pro_pool, 1)

            def bias(g):
                def own(n, ins):
                    ins.then_inc(z_step, 1)
                    await_(z_step, 4 * g + n)

                await_(z_prod, OC * (g + 1))
                own(1, g_.tensor_tensor(prod[:, 0:4 * D], prod[:, 0:4 * D], prod[:, 4 * D:8 * D], ALU.add))
                own(2, g_.tensor_tensor(prod[:, 0:2 * D], prod[:, 0:2 * D], prod[:, 2 * D:4 * D], ALU.add))
                own(3, g_.tensor_tensor(prod[:, 0:D], prod[:, 0:D], prod[:, D:2 * D], ALU.add))
                if later(g):
                    await_(z_hid, g)
                await_(in_b, 32 * (g + 1))
                g_.tensor_tensor(z[:, :], prod[:, 0:D], z0[:, :], ALU.add).then_inc(z_step, 1)

            def bias_lo(g):
                await_(z_hid, g + 1)
                g_.tensor_tensor(z_lo[:, :], z[:, :], f(z_hi[:, :]), ALU.subtract).then_inc(z_lod, 1)

            def round_1a(r):
                if has(r, 1):
                    rstd("B", r - 1)
                    bias_lo(r - 1)
                if is_tail(r):
                    rstd("C", 0)
                if has(r, -2):
                    rstd("A", r + 2)
                if has(r, 0):
                    bias(r)

            loop(pool, round_1a, -1, 2, GROUPS - 2, GROUPS + 1)

            pool.wait_ge(b_out, GROUPS)
            for t, v in ((xn_hi, 1.0), (xn_lo, 0.0)):
                g_.memset(f(t[:, :]).rearrange("p (t n) -> p t n", n=XW)[:, :, D:XW], v)

            def xn_low(g):
                await_(xn_hid, g + 1)
                g_.tensor_tensor(cols(xn_lo, g * (2 * XW), 2 * XW).rearrange("p (t n) -> p t n", n=XW)[:, :, 0:D],
                                 lnx["D"][:, :].rearrange("p (t n) -> p t n", n=D),
                                 f(cols(xn_hi, g * (2 * XW), 2 * XW)).rearrange("p (t n) -> p t n", n=XW)[:, :, 0:D],
                                 ALU.subtract).then_inc(xn_lod, 1)

            def sig_low(g, j):
                await_(s_hid, 4 * g + j + 1)
                g_.tensor_tensor(sig_lo[j][:, :], sig[1][:, :], f(sig_hi[j][:, :]), ALU.subtract).then_inc(s_lod[1], 1)

            def round_1b(r):
                if has(r, -1):
                    rstd("C", r + 1)
                if has(r, 0):
                    sig_low(r, 1)
                if has(r, 1):
                    rstd("D", r - 1)
                if has(r, 0):
                    sig_low(r, 3)
                if has(r, 1):
                    xn_low(r - 1)

            loop(pool, round_1b, 0, 3, GROUPS - 1, GROUPS + 1)

            def e_sub(n, s):
                b, m = n // SM, n % SM
                await_(cm_sb, 2 * (n // SM) + 2)
                if later(n, 4):
                    await_(sl_psum, n - 3)
                g_.tensor_tensor(ef[s][:, :].rearrange("p (t s) -> p t s", t=SM), logits_view(b, m),
                                 cols(cmb, b * SLOTS + m * P, P).unsqueeze(1).to_broadcast([P, SM, P]), ALU.subtract).then_inc(d_sub, 1)

            dispatch_steps(pool, e_sub, 0, 16)

        @block.scalar
        def _(act):
            a_ = nc.scalar
            act.dma_start(ctx_s[:, :], ctx2).then_inc(in_ctx, 16)
            act.dma_start(pe_s[:, :], pe).then_inc(in_ctx, 16)
            act.dma_start(wk0s[:, :].rearrange("p (k n) -> p k n", k=KT), wk0.rearrange("(k p) n -> p k n", p=P)).then_inc(in_kv0, 16)
            act.dma_start(wv0s[:, :].rearrange("p (k n) -> p k n", k=KT), wv0.rearrange("(k p) n -> p k n", p=P)).then_inc(in_kv0, 16)
            act.dma_start(wq0s[:, :].rearrange("p (k n) -> p k n", k=4), wq0T.rearrange("(k p) n -> p k n", p=P)).then_inc(in_o0, 16)
            act.dma_start(wo0s[:, :].rearrange("p (k n) -> p k n", k=4), wo0.rearrange("(k p) n -> p k n", p=P)).then_inc(in_o0, 16)
            act.dma_start(bo_s[:, :], bo.to_broadcast([P, D])).then_inc(in_o0, 16)
            act.dma_start(ident[:, :], ident_in).then_inc(in_id, 16)
            act.dma_start(slot_s[:, :].rearrange("p (m n) -> p m n", m=SM), slot.rearrange("(m p) n -> p m n", p=P)).then_inc(in_slot, 16)
            act.dma_start(sc["gxs"], gx).then_inc(in_g, 16)
            act.dma_start(sc["gss"], gs).then_inc(in_g, 16)
            for dst, src in ((wk1s, wk1T), (wv1s, wv1T), (wq1_f, wq1T), (wo1_f, wo1T)):
                act.dma_start(dst[:, :].rearrange("p (k n) -> p k n", k=KT), src.rearrange("(k p) n -> p k n", p=P)).then_inc(in_l1, 16)
            act.dma_start(mk_s[:, :], mask_k).then_inc(in_l1, 16)
            act.dma_start(mv_s[:, :], mask_v).then_inc(in_l1, 16)

            def copy(dst, src, done, n=1):
                a_.activation(dst, src, ACT.Copy).then_inc(done, n)

            act.wait_ge(in_slot, 16)
            for m in range(SM):
                last = a_.activation(sq[:, m * D:(m + 1) * D], slot_s[:, m * D:(m + 1) * D], ACT.Square, accum_out=sc["ss"][:, m:m + 1])
            last.then_inc(pro_act, 1)
            act.wait_ge(consts, 1)
            copy(ones_r[:, :], ones[:, :], pro_act)
            act.wait_ge(pro_pe, 1)
            copy(kT0[:, :], bank[0][:, :], pro_act)
            for k in range(KT):
                for par in range(2):
                    act.wait_ge(pro_pe, 3)
                    copy(a_hi[:, :].rearrange("p (g k h j) -> p k h g j", g=GROUPS, k=KT, h=H0)[:, k, par::2],
                         bank[2 + 2 * k + par][:, :].rearrange("p (h g j) -> p h g j", h=4, g=GROUPS), pro_act)
            act.wait_ge(in_l1, 96)
            copy(wq1_hi[:, :], wq1_f[:, :], pro_act)
            copy(wo1_hi[:, :], wo1_f[:, :], pro_act)
            act.wait_ge(vw_in, 16 * H0)
            copy(vw_hi[:, :], vw_f[:, :], pro_act)

            def norm_T_hi(ch, g):
                act.wait_ge(xT_psum[ch], g + 1)
                bk = {"A": 0, "B": 3, "C": 0, "D": 1}[ch]
                copy(xT_hi[ch][:, :], bank[bk][:, :], xT_hid[ch])

            def late_prologue():
                act.wait_ge(pro_dve, 16)
                copy(kc_hi[:, :], kc_f[:, :], pro_act)
                copy(vc_hi[:, :], vc_f[:, :], pro_act, 2)
                act.wait_ge(pro_pe, 6)
                act.wait_ge(pro_dve, 17)
                for k in range(KT):
                    for hlf in range(2):
                        a_.activation(se_f[:, k * SLOTS + hlf * 512:k * SLOTS + hlf * 512 + 512], bank[4 + 2 * k + hlf][:, :],
                                      ACT.Copy, scale=sc["gg"][:, k:k + 1]).then_inc(pro_act, 1)
                act.wait_ge(pro_act, 17)
                copy(se_hi[:, :], se_f[:, :], pro_act)

            def bias_product(g, k):
                act.wait_ge(in_w[k], 32 * (g + 1))
                if k == 0:
                    act.wait_ge(in_b, 32 * (g + 1))
                    if later(g):
                        act.wait_ge(z_step, 4 * g)
                for c in (2 * k, 2 * k + 1):
                    a_.activation(prod[:, c * D:(c + 1) * D], w2r[:, c * D:(c + 1) * D], ACT.Copy, scale=b1t[:, c:c + 1]).then_inc(z_prod, 1)

            def query_hi(g):
                act.wait_ge(q_psum, g + 1)
                copy(q_hi[:, :], bank[2][:, :], q_hid)

            def round_1a(r):
                if has(r, -1):
                    norm_T_hi("A", r + 1)
                if has(r, 0):
                    act.wait_ge(e_in, r + 1)
                    a_.activation(probs[:, :], probs[:, :], ACT.Exp, scale=DH0 ** -0.5).then_inc(e_out, 1)
                if has(r, 1):
                    act.wait_ge(z_step, 4 * r)
                    if later(r, 2):
                        act.wait_ge(b_out, r - 1)
                    copy(z_hi[:, :], z[:, :], z_hid)
                if has(r, 0):
                    bias_product(r, 0)
                    bias_product(r, 1)
                if has(r, 1):
                    norm_T_hi("B", r - 1)
                if is_tail(r):
                    norm_T_hi("C", 0)
                    query_hi(0)
                if has(r, 0):
                    act.wait_ge(pT_psum, r + 1)
                    copy(pT_hi[:, :], bank[2][:, 0:2 * P], pT_hid)
                    bias_product(r, 2)
                    bias_product(r, 3)
                    act.wait_ge(w_used, 4 * r + 4)
                    copy(c_hi[:, :], bank[5][:, :], c_hid)

            late_prologue()
            loop(act, round_1a, -1, 2, GROUPS - 2, GROUPS + 1)

            def logit_copy(g, i):
                act.wait_ge(l_psum, 4 * g + i + 1)
                copy(cols(logits, g * (2 * SLOTS) + i * 512, 512), bank[6 + i % 2][:, :], l_sb)

            def sigmoid(g, j):
                act.wait_ge(s_psum, 4 * g + j + 1)
                if later(4 * g + j, 2):
                    act.wait_ge(s_lod[j % 2], 2 * g + j // 2)
                a_.activation(sig[j % 2][:, :], bank[3 + j % 2][:, :], ACT.Sigmoid, scale=DH1 ** -0.5).then_inc(s_sig, 1)
                act.wait_ge(s_sig, 4 * g + j + 1)
                if later(g):
                    act.wait_ge(o_part, 4 * g + j - 3)
                copy(sig_hi[j][:, :], sig[j % 2][:, :], s_hid)

            def e_exp(n, s):
                act.wait_ge(d_sub, n + 1)
                a_.activation(ef[s][:, :], ef[s][:, :], ACT.Exp).then_inc(d_exp, 1)

            def e_high(n, s):
                act.wait_ge(d_exp, n + 1)
                if later(n, 4):
                    act.wait_ge(sl_psum, n - 3)
                copy(e_hi[s][:, :], ef[s][:, :], d_hi)

            def spread_copy(b):
                for i in range(2):
                    act.wait_ge(cm_bc, 2 * b + i + 1)
                    copy(cmb[:, b * SLOTS + i * 512:b * SLOTS + i * 512 + 512], bank[spread_bank[b][i]][:, :], cm_sb)

            def round_1b(r):
                if has(r, 2):
                    norm_T_hi("D", r - 2)
                if is_tail(r, 9):
                    e_exp(0, 0)
                if has(r, 0):
                    sigmoid(r, 0)
                    sigmoid(r, 1)
                if has(r, 2):
                    logit_copy(r - 2, 0)
                if has(r, 0):
                    sigmoid(r, 2)
                if has(r, -1):
                    norm_T_hi("C", r + 1)
                if is_tail(r, 9):
                    e_high(0, 0)
                if has(r, 0):
                    sigmoid(r, 3)
                if has(r, 2):
                    logit_copy(r - 2, 1)
                if has(r, 1):
                    act.wait_ge(ln_ready["D"], 2 * r)
                    copy(cols(xn_hi, (r - 1) * (2 * XW), 2 * XW).rearrange("p (t n) -> p t n", n=XW)[:, :, 0:D],
                         lnx["D"][:, :].rearrange("p (t n) -> p t n", n=D), xn_hid)
                if is_tail(r, 8):
                    spread_copy(0)
                if is_tail(r, 9):
                    e_exp(1, 1)
                if has(r, -1):
                    query_hi(r + 1)
                if has(r, 2):
                    logit_copy(r - 2, 2)
                if is_tail(r, 9):
                    e_high(1, 1)
                if has(r, 0):
                    act.wait_ge(o_part, 4 * r + 4)
                    copy(o_hi[:, :], bank[5][:, :], o_hid)
                if has(r, 2):
                    logit_copy(r - 2, 3)

            loop(act, round_1b, 0, 3, GROUPS - 1, GROUPS + 2)

            def slT_high(n, s):
                act.wait_ge(slT_psum, n + 1)
                copy(cols(slT_hi, n * (2 * P), 2 * P), bank[2 + s % 2][:, 0:2 * P], slT_hid)

            def step_2(n, s):
                if has(n, 2, 16):
                    slT_high(n - 2, (s + 2) % 4)
                if has(n, -2, 16):
                    e_exp(n + 2, (s + 2) % 4)
                    e_high(n + 2, (s + 2) % 4)
                if is_tail(n, 3):
                    spread_copy(1)
                if isinstance(n, int) and 14 <= n:
                    for i in (2 * (n - 14), 2 * (n - 14) + 1) if n < 16 else ():
                        act.wait_ge(in_ew[1], 16)
                        copy(w2_hi[:, i * 512:(i + 1) * 512], w2_f[:, i * 512:(i + 1) * 512], ew_hi)

            dispatch_steps(act, step_2, 0, 18)

            def gelu(c, j):
                act.wait_ge(h_psum, 4 * c + j + 1)
                if later(4 * c + j, 2):
                    act.wait_ge(g_lo, 4 * c + j - 1)
                a_.activation(hf[j % 2][:, :], bank[4 + j % 2][:, :], ACT.Gelu).then_inc(g_act, 1)

            def expert_hi(c):
                act.wait_ge(p_part, 4 * c + 4)
                copy(cols(xn_hi, c * (2 * XW), 2 * XW).rearrange("p (t n) -> p t n", n=XW)[:, :, 0:D],
                     bank[6][:, :].rearrange("p (t n) -> p t n", n=D), pr_hi)

            def chunk(c):
                gelu(c, 0)
                if has(c, 1):
                    expert_hi(c - 1)
                for j in range(1, 4):
                    gelu(c, j)

            loop(act, chunk, 0, 1, GROUPS, GROUPS)

            def comb_exp(t, s):
                act.wait_ge(nrow_done, 1)
                if later(t, 2):
                    act.wait_ge(e2_psum, 2 * t - 2)
                a_.activation(ef[s][:, :], cols(logits, t * SLOTS, SLOTS), ACT.Exp,
                              bias=cols(sc["nrow"], t, 1)).then_inc(e2_act, 1)

            def comb_hi(t, s):
                for i in range(2):
                    act.wait_ge(e2_psum, 2 * t + i + 1)
                    if i == 0 and later(t, 2):
                        act.wait_ge(y_psum, t - 1)
                    copy(e2T_hi[s][:, i * 512:(i + 1) * 512], bank[2 * s + i][:, :], e2_hi)

            def step_4(t, s):
                if has(t, -1, TILES):
                    comb_hi(t + 1, 1 - s)
                if has(t, -2, TILES):
                    comb_exp(t + 2, s)

            comb_exp(0, 0)
            comb_exp(1, 1)
            expert_hi(GROUPS - 1)
            comb_hi(0, 0)
            for t in range(0, 2):
                step_4(t, t % 2)
            with act.Fori(2, 13, 2) as t:
                for s in range(2):
                    step_4(t + s, s)
            for t in range(14, 16):
                step_4(t, t % 2)

        @block.vector
        def _(dve):
            v_ = nc.vector

            def stats(ch, g):
                if ch == "A":
                    dve.wait_ge(in_x0, 16)
                    if later(g):
                        dve.wait_ge(in_x, 16)
                else:
                    held(dve, x_ready[ch], g + 1)
                for u in range(2):
                    v_.bn_stats(sc["bn" + ch][:, 6 * u:6 * u + 6], cols(xs, g * (2 * D) + u * D, D)).then_inc(bn_done[ch], 1)
                held(dve, bn_done[ch], 2 * g + 2)
                for u in range(2):
                    v_.bn_aggr(sc["mv" + ch][:, 2 * u:2 * u + 2], sc["bn" + ch][:, 6 * u:6 * u + 6]).then_inc(st_ready[ch], 1)

            def normed(ch, g):
                dve.wait_ge(rs_ready[ch], g + 1)
                if ch == "D" and later(g):
                    dve.wait_ge(xn_lod, g)
                for u in range(2):
                    v_.tensor_scalar(lnx[ch][:, u * D:(u + 1) * D], cols(xs, g * (2 * D) + u * D, D),
                                     sc["mv" + ch][:, 2 * u:2 * u + 1], sc["rs" + ch][:, u:u + 1],
                                     ALU.subtract, ALU.mult).then_inc(ln_ready[ch], 1)

            def low(dst, src, hi, done, n=1):
                v_.tensor_tensor(dst, src, f(hi), ALU.subtract).then_inc(done, n)

            def norm_T_lo(ch, g):
                dve.wait_ge(xT_hid[ch], g + 1)
                bk = {"A": 0, "B": 3, "C": 0, "D": 1}[ch]
                low(xT_lo[ch][:, :], bank[bk][:, :], xT_hi[ch][:, :], xT_lod[ch])

            def residual(ch, g, bk):
                v_.tensor_tensor(xg(g), xg(g), bank[bk][:, :], ALU.add).then_inc(x_ready[ch], 1)

            stats("A", 0)
            dve.wait_ge(in_ctx, 32)
            ctx5 = ctx_s[:, :].rearrange("p (k b c s) -> p k b c s", k=KT, b=BATCH, c=2)
            v_.tensor_tensor(hcT[:, :].rearrange("p (k b s) -> p k b s", k=KT, b=BATCH), ctx5[:, :, :, 0, :],
                             pe_s[:, :].rearrange("p (k s) -> p k s", k=KT).unsqueeze(2).to_broadcast([P, KT, BATCH, KEYS]),
                             ALU.add).then_inc(pro_dve, 1)
            normed("A", 0)
            dve.wait_ge(in_o0, 48)
            v_.tensor_scalar(bo_s[:, :], bo_s[:, :], 1.0 / H0, None, ALU.mult).then_inc(pro_dve, 1)
            dve.wait_ge(pro_pe, 2)
            v_.tensor_copy(vT0[:, :], bank[1][:, :]).then_inc(pro_dve, 1)
            for i in range(4):
                k, par = i // 2, i % 2
                dve.wait_ge(pro_act, 4 + i)
                view = lambda t: t[:, :].rearrange("p (g k h j) -> p k h g j", g=GROUPS, k=KT, h=H0)[:, k, par::2]
                last = v_.tensor_tensor(view(a_lo), bank[2 + i][:, :].rearrange("p (h g j) -> p h g j", h=4, g=GROUPS),
                                        f(view(a_hi)), ALU.subtract)
            last.then_inc(pro_dve, 1)
            dve.wait_ge(pro_pe, 4)
            for i, (bk, h) in enumerate(((6, 0), (7, 1), (0, 4), (1, 5))):
                v_.tensor_tensor(vwt[:, :].rearrange("p (h n) -> p h n", h=H0)[:, h:h + 3:2], bank[bk][:, :].rearrange("p (h n) -> p h n", h=2),
                                 bo_s[:, :].unsqueeze(1).to_broadcast([P, 2, D]), ALU.add).then_inc(pro_dve, 1 if i < 3 else 2)
            dve.wait_ge(pro_pool, 3)
            v_.tensor_tensor(slot_s[:, :].rearrange("p (m n) -> p m n", m=SM), slot_s[:, :].rearrange("p (m n) -> p m n", m=SM),
                             sc["rss"].unsqueeze(2).to_broadcast([P, SM, D]), ALU.mult).then_inc(pro_dve, 1)
            dve.wait_ge(in_l1, 96)
            dve.wait_ge(pro_act, 9)
            low(wq1_lo[:, :], wq1_f[:, :], wq1_hi[:, :], pro_dve)
            low(wo1_lo[:, :], wo1_f[:, :], wo1_hi[:, :], pro_dve)
            dve.wait_ge(pro_pe, 5)
            kb = bank[2][:, 0:256].rearrange("p (c b s) -> p c b s", c=KT, b=BATCH)
            for b in range(BATCH):
                v_.tensor_tensor(kc_f[:, b * KT * P:(b + 1) * KT * P].rearrange("p (c h s) -> p c h s", c=KT, h=2),
                                 kb[:, :, b, :].unsqueeze(2).to_broadcast([P, KT, 2, KEYS]),
                                 mk_s[:, :].rearrange("p (h s) -> p h s", h=2).unsqueeze(1).to_broadcast([P, KT, 2, KEYS]),
                                 ALU.mult).then_inc(pro_dve, 1)
            v_.tensor_tensor(vc_f[:, :].rearrange("p (m n) -> p m n", n=32), bank[3][:, :].rearrange("p (m n) -> p m n", n=32),
                             mv_s[:, :].unsqueeze(1).to_broadcast([P, BATCH * PAIRS, 32]), ALU.mult).then_inc(pro_dve, 2)
            dve.wait_ge(in_g, 32)
            v_.tensor_tensor(sc["gg"], sc["gxs"], sc["gss"], ALU.mult).then_inc(pro_dve, 1)
            dve.wait_ge(pro_act, 13)
            low(kc_lo[:, :], kc_f[:, :], kc_hi[:, :], tick)
            low(vc_lo[:, :], vc_f[:, :], vc_hi[:, :], pro_dve)
            dve.wait_ge(pro_act, 10)
            low(vw_lo[:, :], vw_f[:, :], vw_hi[:, :], pro_dve)
            dve.wait_ge(pro_act, 18)
            low(se_lo[:, :], se_f[:, :], se_hi[:, :], pro_dve)

            pv = probs[:, :].rearrange("p (a j) -> p a j", j=WK)
            bcast = lambda ap: ap.unsqueeze(2).to_broadcast([P, 2 * H0, WK])

            def query_lo(g):
                dve.wait_ge(q_hid, g + 1)
                low(q_lo[:, :], bank[2][:, :], q_hi[:, :], q_lod)

            def round_1a(r):
                if has(r, 1):
                    dve.wait_ge(a_out, r)
                    residual("B", r - 1, 1)
                    stats("B", r - 1)
                if is_tail(r):
                    stats("C", 0)
                if has(r, 0):
                    scores = bank[6][:, 0:2 * P].rearrange("p (a j) -> p a j", j=WK)
                    dve.wait_ge(sc_psum, r + 1)
                    v_.tensor_reduce(sc["mx"], scores, AXX, ALU.max).then_inc(sm_step, 1)
                    dve.wait_ge(sm_step, 3 * r + 1)
                    if later(r):
                        dve.wait_ge(pT_psum, r)
                    v_.tensor_tensor(pv, scores, bcast(sc["mx"]), ALU.subtract).then_inc(e_in, 1)
                if has(r, -1):
                    norm_T_lo("A", r + 1)
                if has(r, 1):
                    normed("B", r - 1)
                if is_tail(r):
                    normed("C", 0)
                if has(r, 0):
                    dve.wait_ge(e_out, r + 1)
                    v_.tensor_reduce(sc["sm"], pv, AXX, ALU.add).then_inc(sm_step, 1)
                    dve.wait_ge(sm_step, 3 * r + 2)
                    v_.reciprocal(sc["rc"], sc["sm"]).then_inc(sm_step, 1)
                    dve.wait_ge(sm_step, 3 * r + 3)
                    v_.tensor_tensor(pv, pv, bcast(sc["rc"]), ALU.mult).then_inc(p_ready, 1)
                if has(r, -2):
                    stats("A", r + 2)
                if has(r, 1):
                    norm_T_lo("B", r - 1)
                if is_tail(r):
                    norm_T_lo("C", 0)
                if has(r, 0):
                    dve.wait_ge(pT_hid, r + 1)
                    low(pT_lo[:, :], bank[2][:, 0:2 * P], pT_hi[:, :], pT_lod)
                if has(r, -2):
                    normed("A", r + 2)
                if has(r, 1):
                    dve.wait_ge(b_out, r)
                    residual("C", r - 1, 4)
                if is_tail(r):
                    query_lo(0)
                if has(r, 0):
                    dve.wait_ge(c_hid, r + 1)
                    low(c_lo[:, :], bank[5][:, :], c_hi[:, :], c_lod)

            loop(dve, round_1a, -1, 2, GROUPS - 2, GROUPS + 1)

            v_.memset(colmax[:, :], LOWEST).then_inc(colmax_done, 1)
            dve.wait_ge(colmax_done, 1)

            def sig_low(g, j):
                dve.wait_ge(s_hid, 4 * g + j + 1)
                low(sig_lo[j][:, :], sig[0][:, :], sig_hi[j][:, :], s_lod[0])

            def maxima(g, u):
                dve.wait_ge(l_sb, 4 * g + 2 * u + 2)
                tile = cols(logits, g * (2 * SLOTS) + u * SLOTS, SLOTS)
                v_.tensor_reduce(cols(sc["rowmax"], 2 * g + u, 1), tile, AXX, ALU.max).then_inc(rowmax_done, 1)
                dve.wait_ge(colmax_done, 2 * g + u + 1)
                acc = cols(colmax, (g // 4) * SLOTS, SLOTS)
                v_.tensor_tensor(acc, acc, tile, ALU.max).then_inc(colmax_done, 1)

            def column_maxima(b):
                for i in range(2):
                    dve.wait_ge(cmT, 2 * b + i + 1)
                    v_.tensor_reduce(sc["cm"][:, b * SM + 4 * i:b * SM + 4 * i + 4],
                                     bank[cmT_bank[b][i]][:, :].rearrange("p (m t) -> p m t", m=4), AXX, ALU.max).then_inc(cm_red, 1)
                dve.wait_ge(cm_red, 2 * b + 2)
                v_.tensor_tensor(diag[b][:, :].rearrange("p (m s) -> p m s", m=SM),
                                 ident[:, :].unsqueeze(1).to_broadcast([P, SM, P]),
                                 sc["cm"][:, b * SM:(b + 1) * SM].unsqueeze(2).to_broadcast([P, SM, P]), ALU.mult).then_inc(cm_diag, 1)

            def e_low(n, s):
                dve.wait_ge(d_hi, n + 1)
                low(e_lo[s][:, :], ef[s][:, :], e_hi[s][:, :], d_lo)

            def round_1b(r):
                if has(r, -1):
                    stats("C", r + 1)
                if has(r, 2):
                    norm_T_lo("D", r - 2)
                if has(r, 0):
                    sig_low(r, 0)
                if has(r, 1):
                    dve.wait_ge(c_out, r)
                    residual("D", r - 1, 2)
                    stats("D", r - 1)
                if is_tail(r, 8):
                    column_maxima(0)
                if has(r, -1):
                    normed("C", r + 1)
                if is_tail(r, 8):
                    normed("D", r - 1)
                if has(r, 3):
                    maxima(r - 3, 1)
                if has(r, -1):
                    norm_T_lo("C", r + 1)
                if has(r, 0):
                    sig_low(r, 2)
                if has(r, 1) and not is_tail(r, 8):
                    normed("D", r - 1)
                if has(r, -1):
                    query_lo(r + 1)
                if is_tail(r, 9):
                    e_low(0, 0)
                if has(r, 2):
                    maxima(r - 2, 0)
                if has(r, 0):
                    dve.wait_ge(o_hid, r + 1)
                    low(o_lo[:, :], bank[5][:, :], o_hi[:, :], o_lod)

            loop(dve, round_1b, 0, 3, GROUPS - 1, GROUPS + 2)

            def slot_norm(n, s):
                dve.wait_ge(sl_psum, n + 1)
                v_.reciprocal(sc["rec"][:, s % 2:s % 2 + 1], bank[s % 2][:, D:D + 1]).then_inc(sl_rec, 1)
                dve.wait_ge(sl_rec, n + 1)
                v_.tensor_scalar(sf[s % 2][:, :], bank[s % 2][:, 0:D], sc["rec"][:, s % 2:s % 2 + 1], None, ALU.mult).then_inc(sl_norm, 1)

            def slT_low(n, s):
                dve.wait_ge(slT_hid, n + 1)
                low(cols(slT_lo, n * (2 * P), 2 * P), bank[2 + s % 2][:, 0:2 * P], cols(slT_hi, n * (2 * P), 2 * P), slT_lod)

            def w1_split(i):
                dve.wait_ge(in_ew[0], 16)
                part, gamma = slice(i * 512, (i + 1) * 512), sc["gxs"][:, i // 2:i // 2 + 1]
                v_.tensor_scalar(w1_hi[:, part], w1_f[:, part], gamma, None, ALU.mult).then_inc(w1_hid, 1)
                dve.wait_ge(w1_hid, i + 1)
                v_.scalar_tensor_tensor(out=w1_lo[:, part], in0=w1_f[:, part], scalar=gamma, in1=f(w1_hi[:, part]),
                                        op0=ALU.mult, op1=ALU.subtract).then_inc(ew_lo, 1)

            def w2_low(i):
                dve.wait_ge(ew_hi, i + 1)
                part = slice(i * 512, (i + 1) * 512)
                low(w2_lo[:, part], w2_f[:, part], w2_hi[:, part], ew_lo)

            def step_2(n, s):
                if has(n, -1, 16):
                    e_low(n + 1, (s + 1) % 4)
                if has(n, 1, 16):
                    slot_norm(n - 1, (s + 3) % 4)
                if has(n, 2, 16):
                    slT_low(n - 2, (s + 2) % 4)
                if is_tail(n, 0):
                    maxima(GROUPS - 1, 1)
                if is_tail(n, 2):
                    column_maxima(1)
                if isinstance(n, int) and 12 <= n < 16:
                    w1_split(n - 12)
                if isinstance(n, int) and 14 <= n < 18:
                    w2_low(n - 14)

            dispatch_steps(dve, step_2, 0, 18)
            v_.tensor_scalar(sc["nrow"], sc["rowmax"], -1.0, None, ALU.mult).then_inc(nrow_done, 1)

            def gelu_split(c, j):
                dve.wait_ge(g_act, 4 * c + j + 1)
                if later(4 * c + j, 4):
                    dve.wait_ge(p_part, 4 * c + j - 3)
                v_.tensor_copy(h_hi[j][:, :], hf[j % 2][:, :]).then_inc(g_hi, 1)
                dve.wait_ge(g_hi, 4 * c + j + 1)
                low(h_lo[j][:, :], hf[j % 2][:, :], h_hi[j][:, :], g_lo)

            def expert_lo(c):
                dve.wait_ge(pr_hi, c + 1)
                view = lambda t: cols(t, c * (2 * XW), 2 * XW).rearrange("p (t n) -> p t n", n=XW)[:, :, 0:D]
                v_.tensor_tensor(view(xn_lo), bank[6][:, :].rearrange("p (t n) -> p t n", n=D), f(view(xn_hi)), ALU.subtract).then_inc(pr_lo, 1)

            def chunk(c):
                gelu_split(c, 0)
                if has(c, 1):
                    expert_lo(c - 1)
                for j in range(1, 4):
                    gelu_split(c, j)

            loop(dve, chunk, 0, 1, GROUPS, GROUPS)
            expert_lo(GROUPS - 1)

            def comb_lo(t, s):
                for i in range(2):
                    dve.wait_ge(e2_hi, 2 * t + i + 1)
                    low(e2T_lo[s][:, i * 512:(i + 1) * 512], bank[2 * s + i][:, :], e2T_hi[s][:, i * 512:(i + 1) * 512], e2_lo)

            def finish(t, s):
                dve.wait_ge(y_psum, t + 1)
                v_.reciprocal(sc["rec4"][:, s:s + 1], bank[4 + s][:, D:D + 1]).then_inc(y_rec, 1)
                dve.wait_ge(y_rec, t + 1)
                if later(t, 2):
                    dve.wait_ge(out_done[s], (t // 2) * 16)
                v_.scalar_tensor_tensor(out=y[s][:, :], in0=bank[4 + s][:, 0:D], scalar=sc["rec4"][:, s:s + 1],
                                        in1=cols(xs, t * D, D), op0=ALU.mult, op1=ALU.add).then_inc(y_ready, 1)

            def step_4(t, s):
                if has(t, -1, TILES):
                    comb_lo(t + 1, 1 - s)
                if has(t, 0, TILES):
                    finish(t, s)

            for t in range(-1, 2):
                step_4(t, t % 2)
            with dve.Fori(2, 13, 2) as t:
                for s in range(2):
                    step_4(t + s, s)
            for t in range(14, 16):
                step_4(t, t % 2)

        @block.tensor
        def _(pe_):
            mm = nc.tensor.matmul

            pe_.wait_ge(pro_dve, 1)
            pe_.wait_ge(in_kv0, 32)
            for bk, w in ((0, wk0s), (1, wv0s)):
                for ct in range(4):
                    for k in range(KT):
                        last = mm(bank[bk][:, ct * P:(ct + 1) * P], w[:, k * 512 + ct * P:k * 512 + (ct + 1) * P],
                                  hcT[:, k * P:(k + 1) * P], start=k == 0, stop=k == KT - 1)
                last.then_inc(pro_pe, 1)
            pe_.wait_ge(in_o0, 48)
            pe_.wait_ge(pro_act, 3)
            for k in range(KT):
                for h in range(H0):
                    par, i = h % 2, h // 2
                    rows = slice(DH0 * par, DH0 * (par + 1))
                    last = mm(bank[2 + 2 * k + par][:, i * P:(i + 1) * P], wq0s[rows, i * D + k * P:i * D + (k + 1) * P],
                              kT0[rows, i * P:(i + 1) * P], start=True, stop=True)
            last.then_inc(pro_pe, 1)
            pe_.wait_ge(pro_dve, 3)
            for h in range(H0):
                par, i = h % 2, h // 2
                rows = slice(DH0 * par, DH0 * (par + 1))
                bk = (6 if i < 2 else 0) + par
                last = mm(bank[bk][:, (i % 2) * D:(i % 2 + 1) * D], vT0[rows, i * P:(i + 1) * P],
                          wo0s[rows, i * D:(i + 1) * D], start=True, stop=True)
            last.then_inc(pro_pe, 1)
            pe_.wait_ge(in_l1, 96)
            pe_.wait_ge(pro_dve, 9)
            ctx5 = ctx_s[:, :].rearrange("p (k b c s) -> p k b c s", k=KT, b=BATCH, c=2)
            for ct in range(KT):
                for k in range(KT):
                    mm(bank[2][:, ct * P:(ct + 1) * P], wk1s[:, k * D + ct * P:k * D + (ct + 1) * P], ctx5[:, k, :, 0, :],
                       start=k == 0, stop=k == KT - 1)
            for b in range(BATCH):
                for k in range(KT):
                    last = mm(bank[3][:, b * D:(b + 1) * D], ctx_s[:, (k * BATCH + b) * P:(k * BATCH + b + 1) * P],
                              wv1s[:, k * D:(k + 1) * D], start=k == 0, stop=k == KT - 1)
            last.then_inc(pro_pe, 1)
            pe_.wait_ge(in_id, 16)
            pe_.wait_ge(pro_dve, 10)
            for k in range(KT):
                for m in range(SM):
                    last = nc.tensor.transpose(bank[4 + 2 * k + m // 4][:, (m % 4) * P:(m % 4 + 1) * P],
                                               slot_s[:, m * D + k * P:m * D + (k + 1) * P], ident[:, :])
            last.then_inc(pro_pe, 1)

            def norm_T(ch, g):
                pe_.wait_ge(ln_ready[ch], 2 * g + 2)
                bk = {"A": 0, "B": 3, "C": 0, "D": 1}[ch]
                for k in range(KT):
                    for u in range(2):
                        last = nc.tensor.transpose(bank[bk][:, k * GT + u * P:k * GT + (u + 1) * P],
                                                   lnx[ch][:, u * D + k * P:u * D + (k + 1) * P], ident[:, :])
                last.then_inc(xT_psum[ch], 1)

            def xT(ch, k, u=None):
                lo, n = (k * GT, GT) if u is None else (k * GT + u * P, P)
                return xT_hi[ch][:, lo:lo + n], xT_lo[ch][:, lo:lo + n]

            def pair(hi, lo, start, n):
                return cols(hi, start, n), cols(lo, start, n)

            def fuse(g, k):
                pe_.wait_ge(in_w[k], 32 * (g + 1))
                if k == 0 and later(g):
                    pe_.wait_ge(c_lod, g)
                for c in (2 * k, 2 * k + 1):
                    for m in range(KT):
                        last = mm(bank[5][:, m * D:(m + 1) * D], w1r[:, c * D + m * P:c * D + (m + 1) * P],
                                  w2r[:, c * D:(c + 1) * D], start=c == 0 and m == 0, stop=c == OC - 1 and m == KT - 1,
                                  skip_group_check=True)
                last.then_inc(w_used, 1)

            def scores(g):
                pe_.wait_ge(xT_lod["A"], g + 1)
                for u in range(2):
                    for k in range(KT):
                        last = split3(bank[6][:, u * P:(u + 1) * P], xT("A", k, u),
                                      pair(a_hi, a_lo, g * (KT * P) + k * P, P), k == 0, k == KT - 1)
                last.then_inc(sc_psum, 1)

            def probs_T(g):
                pe_.wait_ge(p_ready, g + 1)
                for u in range(2):
                    last = nc.tensor.transpose(bank[2][:, u * P:(u + 1) * P], probs[:, u * P:(u + 1) * P], ident[:, :])
                last.then_inc(pT_psum, 1)

            def attend(g):
                pe_.wait_ge(pT_lod, g + 1)
                for u in range(2):
                    last = split3(bank[1][:, u * D:(u + 1) * D],
                                  (pT_hi[:, u * P:(u + 1) * P], pT_lo[:, u * P:(u + 1) * P]),
                                  pair(vw_hi, vw_lo, g * D, D), True, True)
                last.then_inc(a_out, 1)

            def query(g):
                pe_.wait_ge(xT_lod["C"], g + 1)
                if later(g, 2):
                    pe_.wait_ge(x_ready["D"], g - 1)
                for ct in range(KT):
                    for k in range(KT):
                        o = k * D + ct * P
                        last = split3(bank[2][:, ct * GT:(ct + 1) * GT], (wq1_hi[:, o:o + P], wq1_lo[:, o:o + P]),
                                      xT("C", k), k == 0, k == KT - 1)
                last.then_inc(q_psum, 1)

            def ffn(g):
                pe_.wait_ge(xT_lod["B"], g + 1)
                pe_.wait_ge(c_lod, g + 1)
                pe_.wait_ge(z_lod, g + 1)
                for u in range(2):
                    o = bank[4][:, u * D:(u + 1) * D]
                    for k in range(KT):
                        split3(o, xT("B", k, u), (c_hi[:, k * D:(k + 1) * D], c_lo[:, k * D:(k + 1) * D]), k == 0, False)
                    mm(o, ones_r[:, :], z_lo[:, :], start=False, stop=False, skip_group_check=True)
                    last = mm(o, ones_r[:, :], z_hi[:, :], start=False, stop=True, skip_group_check=True)
                last.then_inc(b_out, 1)

            def round_1a(r):
                if has(r, 0):
                    scores(r)
                if has(r, -1):
                    norm_T("A", r + 1)
                if has(r, 0):
                    fuse(r, 0)
                    fuse(r, 1)
                if has(r, 1):
                    norm_T("B", r - 1)
                if has(r, 0):
                    probs_T(r)
                    fuse(r, 2)
                if has(r, 1):
                    if is_tail(r):
                        norm_T("C", 0)
                    ffn(r - 1)
                    if is_tail(r):
                        query(0)
                if has(r, 0):
                    fuse(r, 3)
                    attend(r)

            pe_.wait_ge(pro_dve, 19)
            pe_.wait_ge(pro_act, 17)
            loop(pe_, round_1a, -1, 2, GROUPS - 2, GROUPS + 1)

            def sig_scores(g, j):
                if j == 0:
                    pe_.wait_ge(k1_in, (g // 4 + 1) * 128)
                    pe_.wait_ge(q_lod, g + 1)
                if later(4 * g + j, 2):
                    pe_.wait_ge(s_sig, 4 * g + j - 1)
                ct = j // 2
                for i in range(2):
                    m = 2 * j + i
                    last = split3(bank[3 + j % 2][:, i * GT:(i + 1) * GT], (kw_hi[:, m * P:(m + 1) * P], kw_lo[:, m * P:(m + 1) * P]),
                                  (q_hi[:, ct * GT:(ct + 1) * GT], q_lo[:, ct * GT:(ct + 1) * GT]), True, True)
                last.then_inc(s_psum, 1)

            def sig_values(g, j):
                pe_.wait_ge(s_lod[j % 2], 2 * g + j // 2 + 1)
                if j == 0:
                    pe_.wait_ge(v1_in, (g // 4 + 1) * 128)
                    if later(g):
                        pe_.wait_ge(o_lod, g)
                ct = j // 2
                for i in range(2):
                    m = 2 * j + i
                    last = split3(bank[5][:, ct * GT:(ct + 1) * GT], (vw1_hi[:, m * P:(m + 1) * P], vw1_lo[:, m * P:(m + 1) * P]),
                                  (sig_hi[j][:, i * GT:(i + 1) * GT], sig_lo[j][:, i * GT:(i + 1) * GT]),
                                  j % 2 == 0 and i == 0, j % 2 == 1 and i == 1)
                last.then_inc(o_part, 1)

            def project(g):
                pe_.wait_ge(o_lod, g + 1)
                for u in range(2):
                    for ct in range(KT):
                        o = ct * GT + u * P
                        last = split3(bank[2][:, u * D:(u + 1) * D], (o_hi[:, o:o + P], o_lo[:, o:o + P]),
                                      (wo1_hi[:, ct * D:(ct + 1) * D], wo1_lo[:, ct * D:(ct + 1) * D]), ct == 0, ct == KT - 1)
                last.then_inc(c_out, 1)

            def logit(g, i):
                u, half = i // 2, i % 2
                if i == 0:
                    pe_.wait_ge(xT_lod["D"], g + 1)
                if later(4 * g + i, 2):
                    pe_.wait_ge(l_sb, 4 * g + i - 1)
                for k in range(KT):
                    o = k * SLOTS + half * 512
                    last = split3(bank[6 + half][:, :], xT("D", k, u), (se_hi[:, o:o + 512], se_lo[:, o:o + 512]),
                                  k == 0, k == KT - 1)
                last.then_inc(l_psum, 1)

            def columns_T(b):
                pe_.wait_ge(colmax_done, SM * (b + 1) + 1)
                if b == 0:
                    pe_.wait_ge(s_sig, 4 * GROUPS)
                for m in range(SM):
                    last = nc.tensor.transpose(bank[cmT_bank[b][m // 4]][:, (m % 4) * P:(m % 4 + 1) * P],
                                               colmax[:, b * SLOTS + m * P:b * SLOTS + (m + 1) * P], ident[:, :])
                    if m % 4 == 3:
                        last.then_inc(cmT, 1)

            def spread(b):
                if b == 1:
                    pe_.wait_ge(l_sb, 4 * GROUPS)
                pe_.wait_ge(cm_diag, b + 1)
                for i in range(2):
                    mm(bank[spread_bank[b][i]][:, :], ones[:, :], diag[b][:, i * 512:(i + 1) * 512], start=True, stop=True).then_inc(cm_bc, 1)

            def round_1b(r):
                if is_tail(r, 8):
                    columns_T(0)
                if has(r, 0):
                    sig_scores(r, 0)
                    sig_scores(r, 1)
                if has(r, 1):
                    project(r - 1)
                if has(r, 2):
                    logit(r - 2, 0)
                if has(r, 0):
                    sig_scores(r, 2)
                    sig_values(r, 0)
                    sig_scores(r, 3)
                if has(r, -1):
                    norm_T("C", r + 1)
                if has(r, 0):
                    sig_values(r, 1)
                if has(r, 2):
                    logit(r - 2, 1)
                if is_tail(r, 8):
                    spread(0)
                if has(r, -1):
                    query(r + 1)
                if has(r, 0):
                    sig_values(r, 2)
                if has(r, 1) and not is_tail(r, 8):
                    norm_T("D", r - 1)
                if has(r, 2):
                    logit(r - 2, 2)
                if has(r, 0):
                    sig_values(r, 3)
                if is_tail(r, 8):
                    norm_T("D", r - 1)
                if has(r, 2):
                    logit(r - 2, 3)

            pe_.wait_ge(pro_dve, 20)
            loop(pe_, round_1b, 0, 3, GROUPS - 1, GROUPS + 2)

            def dispatch(n, s):
                b = n // SM
                pe_.wait_ge(d_lo, n + 1)
                if later(n, 2):
                    pe_.wait_ge(sl_norm, n - 1)
                for t in range(SM):
                    last = split3(bank[s % 2][:, 0:XW], (e_hi[s][:, t * P:(t + 1) * P], e_lo[s][:, t * P:(t + 1) * P]),
                                  pair(xn_hi, xn_lo, b * (SM * XW) + t * XW, XW), t == 0, t == SM - 1)
                last.then_inc(sl_psum, 1)

            def slots_T(n, s):
                pe_.wait_ge(sl_norm, n + 1)
                if later(n, 2):
                    pe_.wait_ge(slT_lod, n - 1)
                for k in range(KT):
                    last = nc.tensor.transpose(bank[2 + s % 2][:, k * P:(k + 1) * P], sf[s % 2][:, k * P:(k + 1) * P], ident[:, :])
                last.then_inc(slT_psum, 1)

            def step_2(n, s):
                if has(n, 0, 16):
                    dispatch(n, s)
                if has(n, 1, 16):
                    slots_T(n - 1, (s + 3) % 4)
                if is_tail(n, 1):
                    columns_T(1)
                if is_tail(n, 3):
                    spread(1)

            pe_.wait_ge(xn_lod, GROUPS)
            dispatch_steps(pe_, step_2, 0, 17)

            def hidden(c, j):
                if later(4 * c + j, 2):
                    pe_.wait_ge(g_act, 4 * c + j - 1)
                for i in range(2):
                    for k in range(KT):
                        o = k * INTER + (2 * j + i) * P
                        rhs = [cols(t, c * (4 * P), 4 * P).rearrange("p (m k s) -> p k m s", m=2, k=KT)[:, k] for t in (slT_hi, slT_lo)]
                        last = split3(bank[4 + j % 2][:, i * GT:(i + 1) * GT], (w1_hi[:, o:o + P], w1_lo[:, o:o + P]), rhs,
                                      k == 0, k == KT - 1)
                last.then_inc(h_psum, 1)

            def expert(c, j):
                pe_.wait_ge(g_lo, 4 * c + j + 1)
                if j == 0 and later(c):
                    pe_.wait_ge(pr_lo, c)
                for u in range(2):
                    for i in range(2):
                        o = (2 * j + i) * D
                        last = split3(bank[6][:, u * D:(u + 1) * D],
                                      (h_hi[j][:, i * GT + u * P:i * GT + (u + 1) * P], h_lo[j][:, i * GT + u * P:i * GT + (u + 1) * P]),
                                      (w2_hi[:, o:o + D], w2_lo[:, o:o + D]), j == 0 and u == 0 and i == 0, j == 3 and u == 1 and i == 1)
                last.then_inc(p_part, 1)

            def chunk(c):
                hidden(c, 0)
                if has(c, 1):
                    expert(c - 1, 3)
                for j in range(1, 4):
                    hidden(c, j)
                    expert(c, j - 1)

            pe_.wait_ge(ew_lo, 8)
            pe_.wait_ge(slT_lod, 16)
            loop(pe_, chunk, 0, 1, GROUPS, GROUPS)
            expert(GROUPS - 1, 3)

            def comb_T(t, s):
                pe_.wait_ge(e2_act, t + 1)
                if later(t, 2):
                    pe_.wait_ge(e2_lo, 2 * t - 2)
                for m in range(SM):
                    last = nc.tensor.transpose(bank[2 * s + m // 4][:, (m % 4) * P:(m % 4 + 1) * P],
                                               ef[s][:, m * P:(m + 1) * P], ident[:, :])
                    if m % 4 == 3:
                        last.then_inc(e2_psum, 1)

            def combine(t, s):
                b = t // SM
                pe_.wait_ge(e2_lo, 2 * t + 2)
                if later(t, 2):
                    pe_.wait_ge(y_ready, t - 1)
                for m in range(SM):
                    last = split3(bank[4 + s][:, 0:XW], (e2T_hi[s][:, m * P:(m + 1) * P], e2T_lo[s][:, m * P:(m + 1) * P]),
                                  pair(xn_hi, xn_lo, b * (SM * XW) + m * XW, XW), m == 0, m == SM - 1)
                last.then_inc(y_psum, 1)

            def step_4(t, s):
                if has(t, -1, TILES):
                    comb_T(t + 1, 1 - s)
                if has(t, 0, TILES):
                    combine(t, s)

            step_4(-1, 1)
            pe_.wait_ge(pr_lo, GROUPS)
            for t in range(2):
                step_4(t, t % 2)
            with pe_.Fori(2, 13, 2) as t:
                for s in range(2):
                    step_4(t + s, s)
            for t in range(14, 16):
                step_4(t, t % 2)


def position_table():
    pos = np.arange(75, dtype=np.float32)[:, None]
    denom = np.power(np.float32(10000.0), np.float32(2.0) * np.arange(D // 2, dtype=np.float32) / np.float32(D)).astype(np.float32)
    ang = (pos / denom).astype(np.float32)
    pe = np.zeros((75, D), np.float32)
    pe[:, 0::2] = np.sin(ang)
    pe[:, 1::2] = np.cos(ang)
    return pe[:KEYS].T


def kernel(**inputs):
    import concourse.bacc as bacc
    from concourse.bass_utils import run_bass_kernel_spmd

    a = {k: np.asarray(v) for k, v in inputs.items()}
    c = np.ascontiguousarray

    def ktiles(m):
        return c(m.reshape(-1, P, m.shape[1]).transpose(1, 0, 2).reshape(P, -1))

    ctxT = a["ctx_1024"].transpose(2, 0, 1)
    ctx2 = np.broadcast_to(ctxT.reshape(KT, P, BATCH, 1, KEYS).transpose(1, 0, 2, 3, 4), (P, KT, BATCH, 2, KEYS))
    p = np.arange(P)
    mask_k = np.repeat((p[:, None] % 32 // DH1 == np.arange(2)[None, :]), KEYS, axis=1).astype(np.float32)
    mask_v = (np.arange(32)[None, :] // DH1 == p[:, None] // KEYS).astype(np.float32)
    arrays = {
        "x": c(a["x"].reshape(TOKENS, D)),
        "ctx2": c(ctx2.reshape(P, -1)),
        "pe": ktiles(position_table()),
        "wq0T": c(a["L0_xattn_Wq"].T), "wk0": a["L0_xattn_Wk"], "wv0": a["L0_xattn_Wv"], "wo0": a["L0_xattn_Wo"],
        "bo": a["L0_xattn_bo"].reshape(1, D),
        "fw1": c(a["L0_ffn_W1"].reshape(GROUPS, P, OC * D)),
        "fb1": c(a["L0_ffn_b1"].reshape(GROUPS, P, OC)),
        "fw2T": c(a["L0_ffn_W2"].transpose(0, 2, 1).reshape(GROUPS, P, OC * D)),
        "fb2": a["L0_ffn_b2"],
        "wq1T": c(a["L1_xattn_Wq"].T), "wk1T": c(a["L1_xattn_Wk"].T), "wv1T": c(a["L1_xattn_Wv"].T), "wo1T": c(a["L1_xattn_Wo"].T),
        "gx": c(a["L1_ffn_gamma_x"].reshape(KT, P).T), "gs": c(a["L1_ffn_gamma_slot"].reshape(KT, P).T),
        "slot": a["L1_ffn_slot_embeds"].reshape(SLOTS, D), "w1": a["L1_ffn_w1"], "w2": a["L1_ffn_w2"],
        "ident_in": np.eye(P, dtype=np.float32), "mask_k": mask_k, "mask_v": mask_v,
    }
    nc = bacc.Bacc("TRN2", target_bir_lowering=False, num_devices=1, dynamic_dma_scratch_size=1024)
    args = {n: nc.dram_tensor(f"in_{n}", v.shape, F32, kind="ExternalInput").ap() for n, v in arrays.items()}
    outp = nc.dram_tensor("out_0", (TOKENS, D), F32, kind="ExternalOutput").ap()
    build(nc, out=outp, **args)
    r = run_bass_kernel_spmd(nc, [{f"in_{n}": c(v) for n, v in arrays.items()}], core_ids=[0])
    return np.asarray(r.results[0]["out_0"]).reshape(BATCH, SEQ, D)
```

```python
import numpy as np
import concourse.bass as bass
from concourse import mybir
from contextlib import ExitStack

F32 = mybir.dt.float32
F32R = mybir.dt.float32r
ALU = mybir.AluOpType
ACT = mybir.ActivationFunctionType
AXX = mybir.AxisListType.X

P = 128
BATCH, SEQ, D = 2, 1024, 256
TOKENS = BATCH * SEQ
TILES = TOKENS // P
GROUPS = 8
GT = TOKENS // GROUPS
KT = D // P
KEYS = 64
H0, DH0 = 8, 64
WK = KEYS // 4
H1, DH1 = 16, 16
PAIRS = H1 // 2
INTER = 1024
OC = INTER // P
SLOTS = 1024
SM = SLOTS // P
XW = D + 2
VW = 4 * (P + 32)
LN_EPS, NORM_EPS = 1e-5, 1e-12
WPARTS = 4
LOWEST = -3.0e38


def build(nc, x, ctx2, pe, wq0T, wk0, wv0, wo0, bo, fw1, fb1, fw2T, fb2, wq1T, wk1T, wv1T, wo1T,
          gx, gs, slot, w1, w2, ident_in, mask_k, mask_v, out):
    es = ExitStack()
    with es:
        base = 1152
        KB = 1024

        def place(name, cols, kb, dt=F32):
            return nc.alloc_sbuf_tensor_at(name, [P, cols], dt, offset=base + int(kb * KB))

        def sem(name):
            return es.enter_context(nc.semaphore(name))

        xs = place("xs", TILES * D, 0)
        ident = place("ident", P, 16)
        ones = place("ones", P, 16.5)
        ones_r = place("ones_r", P, 17, F32R)
        small = place("small", 256, 17.5)
        se_hi = place("se_hi", KT * SLOTS, 19, F32R)
        se_lo = place("se_lo", KT * SLOTS, 27, F32R)
        wq1_hi = place("wq1_hi", KT * D, 35, F32R)
        wq1_lo = place("wq1_lo", KT * D, 37, F32R)
        wq1_f = place("wq1_f", KT * D, 37)
        wo1_hi = place("wo1_hi", KT * D, 39, F32R)
        wo1_lo = place("wo1_lo", KT * D, 41, F32R)
        wo1_f = place("wo1_f", KT * D, 41)
        kc_hi = place("kc_hi", BATCH * KT * P, 43, F32R)
        kc_lo = place("kc_lo", BATCH * KT * P, 45, F32R)
        kc_f = place("kc_f", BATCH * KT * P, 45)
        vc_hi = place("vc_hi", BATCH * PAIRS * 32, 47, F32R)
        vc_lo = place("vc_lo", BATCH * PAIRS * 32, 49, F32R)
        vc_f = place("vc_f", BATCH * PAIRS * 32, 49)
        a_hi = place("a_hi", GROUPS * KT * P, 51, F32R)
        a_lo = place("a_lo", GROUPS * KT * P, 59, F32R)
        vw_hi = place("vw_hi", GROUPS * D, 67, F32R)
        vw_lo = place("vw_lo", GROUPS * D, 75, F32R)
        vw_f = place("vw_f", GROUPS * D, 75)
        w1r = place("w1r", OC * D, 83)
        w2r = place("w2r", OC * D, 91)
        c_hi = place("c_hi", KT * D, 99, F32R)
        c_lo = place("c_lo", KT * D, 101, F32R)
        z0 = place("z0", D, 103)
        z = place("z", D, 104)
        z_hi = place("z_hi", D, 105, F32R)
        z_lo = place("z_lo", D, 106, F32R)
        b1t = place("b1t", OC, 107)
        prod = place("prod", OC * D, 139.5)
        probs = place("probs", 2 * P, 108)
        pT_hi = place("pT_hi", 2 * P, 109, F32R)
        pT_lo = place("pT_lo", 2 * P, 110, F32R)
        vwt = place("vwt", H0 * D, 123)
        wk0s = place("wk0s", KT * 512, 176)
        wv0s = place("wv0s", KT * 512, 180)
        wq0s = place("wq0s", 4 * D, 184)
        wo0s = place("wo0s", 4 * D, 188)
        kT0 = place("kT0", 512, 192)
        vT0 = place("vT0", 512, 194)
        ctx_s = place("ctx_s", KT * BATCH * P, 196)
        hcT = place("hcT", KT * P, 198)
        pe_s = place("pe_s", KT * KEYS, 199)
        mk_s = place("mk_s", P, 199.5)
        mv_s = place("mv_s", 32, 200)
        bo_s = place("bo_s", D, 201)
        wk1s = place("wk1s", KT * D, 202)
        wv1s = place("wv1s", KT * D, 204)
        slot_s = place("slot_s", SM * D, 131)
        sq = place("sq", SM * D, 164)
        xn_hi = place("xn_hi", TILES * XW, 51, F32R)
        xn_lo = place("xn_lo", TILES * XW, 67.125, F32R)
        logits = place("logits", TILES * SLOTS, 84)
        kw_hi = place("kw_hi", PAIRS * P, 148, F32R)
        kw_lo = place("kw_lo", PAIRS * P, 152, F32R)
        vw1_hi = place("vw1_hi", KT * VW, 156, F32R)
        vw1_lo = place("vw1_lo", KT * VW, 212, F32R)
        q_hi = place("q_hi", KT * GT, 176, F32R)
        q_lo = place("q_lo", KT * GT, 178, F32R)
        o_hi = place("o_hi", KT * GT, 180, F32R)
        o_lo = place("o_lo", KT * GT, 170, F32R)
        sig = [place(f"sig{i}", 2 * GT, 172 + 2 * i) for i in range(2)]
        sig_hi = [place(f"sig_hi{i}", 2 * GT, (188, 190, 204, 206)[i], F32R) for i in range(4)]
        sig_lo = [place(f"sig_lo{i}", 2 * GT, (192, 194, 208, 210)[i], F32R) for i in range(4)]
        colmax = place("colmax", BATCH * SLOTS, 196)
        lnx, xT_hi, xT_lo = {}, {}, {}
        for ch, kb in zip("ABCD", (111, 117, 164, 182)):
            lnx[ch] = place(f"ln{ch}", 2 * D, kb)
            xT_hi[ch] = place(f"xT_hi{ch}", KT * GT, kb + 2, F32R)
            xT_lo[ch] = place(f"xT_lo{ch}", KT * GT, kb + 4, F32R)
        w1_hi = place("w1_hi", KT * INTER, 19, F32R)
        w1_lo = place("w1_lo", KT * INTER, 27, F32R)
        w1_f = place("w1_f", KT * INTER, 27)
        w2_hi = place("w2_hi", OC * D, 35, F32R)
        w2_lo = place("w2_lo", OC * D, 43, F32R)
        w2_f = place("w2_f", OC * D, 43)
        cmb = place("cmb", BATCH * SLOTS, 148)
        diag = [place(f"diag{b}", SLOTS, (218, 184)[b]) for b in range(BATCH)]
        e_hi = [place(f"e_hi{i}", SLOTS, 156 + 4 * i, F32R) for i in range(4)]
        e_lo = [place(f"e_lo{i}", SLOTS, 206 + 4 * i, F32R) for i in range(4)]
        ef = [place(f"ef{i}", SLOTS, 206 + 4 * i) for i in range(4)]
        slT_hi = place("slT_hi", KT * BATCH * SLOTS, 172, F32R)
        slT_lo = place("slT_lo", KT * BATCH * SLOTS, 188, F32R)
        sf = [place(f"sf{i}", D, 204 + i) for i in range(2)]
        hf = [place(f"hf{i}", 2 * GT, 148 + 2 * i) for i in range(2)]
        h_hi = [place(f"h_hi{i}", 2 * GT, 152 + 4 * i, F32R) for i in range(4)]
        h_lo = [place(f"h_lo{i}", 2 * GT, 154 + 4 * i, F32R) for i in range(4)]
        e2T_hi = [place(f"e2T_hi{i}", SLOTS, 156 + 8 * i, F32R) for i in range(2)]
        e2T_lo = [place(f"e2T_lo{i}", SLOTS, 160 + 8 * i, F32R) for i in range(2)]
        y = [place(f"y{i}", D, 172 + i) for i in range(2)]

        cmT_bank = ((0, 2), (4, 5))
        spread_bank = ((0, 3), (6, 7))
        vw_bank = (6, 7, 1, 2)

        sc = {}
        at = 0
        for name, n in [("bnA", 12), ("bnB", 12), ("bnC", 12), ("bnD", 12), ("mvA", 4), ("mvB", 4),
                        ("mvC", 4), ("mvD", 4), ("veA", 2), ("veB", 2), ("veC", 2), ("veD", 2),
                        ("rsA", 2), ("rsB", 2), ("rsC", 2), ("rsD", 2), ("t1", 2), ("t2", 2), ("t3", 2),
                        ("rstd", 2), ("eps", 2), ("mhalf", 8), ("mx", 16), ("sm", 16), ("rc", 16),
                        ("rowmax", 16), ("nrow", 16), ("cm", 16), ("ss", 8), ("rss", 8), ("gxs", 2),
                        ("gss", 2), ("gg", 2), ("rec", 2), ("rec4", 2), ("warm", 3)]:
            sc[name] = small[:, at:at + n]
            at += n
        assert at <= 256

        bank = [es.enter_context(nc.psum_tensor(f"bank{i}", [P, 512], F32)) for i in range(8)]
        vw_dram = nc.dram_tensor("vw_bounce", [P, H0 * D], F32).ap()

        in_x0, in_x1, in_x, in_qo, in_ctx, in_k0, in_v0, in_q0, in_o0, in_l1, in_slot, in_g, in_id = (
            sem(n) for n in ("in_x0", "in_x1", "in_x", "in_qo", "in_ctx", "in_k0", "in_v0", "in_q0", "in_o0", "in_l1", "in_slot", "in_g", "in_id"))
        in_w = [sem(f"in_w{k}") for k in range(WPARTS)]
        in_b, vw_out, vw_in, k1_in = (sem(n) for n in ("in_b", "vw_out", "vw_in", "k1_in"))
        v1_in = sem("v1_in")
        in_ew = [sem("in_ew1"), sem("in_ew2")]
        out_done = [sem(f"out_done{i}") for i in range(2)]
        (consts, ones_done, hc_ready, kv0_psum, kT0_done, v0_steps, a_psum, a_hid, a_lod, vw_psum, vwt_done,
         vw_hid, vw_lod, l1_psum, kvc_made, kvc_hid, kvc_lod, wqo_hid, wqo_lod) = (sem(n) for n in (
             "consts", "ones_done", "hc_ready", "kv0_psum", "kT0_done", "v0_steps", "a_psum", "a_hi_done",
             "a_lo_done", "vw_psum", "vwt_done", "vw_hi_done", "vw_lo_done", "l1_psum", "kvc_made",
             "kvc_hi_done", "kvc_lo_done", "wqo_hi_done", "wqo_lo_done"))
        slot_rs, slot_ready, gg_ready, se_psum, se_hid, se_lod = (sem(n) for n in (
            "slot_rs", "slot_ready", "gg_ready", "se_psum", "se_hi_done", "se_lo_done"))
        tick, c_centred = sem("tick"), sem("c_centred")
        bn_done, st_ready, rs_step, rs_ready, ln_ready, xT_psum, xT_hid, xT_lod = ({} for _ in range(8))
        for ch in "ABCD":
            bn_done[ch] = sem(f"bn_done{ch}")
            st_ready[ch] = sem(f"st_ready{ch}")
            rs_step[ch] = sem(f"rs_step{ch}")
            rs_ready[ch] = sem(f"rs_ready{ch}")
            ln_ready[ch] = sem(f"ln_ready{ch}")
            xT_psum[ch] = sem(f"xT_psum{ch}")
            xT_hid[ch] = sem(f"xT_hi_done{ch}")
            xT_lod[ch] = sem(f"xT_lo_done{ch}")
        x_ready = {"B": sem("x1_ready"), "C": sem("x2_ready"), "D": sem("x3_ready")}
        (sc_psum, sm_step, e_in, e_out, p_ready, pT_psum, pT_hid, pT_lod, a_out, w_used, c_hid, c_lod, z_prod, z_step,
         z_hid, z_lod, b_out) = (sem(n) for n in (
             "sc_psum", "sm_step", "e_in", "e_out", "p_ready", "pT_psum", "pT_hi_done", "pT_lo_done", "a_out",
             "w_used", "c_hi_done", "c_lo_done", "z_prod", "z_step", "z_hi_done", "z_lo_done", "b_out"))
        (q_psum, q_hid, q_lod, s_psum, s_sig, s_hid, o_part, o_hid, o_lod, c_out, l_psum, l_sb, rowmax_done,
         colmax_done, xn_hid, xn_lod) = (sem(n) for n in (
             "q_psum", "q_hi_done", "q_lo_done", "s_psum", "s_sig", "s_hi_done", "o_part", "o_hi_done",
             "o_lo_done", "c_out", "l_psum", "l_sb", "rowmax_done", "colmax_done", "xn_hi_done", "xn_lo_done"))
        w1_hid, w2_lod = sem("w1_hi_done"), sem("w2_lo_done")
        s_lod = [sem("s_lo_even"), sem("s_lo_odd")]
        cmT, cm_red, cm_diag, cm_bc, cm_sb = (sem(n) for n in ("cmT", "cm_red", "cm_diag", "cm_bc", "cm_sb"))
        (d_sub, d_exp, d_hi, d_lo, sl_psum, sl_rec, sl_norm, slT_psum, slT_hid, slT_lod) = (sem(n) for n in (
            "d_sub", "d_exp", "d_hi", "d_lo", "sl_psum", "sl_rec", "sl_norm", "slT_psum", "slT_hi_done", "slT_lo_done"))
        (w2_hid, w1_lod, h_psum, g_act, g_hi, g_lo, p_part, pr_hi, pr_lo) = (sem(n) for n in (
            "w2_hi_done", "w1_lo_done", "h_psum", "g_act", "g_hi", "g_lo", "p_part", "pr_hi", "pr_lo"))
        (nrow_done, e2_act, e2_psum, e2_hi, e2_lo, y_psum, y_rec, y_ready) = (sem(n) for n in (
            "nrow_done", "e2_act", "e2_psum", "e2_hi", "e2_lo", "y_psum", "y_rec", "y_ready"))

        def cols(t, start, n):
            return t[:, start:start + n] if isinstance(start, int) else t[:, bass.ds(start, n)]

        def xg(g):
            return cols(xs, g * (2 * D), 2 * D)

        def f(ap):
            return ap.bitcast(F32)

        def split3(outp, lhs, rhs, start, stop):
            nc.tensor.matmul(outp, lhs[0], rhs[1], start=start, stop=False, skip_group_check=True)
            nc.tensor.matmul(outp, lhs[1], rhs[0], start=False, stop=False, skip_group_check=True)
            return nc.tensor.matmul(outp, lhs[0], rhs[0], start=False, stop=stop, skip_group_check=True)

        def later(v, least=1):
            return not isinstance(v, int) or v >= least

        def loop(eng, body, first, lo, hi, end):
            for r in range(first, lo):
                body(r)
            with eng.Fori(lo, hi) as r:
                body(r)
            for r in range(hi, end):
                body(r)

        def has(r, shift, n=GROUPS):
            return not isinstance(r, int) or 0 <= r - shift < n

        def is_tail(r, n=GROUPS):
            return isinstance(r, int) and r == n

        def slot_quarter(r, half):
            return {(6, 0): 0, (6, 1): 1, (7, 0): 2, (7, 1): 3}.get((r, half)) if isinstance(r, int) else None

        def w1_piece(i):
            k, half = i % 2, i // 2
            return slice(k * INTER + half * 512, k * INTER + half * 512 + 512), sc["gxs"][:, k:k + 1]

        def xT_place(ch, g):
            return "C" if ch == "D" and is_tail(g, GROUPS - 1) else ch

        def dispatch_steps(eng, body, first, end):
            for n in range(first, 4):
                body(n, n % 4)
            with eng.Fori(4, 11, 4) as n:
                for s in range(4):
                    body(n + s, s)
            for n in range(12, end):
                body(n, n % 4)

        def logits_view(b, m):
            v4 = logits[:, :].rearrange("p (b t n) -> p b t n", b=BATCH, t=SM)
            if isinstance(b, int):
                return v4[:, b, :, m * P:(m + 1) * P]
            return v4[:, bass.ds(b, 1), :, bass.ds(m * P, P)].rearrange("p b t n -> p (b t) n")

        def held(eng, s, v):
            eng.wait_ge(s, v)
            if not isinstance(v, int):
                eng.sem_inc(tick, 1)

        block = es.enter_context(nc.Block())

        @block.sync
        def _(sp):
            def load_w(g, k):
                part = slice(2 * k * D, 2 * (k + 1) * D)
                if later(g):
                    held(sp, w_used, 4 * g - 3 + k)
                    held(sp, z_prod, OC * (g - 1) + 2 * k + 2)
                for dst, src in ((w1r, fw1), (w2r, fw2T)):
                    s = src[g, :, part] if isinstance(g, int) else src[bass.ds(g, 1), :, part].rearrange("a p n -> (a p) n")
                    sp.dma_start(dst[:, part], s).then_inc(in_w[k], 16)

            def load_b(g):
                if later(g):
                    held(sp, z_step, 4 * g)
                s1 = fb1[g, :, :] if isinstance(g, int) else fb1[bass.ds(g, 1), :, :].rearrange("a p n -> (a p) n")
                s2 = fb2[g:g + 1, :] if isinstance(g, int) else fb2[bass.ds(g, 1), :]
                sp.dma_start(b1t[:, :], s1).then_inc(in_b, 16)
                sp.dma_start(z0[0:1, :], s2).then_inc(in_b, 16)

            xv = x.rearrange("(t p) d -> p t d", p=P)
            xsv = xs[:, :].rearrange("p (t d) -> p t d", d=D)
            sp.dma_start(pe_s[:, :], pe).then_inc(in_ctx, 16)
            sp.dma_start(wk0s[:, :].rearrange("p (k n) -> p k n", k=KT), wk0.rearrange("(k p) n -> p k n", p=P)).then_inc(in_k0, 16)
            sp.dma_start(xsv[:, 0:2], xv[:, 0:2]).then_inc(in_x0, 16)
            sp.dma_start(wq0s[:, :].rearrange("p (k n) -> p k n", k=4), wq0T.rearrange("(k p) n -> p k n", p=P)).then_inc(in_q0, 16)
            sp.dma_start(ident[:, :], ident_in).then_inc(in_id, 16)
            sp.dma_start(xsv[:, 2:4], xv[:, 2:4]).then_inc(in_x1, 16)
            for k in range(WPARTS):
                load_w(0, k)
            sp.wait_ge(consts, 4)
            load_b(0)
            sp.dma_start(xsv[:, 4:], xv[:, 4:]).then_inc(in_x, 16)
            sp.dma_start(sc["gxs"], gx).then_inc(in_g, 16)
            sp.dma_start(sc["gss"], gs).then_inc(in_g, 16)
            for dst, src in ((wk1s, wk1T), (wv1s, wv1T)):
                sp.dma_start(dst[:, :].rearrange("p (k n) -> p k n", k=KT), src.rearrange("(k p) n -> p k n", p=P)).then_inc(in_l1, 16)
            sp.dma_start(mk_s[:, :], mask_k).then_inc(in_l1, 16)
            sp.dma_start(mv_s[:, :], mask_v).then_inc(in_l1, 16)
            sp.wait_ge(vwt_done, 4)
            sp.dma_start(vw_dram, vwt[:, :]).then_inc(vw_out, 16)
            load_w(1, 0)
            sp.wait_ge(vw_out, 16)
            for h in range(H0):
                sp.dma_start(vw_f[WK * h:WK * (h + 1), :].rearrange("j (g n) -> j g n", g=GROUPS),
                             vw_dram[:, h * D:(h + 1) * D].rearrange("(g j) n -> j g n", g=GROUPS)).then_inc(vw_in, 16)

            sp.dma_start(slot_s[:, :].rearrange("p (m n) -> p m n", m=SM), slot.rearrange("(m p) n -> p m n", p=P)).then_inc(in_slot, 16)
            for dst, src in ((wq1_f, wq1T), (wo1_f, wo1T)):
                sp.dma_start(dst[:, :].rearrange("p (k n) -> p k n", k=KT), src.rearrange("(k p) n -> p k n", p=P)).then_inc(in_qo, 16)

            def load_k1(b, parts=(0, 1)):
                for dst, src in [((kw_hi, kc_hi), (kw_lo, kc_lo))[part] for part in parts]:
                    d4 = f(dst[:, :]).rearrange("p (c i n) -> p c i n", c=KT, i=4)
                    s3 = f(src[:, b * KT * P:(b + 1) * KT * P]).rearrange("p (c n) -> p c n", c=KT)
                    for i in range(4):
                        sp.dma_start(d4[32 * i:32 * i + 32, :, i, :], s3[32 * i:32 * i + 32, :, :]).then_inc(k1_in, 16)

            def load_v1(b):
                for dst, src in ((vw1_hi, vc_hi), (vw1_lo, vc_lo)):
                    for c in range(KT):
                        o = (b * KT + c) * (4 * 32)
                        sp.dma_start(f(dst[:, c * VW:(c + 1) * VW]).rearrange("p (i n) -> p i n", i=4)[:, :, 0:32],
                                     f(src[:, o:o + 4 * 32]).rearrange("p (i n) -> p i n", i=4)).then_inc(v1_in, 16)

            for k in range(1, WPARTS):
                load_w(1, k)
            load_b(1)
            with sp.Fori(2, GROUPS - 1) as g:
                for k in range(WPARTS):
                    load_w(g, k)
                load_b(g)
            load_w(GROUPS - 1, 0)
            sp.wait_ge(consts, 6)
            sp.wait_ge(kvc_hid, 2)
            sp.wait_ge(kvc_lod, 2)
            load_k1(0, (0,))
            load_w(GROUPS - 1, 1)
            load_k1(0, (1,))
            load_w(GROUPS - 1, 2)
            load_w(GROUPS - 1, 3)
            load_b(GROUPS - 1)
            load_v1(0)
            sp.wait_ge(s_psum, 4 * (GROUPS // 2))
            load_k1(1)
            sp.wait_ge(o_part, 4 * (GROUPS // 2))
            load_v1(1)
            sp.wait_ge(c_out, GROUPS)
            sp.dma_start(w2_f[:, :].rearrange("p (c n) -> p c n", c=OC), w2.rearrange("(c p) n -> p c n", p=P)).then_inc(in_ew[1], 16)
            sp.wait_ge(l_psum, 4 * GROUPS)
            sp.dma_start(w1_f[:, :].rearrange("p (k n) -> p k n", k=KT), w1.rearrange("(k p) n -> p k n", p=P)).then_inc(in_ew[0], 16)

            ov = out.rearrange("(t p) d -> t p d", p=P)
            with sp.Fori(0, TILES - 1, 2) as t:
                for s in range(2):
                    held(sp, y_ready, t + s + 1)
                    sp.dma_start(ov[bass.ds(t + s, 1), :, :].rearrange("a p d -> (a p) d"), y[s][:, :]).then_inc(out_done[s], 16)
            for s in range(2):
                sp.wait_ge(out_done[s], 16 * (TILES // 2))

        @block.gpsimd
        def _(pool):
            g_ = nc.gpsimd

            def await_(s, v):
                held(pool, s, v)

            g_.memset(ones[:, :], 1.0).then_inc(consts, 1)
            g_.memset(sc["eps"], LN_EPS).then_inc(consts, 1)
            g_.memset(sc["mhalf"], -0.5).then_inc(consts, 1)
            g_.memset(z0[:, :], 0.0).then_inc(consts, 1)
            for t in (kw_hi, kw_lo, vw1_hi, vw1_lo):
                last = g_.memset(f(t[:, :]), 0.0)
            last.then_inc(consts, 2)
            pool.wait_ge(consts, 6)

            def rstd(ch, g):
                await_(st_ready[ch], 2 * g + 2)
                n = 1 if ch != "D" else 6
                step = [0]

                def own(ins):
                    step[0] += 1
                    ins.then_inc(rs_step[ch], 1)
                    await_(rs_step[ch], n * g + step[0])

                var = sc["mv" + ch][:, 1:4:2]
                own(g_.tensor_tensor(sc["ve" + ch], var, sc["eps"], ALU.add))
                if ch != "D":
                    g_.tensor_tensor(sc["rs" + ch], sc["ve" + ch], sc["mhalf"][:, 0:2], ALU.pow).then_inc(rs_ready[ch], 1)
                    return
                own(g_.tensor_tensor(sc["rstd"], sc["veD"], sc["mhalf"][:, 0:2], ALU.pow))
                own(g_.tensor_tensor(sc["t1"], var, sc["rstd"], ALU.mult))
                own(g_.tensor_tensor(sc["t2"], sc["t1"], sc["rstd"], ALU.mult))
                own(g_.tensor_scalar(sc["t3"], sc["t2"], NORM_EPS ** 2 / D, None, ALU.max))
                own(g_.tensor_tensor(sc["t1"], sc["t3"], sc["mhalf"][:, 0:2], ALU.pow))
                g_.tensor_tensor(sc["rsD"], sc["t1"], sc["rstd"], ALU.mult).then_inc(rs_ready[ch], 1)

            rstd("A", 0)
            rstd("A", 1)
            def slot_scales():
                pool.wait_ge(slot_rs, 1)
                g_.tensor_scalar(sc["ss"], sc["ss"], NORM_EPS ** 2, None, ALU.max).then_inc(slot_rs, 1)
                pool.wait_ge(slot_rs, 2)
                g_.tensor_tensor(sc["rss"], sc["ss"], sc["mhalf"], ALU.pow).then_inc(slot_rs, 1)
                pool.wait_ge(slot_rs, 3)
                g_.tensor_scalar(sc["rss"], sc["rss"], float(D) ** 0.5, None, ALU.mult).then_inc(slot_rs, 1)
                pool.wait_ge(slot_rs, 4)

            def slot_rows(i):
                rows = cols(slot_s, i * (2 * D), 2 * D).rearrange("p (m n) -> p m n", m=2)
                g_.tensor_tensor(rows, rows, cols(sc["rss"], 2 * i, 2).unsqueeze(2).to_broadcast([P, 2, D]), ALU.mult).then_inc(slot_ready, 1)

            def bias(g):
                def own(n, ins):
                    ins.then_inc(z_step, 1)
                    await_(z_step, 4 * g + n)

                await_(z_step, 4 * g + 1)
                own(2, g_.tensor_tensor(prod[:, 0:2 * D], prod[:, 0:2 * D], prod[:, 2 * D:4 * D], ALU.add))
                own(3, g_.tensor_tensor(prod[:, 0:D], prod[:, 0:D], prod[:, D:2 * D], ALU.add))
                if later(g):
                    await_(z_hid, g)
                await_(in_b, 32 * (g + 1))
                g_.tensor_tensor(z[:, :], prod[:, 0:D], z0[:, :], ALU.add).then_inc(z_step, 1)

            def bias_lo(g):
                await_(z_hid, g + 1)
                g_.tensor_tensor(z_lo[:, :], z[:, :], f(z_hi[:, :]), ALU.subtract).then_inc(z_lod, 1)

            def sig_low(g, j):
                await_(s_hid, 4 * g + j + 1)
                g_.tensor_tensor(sig_lo[j][:, :], sig[1][:, :], f(sig_hi[j][:, :]), ALU.subtract).then_inc(s_lod[1], 1)

            def round_1a(r):
                if has(r, 1) and not is_tail(r):
                    rstd("B", r - 1)
                if has(r, 1):
                    bias_lo(r - 1)
                if has(r, -2):
                    rstd("A", r + 2)
                if is_tail(r, GROUPS - 2):
                    rstd("C", 0)
                if is_tail(r, GROUPS - 1):
                    rstd("C", 1)
                    rstd("B", r)
                if is_tail(r, 1):
                    slot_scales()
                if has(r, 2, 4):
                    slot_rows(r - 2)
                if has(r, 0):
                    bias(r)
                if is_tail(r):
                    sig_low(0, 1)

            loop(pool, round_1a, 0, 2, GROUPS - 2, GROUPS + 1)

            pool.wait_ge(b_out, GROUPS)
            g_.memset(colmax[:, :], LOWEST).then_inc(colmax_done, 1)
            for t, v in ((xn_hi, 1.0), (xn_lo, 0.0)):
                g_.memset(f(t[:, :]).rearrange("p (t n) -> p t n", n=XW)[:, :, D:XW], v)

            def xn_low(g):
                await_(xn_hid, g + 1)
                g_.tensor_tensor(cols(xn_lo, g * (2 * XW), 2 * XW).rearrange("p (t n) -> p t n", n=XW)[:, :, 0:D],
                                 lnx["D"][:, :].rearrange("p (t n) -> p t n", n=D),
                                 f(cols(xn_hi, g * (2 * XW), 2 * XW)).rearrange("p (t n) -> p t n", n=XW)[:, :, 0:D],
                                 ALU.subtract).then_inc(xn_lod, 1)

            def normed_c(g):
                await_(rs_ready["C"], g + 1)
                await_(xT_psum["C"], g)
                rows = lnx["C"][:, :].rearrange("p (u n) -> p u n", u=2)
                wide = lambda ap: ap.unsqueeze(2).to_broadcast([P, 2, D])
                g_.tensor_tensor(rows, xg(g).rearrange("p (u n) -> p u n", u=2), wide(sc["mvC"][:, 0:4:2]), ALU.subtract).then_inc(c_centred, 1)
                await_(c_centred, g - 1)
                g_.tensor_tensor(rows, rows, wide(sc["rsC"]), ALU.mult).then_inc(ln_ready["C"], 2)

            def e_sub(n, s):
                b, m = n // SM, n % SM
                await_(cm_sb, 2 * (n // SM) + 2)
                if later(n, 4):
                    await_(sl_psum, n - 3)
                g_.tensor_tensor(ef[s][:, :].rearrange("p (t s) -> p t s", t=SM), logits_view(b, m),
                                 cols(cmb, b * SLOTS + m * P, P).unsqueeze(1).to_broadcast([P, SM, P]), ALU.subtract).then_inc(d_sub, 1)

            def round_1b(r):
                if has(r, -1) and not is_tail(r, 0) and not is_tail(r, 1):
                    rstd("C", r + 1)
                    normed_c(r + 1)
                if has(r, 0) and not is_tail(r, 0):
                    sig_low(r, 1)
                if has(r, 1):
                    rstd("D", r - 1)
                if has(r, 0):
                    sig_low(r, 3)
                if is_tail(r, 0):
                    rstd("C", 2)
                    normed_c(2)
                if is_tail(r, 8):
                    e_sub(0, 0)
                if has(r, 1):
                    xn_low(r - 1)

            loop(pool, round_1b, 0, 3, GROUPS - 1, GROUPS + 1)

            dispatch_steps(pool, e_sub, 1, 16)
            for i in range(4):
                await_(w2_hid, i + 1)
                part = slice(i * 512, (i + 1) * 512)
                g_.tensor_tensor(w2_lo[:, part], w2_f[:, part], f(w2_hi[:, part]), ALU.subtract).then_inc(w2_lod, 1)

        @block.scalar
        def _(act):
            a_ = nc.scalar
            act.dma_start(ctx_s[:, :], ctx2).then_inc(in_ctx, 16)
            act.dma_start(wv0s[:, :].rearrange("p (k n) -> p k n", k=KT), wv0.rearrange("(k p) n -> p k n", p=P)).then_inc(in_v0, 16)
            act.dma_start(wo0s[:, :].rearrange("p (k n) -> p k n", k=4), wo0.rearrange("(k p) n -> p k n", p=P)).then_inc(in_o0, 16)
            act.dma_start(bo_s[:, :], bo.to_broadcast([P, D])).then_inc(in_o0, 16)
            def copy(dst, src, done, n=1):
                a_.activation(dst, src, ACT.Copy).then_inc(done, n)

            def norm_T_hi(ch, g):
                act.wait_ge(xT_psum[ch], g + 1)
                bk = {"A": 0, "B": 7, "C": 0, "D": 1}[ch]
                copy(xT_hi[xT_place(ch, g)][:, :], bank[bk][:, :], xT_hid[ch])

            act.wait_ge(consts, 1)
            copy(ones_r[:, :], ones[:, :], ones_done)
            act.wait_ge(kv0_psum, 1)
            copy(kT0[:, :], bank[0][:, :], kT0_done)
            norm_T_hi("A", 0)
            act.wait_ge(a_psum, 1)
            for k in range(KT):
                for par in range(2):
                    copy(a_hi[:, :].rearrange("p (g k h j) -> p k h g j", g=GROUPS, k=KT, h=H0)[:, k, par::2],
                         bank[2 + 2 * k + par][:, :].rearrange("p (h g j) -> p h g j", h=4, g=GROUPS), a_hid)

            def side_work(r, half):
                if is_tail(r, 1) and half == 1:
                    act.wait_ge(in_qo, 32)
                    copy(wq1_hi[:, :], wq1_f[:, :], wqo_hid)
                    copy(wo1_hi[:, :], wo1_f[:, :], wqo_hid)
                if is_tail(r, 0) and half == 0:
                    act.wait_ge(kvc_made, 2)
                    copy(kc_hi[:, :], kc_f[:, :], kvc_hid)
                if is_tail(r, 0) and half == 1:
                    act.wait_ge(vw_in, 16 * H0)
                    copy(vw_hi[:, 0:D], vw_f[:, 0:D], vw_hid)
                    act.wait_ge(kvc_made, 3)
                    copy(vc_hi[:, :], vc_f[:, :], kvc_hid)
                    copy(vw_hi[:, D:], vw_f[:, D:], vw_hid)
                q = slot_quarter(r, half)
                if q is not None:
                    act.wait_ge(gg_ready, 1)
                    act.wait_ge(se_psum, q + 1)
                    a_.activation(se_hi[:, q * 512:(q + 1) * 512], bank[3][:, :], ACT.Copy,
                                  scale=sc["gg"][:, q // 2:q // 2 + 1]).then_inc(se_hid, 1)

            def bias_product(g, k):
                act.wait_ge(in_w[k], 32 * (g + 1))
                if k == 0:
                    act.wait_ge(in_b, 32 * (g + 1))
                    if later(g):
                        act.wait_ge(z_step, 4 * g)
                for c in (2 * k, 2 * k + 1):
                    a_.activation(prod[:, c * D:(c + 1) * D], w2r[:, c * D:(c + 1) * D], ACT.Copy, scale=b1t[:, c:c + 1]).then_inc(z_prod, 1)

            def query_hi(g):
                act.wait_ge(q_psum, g + 1)
                copy(q_hi[:, :], bank[2][:, :], q_hid)

            def sigmoid(g, j):
                act.wait_ge(s_psum, 4 * g + j + 1)
                if later(4 * g + j, 2):
                    act.wait_ge(s_lod[j % 2], 2 * g + j // 2)
                a_.activation(sig[j % 2][:, :], bank[3 + j % 2][:, :], ACT.Sigmoid, scale=DH1 ** -0.5).then_inc(s_sig, 1)
                act.wait_ge(s_sig, 4 * g + j + 1)
                if later(g):
                    act.wait_ge(o_part, 4 * g + j - 3)
                copy(sig_hi[j][:, :], sig[j % 2][:, :], s_hid)

            def round_1a(r):
                if has(r, -1):
                    norm_T_hi("A", r + 1)
                if has(r, 0):
                    act.wait_ge(e_in, r + 1)
                    a_.activation(probs[:, :], probs[:, :], ACT.Exp, scale=DH0 ** -0.5).then_inc(e_out, 1)
                if is_tail(r):
                    sigmoid(0, 0)
                    norm_T_hi("B", r - 1)
                    sigmoid(0, 1)
                if has(r, 1):
                    act.wait_ge(z_step, 4 * r)
                    if later(r, 2):
                        act.wait_ge(b_out, r - 1)
                    copy(z_hi[:, :], z[:, :], z_hid)
                if is_tail(r, 0):
                    bias_product(r, 0)
                    bias_product(r, 1)
                side_work(r, 0)
                if has(r, 1) and not is_tail(r):
                    norm_T_hi("B", r - 1)
                if has(r, 0):
                    if not is_tail(r, 0):
                        bias_product(r, 0)
                        bias_product(r, 1)
                    act.wait_ge(pT_psum, r + 1)
                    copy(pT_hi[:, :], bank[2][:, 0:2 * P], pT_hid)
                if is_tail(r, GROUPS - 1):
                    norm_T_hi("C", 0)
                if is_tail(r):
                    sigmoid(0, 2)
                if has(r, 0):
                    bias_product(r, 2)
                    bias_product(r, 3)
                    side_work(r, 1)
                    if is_tail(r, GROUPS - 1):
                        query_hi(0)
                    act.wait_ge(w_used, 4 * r + 4)
                    copy(c_hi[:, :], bank[5][:, :], c_hid)
                    if is_tail(r, GROUPS - 1):
                        a_.activation(sc["warm"][:, 1:2], ones[:, 0:1], ACT.Sigmoid).then_inc(tick, 1)
                if is_tail(r, 0):
                    act.wait_ge(in_slot, 16)
                    for m in range(SM):
                        last = a_.activation(sq[:, m * D:(m + 1) * D], slot_s[:, m * D:(m + 1) * D], ACT.Square, accum_out=sc["ss"][:, m:m + 1])
                    last.then_inc(slot_rs, 1)

            loop(act, round_1a, 0, 2, GROUPS - 2, GROUPS + 1)

            def logit_copy(g, i):
                act.wait_ge(l_psum, 4 * g + i + 1)
                copy(cols(logits, g * (2 * SLOTS) + i * 512, 512), bank[6 + i % 2][:, :], l_sb)

            def e_exp(n, s):
                act.wait_ge(d_sub, n + 1)
                a_.activation(ef[s][:, :], ef[s][:, :], ACT.Exp).then_inc(d_exp, 1)

            def e_high(n, s):
                act.wait_ge(d_exp, n + 1)
                if later(n, 4):
                    act.wait_ge(sl_psum, n - 3)
                copy(e_hi[s][:, :], ef[s][:, :], d_hi)

            def spread_copy(b):
                for i in range(2):
                    act.wait_ge(cm_bc, 2 * b + i + 1)
                    copy(cmb[:, b * SLOTS + i * 512:b * SLOTS + i * 512 + 512], bank[spread_bank[b][i]][:, :], cm_sb)

            def round_1b(r):
                if has(r, 2) and not is_tail(r, 9):
                    norm_T_hi("D", r - 2)
                if is_tail(r, 8):
                    a_.activation(sc["warm"][:, 2:3], ones[:, 0:1], ACT.Exp).then_inc(tick, 1)
                    spread_copy(0)
                if is_tail(r, 9):
                    e_exp(0, 0)
                if has(r, 0) and not is_tail(r, 0):
                    sigmoid(r, 0)
                    sigmoid(r, 1)
                if has(r, 2):
                    logit_copy(r - 2, 0)
                if has(r, 0) and not is_tail(r, 0):
                    sigmoid(r, 2)
                if has(r, -1):
                    norm_T_hi("C", r + 1)
                if has(r, 0):
                    sigmoid(r, 3)
                if is_tail(r, 9):
                    e_high(0, 0)
                if has(r, 2):
                    logit_copy(r - 2, 1)
                if has(r, 1):
                    act.wait_ge(ln_ready["D"], 2 * r)
                    copy(cols(xn_hi, (r - 1) * (2 * XW), 2 * XW).rearrange("p (t n) -> p t n", n=XW)[:, :, 0:D],
                         lnx["D"][:, :].rearrange("p (t n) -> p t n", n=D), xn_hid)
                if has(r, -1):
                    query_hi(r + 1)
                if has(r, 2):
                    logit_copy(r - 2, 2)
                if is_tail(r, 8):
                    norm_T_hi("D", r - 1)
                if is_tail(r, 9):
                    e_exp(1, 1)
                    e_high(1, 1)
                if has(r, 0):
                    act.wait_ge(o_part, 4 * r + 4)
                    copy(o_hi[:, :], bank[5][:, :], o_hid)
                if has(r, 2):
                    logit_copy(r - 2, 3)

            loop(act, round_1b, 0, 3, GROUPS - 1, GROUPS + 2)

            def slT_high(n, s):
                act.wait_ge(slT_psum, n + 1)
                copy(cols(slT_hi, n * (2 * P), 2 * P), bank[2 + s % 2][:, 0:2 * P], slT_hid)

            def step_2(n, s):
                if has(n, 2, 16):
                    slT_high(n - 2, (s + 2) % 4)
                if has(n, -2, 16):
                    e_exp(n + 2, (s + 2) % 4)
                    e_high(n + 2, (s + 2) % 4)
                if is_tail(n, 3):
                    spread_copy(1)
                if is_tail(n, 14):
                    a_.activation(sc["warm"][:, 0:1], ones[:, 0:1], ACT.Gelu).then_inc(tick, 1)
                for i in (2 * (n - 12), 2 * (n - 12) + 1) if isinstance(n, int) and 12 <= n < 14 else ():
                    act.wait_ge(in_ew[0], 16)
                    part, gamma = w1_piece(i)
                    a_.activation(w1_hi[:, part], w1_f[:, part], ACT.Copy, scale=gamma).then_inc(w1_hid, 1)
                for i in (2 * (n - 14), 2 * (n - 14) + 1) if isinstance(n, int) and 14 <= n < 16 else ():
                    act.wait_ge(in_ew[1], 16)
                    copy(w2_hi[:, i * 512:(i + 1) * 512], w2_f[:, i * 512:(i + 1) * 512], w2_hid)

            dispatch_steps(act, step_2, 0, 17)

            def gelu(c, j):
                act.wait_ge(h_psum, 4 * c + j + 1)
                if later(4 * c + j, 2):
                    act.wait_ge(g_lo, 4 * c + j - 1)
                a_.activation(hf[j % 2][:, :], bank[4 + j % 2][:, :], ACT.Gelu).then_inc(g_act, 1)

            def expert_hi(c):
                act.wait_ge(p_part, 4 * c + 4)
                copy(cols(xn_hi, c * (2 * XW), 2 * XW).rearrange("p (t n) -> p t n", n=XW)[:, :, 0:D],
                     bank[6][:, :].rearrange("p (t n) -> p t n", n=D), pr_hi)

            def chunk(c):
                gelu(c, 0)
                if has(c, 1):
                    expert_hi(c - 1)
                for j in range(1, 4):
                    gelu(c, j)
                    if is_tail(c, 0) and j == 1:
                        slT_high(15, 3)

            loop(act, chunk, 0, 1, GROUPS, GROUPS)

            def comb_exp(t, s):
                act.wait_ge(nrow_done, 1)
                if later(t, 2):
                    act.wait_ge(e2_psum, 2 * t - 2)
                a_.activation(ef[s][:, :], cols(logits, t * SLOTS, SLOTS), ACT.Exp,
                              bias=cols(sc["nrow"], t, 1)).then_inc(e2_act, 1)

            def comb_hi(t, s):
                for i in range(2):
                    act.wait_ge(e2_psum, 2 * t + i + 1)
                    if i == 0 and later(t, 2):
                        act.wait_ge(y_psum, t - 1)
                    copy(e2T_hi[s][:, i * 512:(i + 1) * 512], bank[2 * s + i][:, :], e2_hi)

            def step_4(t, s):
                if has(t, -1, TILES):
                    comb_hi(t + 1, 1 - s)
                if has(t, -2, TILES):
                    comb_exp(t + 2, s)

            comb_exp(0, 0)
            comb_exp(1, 1)
            comb_hi(0, 0)
            expert_hi(GROUPS - 1)
            for t in range(0, 2):
                step_4(t, t % 2)
            with act.Fori(2, 13, 2) as t:
                for s in range(2):
                    step_4(t + s, s)
            for t in range(14, 16):
                step_4(t, t % 2)

        @block.vector
        def _(dve):
            v_ = nc.vector

            def stats(ch, g):
                if ch == "A":
                    if later(g, 2):
                        dve.wait_ge(in_x, 16)
                    else:
                        dve.wait_ge((in_x0, in_x1)[g], 16)
                else:
                    held(dve, x_ready[ch], g + 1)
                for u in range(2):
                    v_.bn_stats(sc["bn" + ch][:, 6 * u:6 * u + 6], cols(xs, g * (2 * D) + u * D, D)).then_inc(bn_done[ch], 1)
                held(dve, bn_done[ch], 2 * g + 2)
                for u in range(2):
                    v_.bn_aggr(sc["mv" + ch][:, 2 * u:2 * u + 2], sc["bn" + ch][:, 6 * u:6 * u + 6]).then_inc(st_ready[ch], 1)

            def normed(ch, g):
                dve.wait_ge(rs_ready[ch], g + 1)
                if ch == "D" and later(g):
                    dve.wait_ge(xn_lod, g)
                for u in range(2):
                    v_.tensor_scalar(lnx[ch][:, u * D:(u + 1) * D], cols(xs, g * (2 * D) + u * D, D),
                                     sc["mv" + ch][:, 2 * u:2 * u + 1], sc["rs" + ch][:, u:u + 1],
                                     ALU.subtract, ALU.mult).then_inc(ln_ready[ch], 1)

            def low(dst, src, hi, done, n=1):
                v_.tensor_tensor(dst, src, f(hi), ALU.subtract).then_inc(done, n)

            def norm_T_lo(ch, g):
                bk = {"A": 0, "B": 7, "C": 0, "D": 1}[ch]
                dve.wait_ge(xT_hid[ch], g + 1)
                low(xT_lo[xT_place(ch, g)][:, :], bank[bk][:, :], xT_hi[xT_place(ch, g)][:, :], xT_lod[ch])

            def residual(ch, g, bk):
                v_.tensor_tensor(xg(g), xg(g), bank[bk][:, :], ALU.add).then_inc(x_ready[ch], 1)

            dve.wait_ge(in_ctx, 32)
            ctx5 = ctx_s[:, :].rearrange("p (k b c s) -> p k b c s", k=KT, b=BATCH, c=2)
            v_.tensor_tensor(hcT[:, :].rearrange("p (k b s) -> p k b s", k=KT, b=BATCH), ctx5[:, :, :, 0, :],
                             pe_s[:, :].rearrange("p (k s) -> p k s", k=KT).unsqueeze(2).to_broadcast([P, KT, BATCH, KEYS]),
                             ALU.add).then_inc(hc_ready, 1)
            stats("A", 0)
            normed("A", 0)
            stats("A", 1)
            dve.wait_ge(in_o0, 32)
            v_.tensor_scalar(bo_s[:, :], bo_s[:, :], 1.0 / H0, None, ALU.mult).then_inc(v0_steps, 1)
            dve.wait_ge(kv0_psum, 2)
            v_.tensor_copy(vT0[:, :], bank[1][:, :]).then_inc(v0_steps, 1)
            norm_T_lo("A", 0)
            normed("A", 1)
            for i in range(4):
                k, par = i // 2, i % 2
                dve.wait_ge(a_hid, i + 1)
                view = lambda t: t[:, :].rearrange("p (g k h j) -> p k h g j", g=GROUPS, k=KT, h=H0)[:, k, par::2]
                v_.tensor_tensor(view(a_lo), bank[2 + i][:, :].rearrange("p (h g j) -> p h g j", h=4, g=GROUPS),
                                 f(view(a_hi)), ALU.subtract).then_inc(a_lod, 1)
            dve.wait_ge(vw_psum, 1)
            dve.wait_ge(v0_steps, 1)
            for bk, h in zip(vw_bank, (0, 1, 4, 5)):
                v_.tensor_tensor(vwt[:, :].rearrange("p (h n) -> p h n", h=H0)[:, h:h + 3:2], bank[bk][:, :].rearrange("p (h n) -> p h n", h=2),
                                 bo_s[:, :].unsqueeze(1).to_broadcast([P, 2, D]), ALU.add).then_inc(vwt_done, 1)
            def side_work(r, half):
                if is_tail(r, 0) and half == 0:
                    dve.wait_ge(l1_psum, 1)
                    kb = bank[3][:, 0:256].rearrange("p (c b s) -> p c b s", c=KT, b=BATCH)
                    for b in range(BATCH):
                        v_.tensor_tensor(kc_f[:, b * KT * P:(b + 1) * KT * P].rearrange("p (c h s) -> p c h s", c=KT, h=2),
                                         kb[:, :, b, :].unsqueeze(2).to_broadcast([P, KT, 2, KEYS]),
                                         mk_s[:, :].rearrange("p (h s) -> p h s", h=2).unsqueeze(1).to_broadcast([P, KT, 2, KEYS]),
                                         ALU.mult).then_inc(kvc_made, 1)
                if is_tail(r, 0) and half == 1:
                    dve.wait_ge(l1_psum, 2)
                    v_.tensor_tensor(vc_f[:, :].rearrange("p (m n) -> p m n", n=32), bank[3][:, :].rearrange("p (m n) -> p m n", n=32),
                                     mv_s[:, :].unsqueeze(1).to_broadcast([P, BATCH * PAIRS, 32]), ALU.mult).then_inc(kvc_made, 1)
                    dve.wait_ge(vw_hid, 1)
                    low(vw_lo[:, 0:D], vw_f[:, 0:D], vw_hi[:, 0:D], vw_lod)
                    dve.wait_ge(kvc_hid, 2)
                    low(kc_lo[:, :], kc_f[:, :], kc_hi[:, :], kvc_lod)
                    low(vc_lo[:, :], vc_f[:, :], vc_hi[:, :], kvc_lod)
                if is_tail(r, 1) and half == 1:
                    dve.wait_ge(vw_hid, 2)
                    low(vw_lo[:, D:], vw_f[:, D:], vw_hi[:, D:], vw_lod)
                if is_tail(r, 1) and half == 1:
                    dve.wait_ge(in_g, 32)
                    v_.tensor_tensor(sc["gg"], sc["gxs"], sc["gss"], ALU.mult).then_inc(gg_ready, 1)
                    dve.wait_ge(wqo_hid, 2)
                    low(wq1_lo[:, :], wq1_f[:, :], wq1_hi[:, :], wqo_lod)
                    low(wo1_lo[:, :], wo1_f[:, :], wo1_hi[:, :], wqo_lod)
                q = slot_quarter(r, half)
                if q is not None:
                    dve.wait_ge(se_hid, q + 1)
                    part = slice(q * 512, (q + 1) * 512)
                    v_.scalar_tensor_tensor(out=se_lo[:, part], in0=bank[3][:, :], scalar=sc["gg"][:, q // 2:q // 2 + 1],
                                            in1=f(se_hi[:, part]), op0=ALU.mult, op1=ALU.subtract).then_inc(se_lod, 1)

            pv = probs[:, :].rearrange("p (a j) -> p a j", j=WK)
            bcast = lambda ap: ap.unsqueeze(2).to_broadcast([P, 2 * H0, WK])

            def sig_low(g, j):
                dve.wait_ge(s_hid, 4 * g + j + 1)
                low(sig_lo[j][:, :], sig[0][:, :], sig_hi[j][:, :], s_lod[0])

            def bias_first(g):
                dve.wait_ge(z_prod, OC * (g + 1))
                v_.tensor_tensor(prod[:, 0:4 * D], prod[:, 0:4 * D], prod[:, 4 * D:8 * D], ALU.add).then_inc(z_step, 1)

            def query_lo(g):
                dve.wait_ge(q_hid, g + 1)
                low(q_lo[:, :], bank[2][:, :], q_hi[:, :], q_lod)

            def round_1a(r):
                if has(r, 1) and not is_tail(r):
                    dve.wait_ge(a_out, r)
                    residual("B", r - 1, 1)
                    stats("B", r - 1)
                if is_tail(r):
                    sig_low(0, 0)
                if has(r, 0):
                    scores = bank[6][:, 0:2 * P].rearrange("p (a j) -> p a j", j=WK)
                    dve.wait_ge(sc_psum, r + 1)
                    v_.tensor_reduce(sc["mx"], scores, AXX, ALU.max).then_inc(sm_step, 1)
                    dve.wait_ge(sm_step, 3 * r + 1)
                    if later(r):
                        dve.wait_ge(pT_psum, r)
                    v_.tensor_tensor(pv, scores, bcast(sc["mx"]), ALU.subtract).then_inc(e_in, 1)
                if has(r, -1):
                    norm_T_lo("A", r + 1)
                if has(r, 1) and not is_tail(r):
                    normed("B", r - 1)
                if has(r, 0):
                    dve.wait_ge(e_out, r + 1)
                    v_.tensor_reduce(sc["sm"], pv, AXX, ALU.add).then_inc(sm_step, 1)
                    dve.wait_ge(sm_step, 3 * r + 2)
                    v_.reciprocal(sc["rc"], sc["sm"]).then_inc(sm_step, 1)
                    dve.wait_ge(sm_step, 3 * r + 3)
                    v_.tensor_tensor(pv, pv, bcast(sc["rc"]), ALU.mult).then_inc(p_ready, 1)
                side_work(r, 0)
                if has(r, -2):
                    stats("A", r + 2)
                if is_tail(r, GROUPS - 2):
                    stats("C", 0)
                if has(r, 1):
                    norm_T_lo("B", r - 1)
                if has(r, 0):
                    dve.wait_ge(pT_hid, r + 1)
                    low(pT_lo[:, :], bank[2][:, 0:2 * P], pT_hi[:, :], pT_lod)
                if is_tail(r, GROUPS - 1):
                    norm_T_lo("C", 0)
                    stats("C", 1)
                if has(r, -2):
                    normed("A", r + 2)
                if is_tail(r, GROUPS - 2):
                    normed("C", 0)
                side_work(r, 1)
                if is_tail(r, GROUPS - 1):
                    dve.wait_ge(b_out, r)
                    residual("C", r - 1, 4)
                    dve.wait_ge(a_out, r + 1)
                    residual("B", r, 1)
                    stats("B", r)
                    query_lo(0)
                if has(r, 0):
                    bias_first(r)
                if has(r, 1) and not is_tail(r, GROUPS - 1):
                    dve.wait_ge(b_out, r)
                    residual("C", r - 1, 4)
                if is_tail(r, GROUPS - 1):
                    normed("B", r)
                    normed("C", 1)
                if has(r, 0):
                    dve.wait_ge(c_hid, r + 1)
                    low(c_lo[:, :], bank[5][:, :], c_hi[:, :], c_lod)

            loop(dve, round_1a, 0, 2, GROUPS - 2, GROUPS + 1)


            def maxima(g, u):
                dve.wait_ge(l_sb, 4 * g + 2 * u + 2)
                tile = cols(logits, g * (2 * SLOTS) + u * SLOTS, SLOTS)
                v_.tensor_reduce(cols(sc["rowmax"], 2 * g + u, 1), tile, AXX, ALU.max).then_inc(rowmax_done, 1)
                dve.wait_ge(colmax_done, 2 * g + u + 1)
                acc = cols(colmax, (g // 4) * SLOTS, SLOTS)
                v_.tensor_tensor(acc, acc, tile, ALU.max).then_inc(colmax_done, 1)

            def column_maxima(b):
                for i in range(2):
                    dve.wait_ge(cmT, 2 * b + i + 1)
                    v_.tensor_reduce(sc["cm"][:, b * SM + 4 * i:b * SM + 4 * i + 4],
                                     bank[cmT_bank[b][i]][:, :].rearrange("p (m t) -> p m t", m=4), AXX, ALU.max).then_inc(cm_red, 1)
                dve.wait_ge(cm_red, 2 * b + 2)
                v_.tensor_tensor(diag[b][:, :].rearrange("p (m s) -> p m s", m=SM),
                                 ident[:, :].unsqueeze(1).to_broadcast([P, SM, P]),
                                 sc["cm"][:, b * SM:(b + 1) * SM].unsqueeze(2).to_broadcast([P, SM, P]), ALU.mult).then_inc(cm_diag, 1)

            def e_low(n, s):
                dve.wait_ge(d_hi, n + 1)
                low(e_lo[s][:, :], ef[s][:, :], e_hi[s][:, :], d_lo)

            def round_1b(r):
                if is_tail(r, 0):
                    stats("C", 2)
                if has(r, -1) and not is_tail(r, 0) and not is_tail(r, 1):
                    dve.wait_ge(ln_ready["C"], 2 * r + 2)
                    stats("C", r + 1)
                if has(r, 2) and not is_tail(r, 9):
                    norm_T_lo("D", r - 2)
                if has(r, 0) and not is_tail(r, 0):
                    sig_low(r, 0)
                if has(r, 1):
                    dve.wait_ge(c_out, r)
                    residual("D", r - 1, 2)
                    stats("D", r - 1)
                if is_tail(r, 8):
                    maxima(r - 3, 0)
                elif has(r, 3):
                    maxima(r - 3, 1)
                if is_tail(r, 9):
                    e_low(0, 0)
                if has(r, -1):
                    norm_T_lo("C", r + 1)
                if has(r, 0):
                    sig_low(r, 2)
                if has(r, 1):
                    normed("D", r - 1)
                if is_tail(r, 8):
                    maxima(r - 3, 1)
                    norm_T_lo("D", r - 1)
                    maxima(r - 2, 0)
                if has(r, -1):
                    query_lo(r + 1)
                if is_tail(r, 7):
                    column_maxima(0)
                if has(r, 2) and not is_tail(r, 7) and not is_tail(r, 8):
                    maxima(r - 2, 0)
                if has(r, 0):
                    dve.wait_ge(o_hid, r + 1)
                    low(o_lo[:, :], bank[5][:, :], o_hi[:, :], o_lod)

            loop(dve, round_1b, 0, 3, GROUPS - 1, GROUPS + 2)

            def slot_norm(n, s):
                dve.wait_ge(sl_psum, n + 1)
                v_.reciprocal(sc["rec"][:, s % 2:s % 2 + 1], bank[s % 2][:, D:D + 1]).then_inc(sl_rec, 1)
                dve.wait_ge(sl_rec, n + 1)
                v_.tensor_scalar(sf[s % 2][:, :], bank[s % 2][:, 0:D], sc["rec"][:, s % 2:s % 2 + 1], None, ALU.mult).then_inc(sl_norm, 1)

            def slT_low(n, s):
                dve.wait_ge(slT_hid, n + 1)
                low(cols(slT_lo, n * (2 * P), 2 * P), bank[2 + s % 2][:, 0:2 * P], cols(slT_hi, n * (2 * P), 2 * P), slT_lod)

            def w1_low(i):
                part, gamma = w1_piece(i)
                dve.wait_ge(w1_hid, i + 1)
                v_.scalar_tensor_tensor(out=w1_lo[:, part], in0=w1_f[:, part], scalar=gamma, in1=f(w1_hi[:, part]),
                                        op0=ALU.mult, op1=ALU.subtract).then_inc(w1_lod, 1)

            def step_2(n, s):
                if has(n, 1, 16):
                    slot_norm(n - 1, (s + 3) % 4)
                if has(n, -1, 16):
                    e_low(n + 1, (s + 1) % 4)
                if has(n, 2, 16):
                    slT_low(n - 2, (s + 2) % 4)
                if is_tail(n, 1):
                    maxima(GROUPS - 1, 1)
                if is_tail(n, 2):
                    column_maxima(1)
                for i in (2 * (n - 13), 2 * (n - 13) + 1) if isinstance(n, int) and 13 <= n < 15 else ():
                    w1_low(i)

            dispatch_steps(dve, step_2, 0, 17)
            v_.tensor_scalar(sc["nrow"], sc["rowmax"], -1.0, None, ALU.mult).then_inc(nrow_done, 1)

            def gelu_split(c, j):
                dve.wait_ge(g_act, 4 * c + j + 1)
                if later(4 * c + j, 4):
                    dve.wait_ge(p_part, 4 * c + j - 3)
                v_.tensor_copy(h_hi[j][:, :], hf[j % 2][:, :]).then_inc(g_hi, 1)
                dve.wait_ge(g_hi, 4 * c + j + 1)
                low(h_lo[j][:, :], hf[j % 2][:, :], h_hi[j][:, :], g_lo)

            def expert_lo(c):
                dve.wait_ge(pr_hi, c + 1)
                view = lambda t: cols(t, c * (2 * XW), 2 * XW).rearrange("p (t n) -> p t n", n=XW)[:, :, 0:D]
                v_.tensor_tensor(view(xn_lo), bank[6][:, :].rearrange("p (t n) -> p t n", n=D), f(view(xn_hi)), ALU.subtract).then_inc(pr_lo, 1)

            def chunk(c):
                gelu_split(c, 0)
                if has(c, 1):
                    expert_lo(c - 1)
                for j in range(1, 4):
                    gelu_split(c, j)
                    if is_tail(c, 0) and j == 1:
                        slT_low(15, 3)

            loop(dve, chunk, 0, 1, GROUPS, GROUPS)

            def comb_lo(t, s):
                for i in range(2):
                    dve.wait_ge(e2_hi, 2 * t + i + 1)
                    low(e2T_lo[s][:, i * 512:(i + 1) * 512], bank[2 * s + i][:, :], e2T_hi[s][:, i * 512:(i + 1) * 512], e2_lo)

            def finish(t, s):
                dve.wait_ge(y_psum, t + 1)
                v_.reciprocal(sc["rec4"][:, s:s + 1], bank[4 + s][:, D:D + 1]).then_inc(y_rec, 1)
                dve.wait_ge(y_rec, t + 1)
                if later(t, 2):
                    dve.wait_ge(out_done[s], (t // 2) * 16)
                v_.scalar_tensor_tensor(out=y[s][:, :], in0=bank[4 + s][:, 0:D], scalar=sc["rec4"][:, s:s + 1],
                                        in1=cols(xs, t * D, D), op0=ALU.mult, op1=ALU.add).then_inc(y_ready, 1)

            def step_4(t, s):
                if has(t, -1, TILES):
                    comb_lo(t + 1, 1 - s)
                if has(t, 0, TILES):
                    finish(t, s)

            comb_lo(0, 0)
            expert_lo(GROUPS - 1)
            for t in range(0, 2):
                step_4(t, t % 2)
            with dve.Fori(2, 13, 2) as t:
                for s in range(2):
                    step_4(t + s, s)
            for t in range(14, 16):
                step_4(t, t % 2)

        @block.tensor
        def _(pe_):
            mm = nc.tensor.matmul

            def norm_T(ch, g):
                pe_.wait_ge(ln_ready[ch], 2 * g + 2)
                bk = {"A": 0, "B": 7, "C": 0, "D": 1}[ch]
                for k in range(KT):
                    for u in range(2):
                        last = nc.tensor.transpose(bank[bk][:, k * GT + u * P:k * GT + (u + 1) * P],
                                                   lnx[ch][:, u * D + k * P:u * D + (k + 1) * P], ident[:, :])
                last.then_inc(xT_psum[ch], 1)

            def xT(ch, k, u=None):
                lo, n = (k * GT, GT) if u is None else (k * GT + u * P, P)
                return xT_hi[ch][:, lo:lo + n], xT_lo[ch][:, lo:lo + n]

            def pair(hi, lo, start, n):
                return cols(hi, start, n), cols(lo, start, n)

            pe_.wait_ge(hc_ready, 1)
            for bk, w, there in ((0, wk0s, in_k0), (1, wv0s, in_v0)):
                pe_.wait_ge(there, 16)
                for ct in range(4):
                    for k in range(KT):
                        last = mm(bank[bk][:, ct * P:(ct + 1) * P], w[:, k * 512 + ct * P:k * 512 + (ct + 1) * P],
                                  hcT[:, k * P:(k + 1) * P], start=k == 0, stop=k == KT - 1)
                last.then_inc(kv0_psum, 1)
            pe_.wait_ge(kT0_done, 1)
            pe_.wait_ge(in_id, 16)
            norm_T("A", 0)
            pe_.wait_ge(in_q0, 16)
            for k in range(KT):
                for h in range(H0):
                    par, i = h % 2, h // 2
                    rows = slice(DH0 * par, DH0 * (par + 1))
                    last = mm(bank[2 + 2 * k + par][:, i * P:(i + 1) * P], wq0s[rows, i * D + k * P:i * D + (k + 1) * P],
                              kT0[rows, i * P:(i + 1) * P], start=True, stop=True)
            last.then_inc(a_psum, 1)
            pe_.wait_ge(v0_steps, 2)
            pe_.wait_ge(in_o0, 32)
            for h in range(H0):
                par, i = h % 2, h // 2
                rows = slice(DH0 * par, DH0 * (par + 1))
                if h == 5:
                    pe_.wait_ge(a_lod, 1)
                last = mm(bank[vw_bank[2 * (i // 2) + par]][:, (i % 2) * D:(i % 2 + 1) * D], vT0[rows, i * P:(i + 1) * P],
                          wo0s[rows, i * D:(i + 1) * D], start=True, stop=True)
            last.then_inc(vw_psum, 1)

            def layer1_keys():
                pe_.wait_ge(in_l1, 64)
                ctx5 = ctx_s[:, :].rearrange("p (k b c s) -> p k b c s", k=KT, b=BATCH, c=2)
                for ct in range(KT):
                    for k in range(KT):
                        last = mm(bank[3][:, ct * P:(ct + 1) * P], wk1s[:, k * D + ct * P:k * D + (ct + 1) * P], ctx5[:, k, :, 0, :],
                                  start=k == 0, stop=k == KT - 1)
                last.then_inc(l1_psum, 1)

            def layer1_values():
                pe_.wait_ge(kvc_made, 2)
                for b in range(BATCH):
                    for k in range(KT):
                        last = mm(bank[3][:, b * D:(b + 1) * D], ctx_s[:, (k * BATCH + b) * P:(k * BATCH + b + 1) * P],
                                  wv1s[:, k * D:(k + 1) * D], start=k == 0, stop=k == KT - 1)
                last.then_inc(l1_psum, 1)

            def side_work(r, half):
                if is_tail(r, 0):
                    (layer1_keys, layer1_values)[half]()
                q = slot_quarter(r, half)
                if q is not None:
                    pe_.wait_ge(slot_ready, 4)
                    pe_.wait_ge(kvc_made, 3)
                    if q > 0:
                        pe_.wait_ge(se_lod, q)
                    k, first = q // 2, 4 * (q % 2)
                    for m in range(first, first + 4):
                        last = nc.tensor.transpose(bank[3][:, (m - first) * P:(m - first + 1) * P],
                                                   slot_s[:, m * D + k * P:m * D + (k + 1) * P], ident[:, :])
                    last.then_inc(se_psum, 1)

            def fuse(g, k):
                pe_.wait_ge(in_w[k], 32 * (g + 1))
                if k == 0 and later(g):
                    pe_.wait_ge(c_lod, g)
                for c in (2 * k, 2 * k + 1):
                    for m in range(KT):
                        last = mm(bank[5][:, m * D:(m + 1) * D], w1r[:, c * D + m * P:c * D + (m + 1) * P],
                                  w2r[:, c * D:(c + 1) * D], start=c == 0 and m == 0, stop=c == OC - 1 and m == KT - 1,
                                  skip_group_check=True)
                last.then_inc(w_used, 1)

            def scores(g):
                pe_.wait_ge(xT_lod["A"], g + 1)
                for u in range(2):
                    for k in range(KT):
                        last = split3(bank[6][:, u * P:(u + 1) * P], xT("A", k, u),
                                      pair(a_hi, a_lo, g * (KT * P) + k * P, P), k == 0, k == KT - 1)
                last.then_inc(sc_psum, 1)

            def probs_T(g):
                pe_.wait_ge(p_ready, g + 1)
                for u in range(2):
                    last = nc.tensor.transpose(bank[2][:, u * P:(u + 1) * P], probs[:, u * P:(u + 1) * P], ident[:, :])
                last.then_inc(pT_psum, 1)

            def attend(g):
                pe_.wait_ge(pT_lod, g + 1)
                for u in range(2):
                    last = split3(bank[1][:, u * D:(u + 1) * D],
                                  (pT_hi[:, u * P:(u + 1) * P], pT_lo[:, u * P:(u + 1) * P]),
                                  pair(vw_hi, vw_lo, g * D, D), True, True)
                last.then_inc(a_out, 1)

            def query(g):
                if isinstance(g, int) and g == 0:
                    pe_.wait_ge(wqo_lod, 2)
                pe_.wait_ge(xT_lod["C"], g + 1)
                if later(g, 2):
                    pe_.wait_ge(x_ready["D"], g - 1)
                for ct in range(KT):
                    for k in range(KT):
                        o = k * D + ct * P
                        last = split3(bank[2][:, ct * GT:(ct + 1) * GT], (wq1_hi[:, o:o + P], wq1_lo[:, o:o + P]),
                                      xT("C", k), k == 0, k == KT - 1)
                last.then_inc(q_psum, 1)

            def ffn(g):
                pe_.wait_ge(c_lod, g + 1)
                pe_.wait_ge(z_lod, g + 1)
                pe_.wait_ge(xT_lod["B"], g + 1)
                if isinstance(g, int) and g == 0:
                    pe_.wait_ge(ones_done, 1)
                for u in range(2):
                    o = bank[4][:, u * D:(u + 1) * D]
                    for k in range(KT):
                        split3(o, xT("B", k, u), (c_hi[:, k * D:(k + 1) * D], c_lo[:, k * D:(k + 1) * D]), k == 0, False)
                    mm(o, ones_r[:, :], z_lo[:, :], start=False, stop=False, skip_group_check=True)
                    last = mm(o, ones_r[:, :], z_hi[:, :], start=False, stop=True, skip_group_check=True)
                last.then_inc(b_out, 1)

            def sig_scores(g, j):
                if j == 0:
                    pe_.wait_ge(k1_in, (g // 4 + 1) * 128)
                    pe_.wait_ge(q_lod, g + 1)
                if later(4 * g + j, 2):
                    pe_.wait_ge(s_sig, 4 * g + j - 1)
                if is_tail(g, 0) and j in (1, 3):
                    pe_.wait_ge(x_ready["C"], GROUPS - 1 + j // 3)
                ct = j // 2
                for i in range(2):
                    m = 2 * j + i
                    last = split3(bank[3 + j % 2][:, i * GT:(i + 1) * GT], (kw_hi[:, m * P:(m + 1) * P], kw_lo[:, m * P:(m + 1) * P]),
                                  (q_hi[:, ct * GT:(ct + 1) * GT], q_lo[:, ct * GT:(ct + 1) * GT]), True, True)
                last.then_inc(s_psum, 1)

            def v_at(m):
                return (m // 4) * VW + (m % 4) * P

            def sig_values(g, j):
                pe_.wait_ge(s_lod[j % 2], 2 * g + j // 2 + 1)
                if j == 0:
                    pe_.wait_ge(v1_in, (g // 4 + 1) * 64)
                    if later(g):
                        pe_.wait_ge(o_lod, g)
                ct = j // 2
                for i in range(2):
                    m = 2 * j + i
                    last = split3(bank[5][:, ct * GT:(ct + 1) * GT], [t[:, v_at(m):v_at(m) + P] for t in (vw1_hi, vw1_lo)],
                                  (sig_hi[j][:, i * GT:(i + 1) * GT], sig_lo[j][:, i * GT:(i + 1) * GT]),
                                  j % 2 == 0 and i == 0, j % 2 == 1 and i == 1)
                last.then_inc(o_part, 1)

            def round_1a(r):
                if has(r, 0):
                    if is_tail(r, 0):
                        pe_.wait_ge(a_lod, 4)
                        pe_.wait_ge(vwt_done, 1)
                    scores(r)
                if has(r, -1):
                    norm_T("A", r + 1)
                if has(r, 0):
                    if is_tail(r, 0):
                        pe_.wait_ge(vwt_done, 4)
                    fuse(r, 0)
                side_work(r, 0)
                if has(r, 0):
                    fuse(r, 1)
                if is_tail(r):
                    sig_scores(0, 0)
                    sig_scores(0, 1)
                if has(r, 1):
                    norm_T("B", r - 1)
                if is_tail(r):
                    norm_T("C", 1)
                    sig_scores(0, 2)
                    sig_values(0, 0)
                if has(r, 0):
                    fuse(r, 2)
                    probs_T(r)
                side_work(r, 1)
                if is_tail(r, GROUPS - 1):
                    norm_T("C", 0)
                if has(r, 1):
                    ffn(r - 1)
                if is_tail(r, GROUPS - 1):
                    attend(r)
                    query(0)
                    fuse(r, 3)
                elif has(r, 0):
                    fuse(r, 3)
                    if is_tail(r, 0) or is_tail(r, 1):
                        pe_.wait_ge(vw_lod, r + 1)
                    attend(r)

            loop(pe_, round_1a, 0, 2, GROUPS - 2, GROUPS + 1)

            def project(g):
                pe_.wait_ge(o_lod, g + 1)
                for u in range(2):
                    for ct in range(KT):
                        o = ct * GT + u * P
                        last = split3(bank[2][:, u * D:(u + 1) * D], (o_hi[:, o:o + P], o_lo[:, o:o + P]),
                                      (wo1_hi[:, ct * D:(ct + 1) * D], wo1_lo[:, ct * D:(ct + 1) * D]), ct == 0, ct == KT - 1)
                last.then_inc(c_out, 1)

            def logit(g, i):
                u, half = i // 2, i % 2
                if i == 0:
                    pe_.wait_ge(xT_lod["D"], g + 1)
                if later(4 * g + i, 2):
                    pe_.wait_ge(l_sb, 4 * g + i - 1)
                for k in range(KT):
                    o = k * SLOTS + half * 512
                    last = split3(bank[6 + half][:, :], xT(xT_place("D", g), k, u), (se_hi[:, o:o + 512], se_lo[:, o:o + 512]),
                                  k == 0, k == KT - 1)
                last.then_inc(l_psum, 1)

            def columns_T(b):
                pe_.wait_ge(colmax_done, SM * (b + 1) + 1)
                if b == 0:
                    pe_.wait_ge(x_ready["D"], GROUPS - 1)
                for m in range(SM):
                    last = nc.tensor.transpose(bank[cmT_bank[b][m // 4]][:, (m % 4) * P:(m % 4 + 1) * P],
                                               colmax[:, b * SLOTS + m * P:b * SLOTS + (m + 1) * P], ident[:, :])
                    if m % 4 == 3:
                        last.then_inc(cmT, 1)

            def spread(b):
                if b == 0:
                    pe_.wait_ge(s_sig, 4 * GROUPS)
                else:
                    pe_.wait_ge(l_sb, 4 * GROUPS)
                pe_.wait_ge(cm_diag, b + 1)
                for i in range(2):
                    mm(bank[spread_bank[b][i]][:, :], ones[:, :], diag[b][:, i * 512:(i + 1) * 512], start=True, stop=True).then_inc(cm_bc, 1)

            def round_1b(r):
                if has(r, 0) and not is_tail(r, 0):
                    sig_scores(r, 0)
                    sig_scores(r, 1)
                if has(r, 1):
                    project(r - 1)
                if is_tail(r, 8):
                    spread(0)
                if has(r, 2):
                    if is_tail(r, 2):
                        pe_.wait_ge(se_lod, 4)
                    logit(r - 2, 0)
                if has(r, 0) and not is_tail(r, 0):
                    sig_scores(r, 2)
                    sig_values(r, 0)
                if has(r, -1) and not is_tail(r, 0):
                    norm_T("C", r + 1)
                if has(r, 0):
                    sig_scores(r, 3)
                if has(r, 0):
                    sig_values(r, 1)
                if has(r, 2):
                    logit(r - 2, 1)
                if has(r, -1):
                    query(r + 1)
                if is_tail(r, 7):
                    columns_T(0)
                if has(r, 0):
                    sig_values(r, 2)
                if has(r, 1) and not is_tail(r, 8):
                    norm_T("D", r - 1)
                if has(r, 2):
                    logit(r - 2, 2)
                if has(r, 0):
                    sig_values(r, 3)
                if is_tail(r, 8):
                    norm_T("D", r - 1)
                if has(r, 2):
                    logit(r - 2, 3)

            loop(pe_, round_1b, 0, 3, GROUPS - 1, GROUPS + 2)

            def dispatch(n, s):
                b = n // SM
                pe_.wait_ge(d_lo, n + 1)
                if later(n, 2):
                    pe_.wait_ge(sl_norm, n - 1)
                for t in range(SM):
                    last = split3(bank[s % 2][:, 0:XW], (e_hi[s][:, t * P:(t + 1) * P], e_lo[s][:, t * P:(t + 1) * P]),
                                  pair(xn_hi, xn_lo, b * (SM * XW) + t * XW, XW), t == 0, t == SM - 1)
                last.then_inc(sl_psum, 1)

            def slots_T(n, s):
                pe_.wait_ge(sl_norm, n + 1)
                if later(n, 2):
                    pe_.wait_ge(slT_lod, n - 1)
                for k in range(KT):
                    last = nc.tensor.transpose(bank[2 + s % 2][:, k * P:(k + 1) * P], sf[s % 2][:, k * P:(k + 1) * P], ident[:, :])
                last.then_inc(slT_psum, 1)

            def step_2(n, s):
                if has(n, 0, 16):
                    dispatch(n, s)
                if has(n, 1, 16):
                    slots_T(n - 1, (s + 3) % 4)
                if is_tail(n, 2):
                    columns_T(1)
                if is_tail(n, 3):
                    spread(1)

            pe_.wait_ge(xn_lod, GROUPS)
            dispatch_steps(pe_, step_2, 0, 16)

            def hidden(c, j):
                if later(4 * c + j, 2):
                    pe_.wait_ge(g_act, 4 * c + j - 1)
                for i in range(2):
                    for k in range(KT):
                        o = k * INTER + (2 * j + i) * P
                        rhs = [cols(t, c * (4 * P), 4 * P).rearrange("p (m k s) -> p k m s", m=2, k=KT)[:, k] for t in (slT_hi, slT_lo)]
                        last = split3(bank[4 + j % 2][:, i * GT:(i + 1) * GT], (w1_hi[:, o:o + P], w1_lo[:, o:o + P]), rhs,
                                      k == 0, k == KT - 1)
                last.then_inc(h_psum, 1)

            def expert(c, j):
                pe_.wait_ge(g_lo, 4 * c + j + 1)
                if j == 0 and later(c):
                    pe_.wait_ge(pr_lo, c)
                for u in range(2):
                    for i in range(2):
                        o = (2 * j + i) * D
                        last = split3(bank[6][:, u * D:(u + 1) * D],
                                      (h_hi[j][:, i * GT + u * P:i * GT + (u + 1) * P], h_lo[j][:, i * GT + u * P:i * GT + (u + 1) * P]),
                                      (w2_hi[:, o:o + D], w2_lo[:, o:o + D]), j == 0 and u == 0 and i == 0, j == 3 and u == 1 and i == 1)
                last.then_inc(p_part, 1)

            def chunk(c):
                hidden(c, 0)
                if has(c, 1):
                    expert(c - 1, 2)
                    expert(c - 1, 3)
                hidden(c, 1)
                if is_tail(c, 0):
                    slots_T(15, 3)
                if is_tail(c, 0):
                    pe_.wait_ge(w1_lod, 4)
                hidden(c, 2)
                if is_tail(c, 0):
                    pe_.wait_ge(w2_lod, 4)
                expert(c, 0)
                hidden(c, 3)
                expert(c, 1)

            pe_.wait_ge(w1_lod, 2)
            pe_.wait_ge(slT_lod, 2)
            chunk(0)
            pe_.wait_ge(slT_lod, 16)
            loop(pe_, chunk, 1, 1, GROUPS, GROUPS)
            expert(GROUPS - 1, 2)

            def comb_T(t, s):
                pe_.wait_ge(e2_act, t + 1)
                if later(t, 2):
                    pe_.wait_ge(e2_lo, 2 * t - 2)
                for m in range(SM):
                    last = nc.tensor.transpose(bank[2 * s + m // 4][:, (m % 4) * P:(m % 4 + 1) * P],
                                               ef[s][:, m * P:(m + 1) * P], ident[:, :])
                    if m % 4 == 3:
                        last.then_inc(e2_psum, 1)

            def combine(t, s):
                b = t // SM
                pe_.wait_ge(e2_lo, 2 * t + 2)
                if is_tail(t, 0):
                    pe_.wait_ge(pr_lo, GROUPS)
                if later(t, 2):
                    pe_.wait_ge(y_ready, t - 1)
                for m in range(SM):
                    last = split3(bank[4 + s][:, 0:XW], (e2T_hi[s][:, m * P:(m + 1) * P], e2T_lo[s][:, m * P:(m + 1) * P]),
                                  pair(xn_hi, xn_lo, b * (SM * XW) + m * XW, XW), m == 0, m == SM - 1)
                last.then_inc(y_psum, 1)

            def step_4(t, s):
                if has(t, -1, TILES):
                    comb_T(t + 1, 1 - s)
                if has(t, 0, TILES):
                    combine(t, s)

            comb_T(0, 0)
            expert(GROUPS - 1, 3)
            for t in range(2):
                step_4(t, t % 2)
            with pe_.Fori(2, 13, 2) as t:
                for s in range(2):
                    step_4(t + s, s)
            for t in range(14, 16):
                step_4(t, t % 2)


def position_table():
    pos = np.arange(75, dtype=np.float32)[:, None]
    denom = np.power(np.float32(10000.0), np.float32(2.0) * np.arange(D // 2, dtype=np.float32) / np.float32(D)).astype(np.float32)
    ang = (pos / denom).astype(np.float32)
    pe = np.zeros((75, D), np.float32)
    pe[:, 0::2] = np.sin(ang)
    pe[:, 1::2] = np.cos(ang)
    return pe[:KEYS].T


def kernel(**inputs):
    import concourse.bacc as bacc
    from concourse.bass_utils import run_bass_kernel_spmd

    a = {k: np.asarray(v) for k, v in inputs.items()}
    c = np.ascontiguousarray

    def ktiles(m):
        return c(m.reshape(-1, P, m.shape[1]).transpose(1, 0, 2).reshape(P, -1))

    ctxT = a["ctx_1024"].transpose(2, 0, 1)
    ctx2 = np.broadcast_to(ctxT.reshape(KT, P, BATCH, 1, KEYS).transpose(1, 0, 2, 3, 4), (P, KT, BATCH, 2, KEYS))
    p = np.arange(P)
    mask_k = np.repeat((p[:, None] % 32 // DH1 == np.arange(2)[None, :]), KEYS, axis=1).astype(np.float32)
    mask_v = (np.arange(32)[None, :] // DH1 == p[:, None] // KEYS).astype(np.float32)
    arrays = {
        "x": c(a["x"].reshape(TOKENS, D)),
        "ctx2": c(ctx2.reshape(P, -1)),
        "pe": ktiles(position_table()),
        "wq0T": c(a["L0_xattn_Wq"].T), "wk0": a["L0_xattn_Wk"], "wv0": a["L0_xattn_Wv"], "wo0": a["L0_xattn_Wo"],
        "bo": a["L0_xattn_bo"].reshape(1, D),
        "fw1": c(a["L0_ffn_W1"].reshape(GROUPS, P, OC * D)),
        "fb1": c(a["L0_ffn_b1"].reshape(GROUPS, P, OC)),
        "fw2T": c(a["L0_ffn_W2"].transpose(0, 2, 1).reshape(GROUPS, P, OC * D)),
        "fb2": a["L0_ffn_b2"],
        "wq1T": c(a["L1_xattn_Wq"].T), "wk1T": c(a["L1_xattn_Wk"].T), "wv1T": c(a["L1_xattn_Wv"].T), "wo1T": c(a["L1_xattn_Wo"].T),
        "gx": c(a["L1_ffn_gamma_x"].reshape(KT, P).T), "gs": c(a["L1_ffn_gamma_slot"].reshape(KT, P).T),
        "slot": a["L1_ffn_slot_embeds"].reshape(SLOTS, D), "w1": a["L1_ffn_w1"], "w2": a["L1_ffn_w2"],
        "ident_in": np.eye(P, dtype=np.float32), "mask_k": mask_k, "mask_v": mask_v,
    }
    nc = bacc.Bacc("TRN2", target_bir_lowering=False, num_devices=1, dynamic_dma_scratch_size=1024)
    args = {n: nc.dram_tensor(f"in_{n}", v.shape, F32, kind="ExternalInput").ap() for n, v in arrays.items()}
    outp = nc.dram_tensor("out_0", (TOKENS, D), F32, kind="ExternalOutput").ap()
    build(nc, out=outp, **args)
    r = run_bass_kernel_spmd(nc, [{f"in_{n}": c(v) for n, v in arrays.items()}], core_ids=[0])
    return np.asarray(r.results[0]["out_0"]).reshape(BATCH, SEQ, D)
```
